# Optimizing a Trainium2 kernel written in Bass

```python
import numpy as np
import jax
import jax.numpy as jnp

def _softmax(x, axis=-1):
    return jax.nn.softmax(x, axis=axis)

def _gelu(x):
    return jax.nn.gelu(x, approximate=True)

def _silu(x):
    return jax.nn.silu(x)

def _sigmoid(x):
    return jax.nn.sigmoid(x)

def _layernorm(x, axis=-1, eps=1e-05):
    m = jnp.mean(x, axis=axis, keepdims=True)
    v = jnp.var(x, axis=axis, keepdims=True)
    return (x - m) / jnp.sqrt(v + eps)

def _scatter_add(tgt, idx, src, axis=0):
    return tgt.at[idx].add(src)

def _segment_sum(src, seg, n):
    return jax.ops.segment_sum(src, seg, n)
kernel_name = 'mk_xattn_ffn_d1_seqx_r8_7a35f1'

def setup_inputs(seed: int=0):
    np.random.seed(seed)
    _w = jnp.asarray

    def _rec_inputs():
        import jax
        import jax.numpy as jnp
        _rk = jax.random.key(seed)
        x = 0.002226 + 0.9996 * jax.random.normal(jax.random.fold_in(_rk, 1), (32, 56, 128), jnp.float32)
        _lenS = 56 - jax.random.randint(jax.random.fold_in(_rk, 7), (32,), 0, max(1, 56 // 4) + 1, jnp.int32)
        _lenS2 = 1500 - jax.random.randint(jax.random.fold_in(_rk, 8), (32,), 0, max(1, 1500 // 4) + 1, jnp.int32)
        _ctx_1024P = jax.random.normal(jax.random.fold_in(_rk, 11), (32, 16, 128), jnp.float32)
        _ctx_1024c = jax.random.dirichlet(jax.random.fold_in(_rk, 511), 0.3 * jnp.ones((16,), jnp.float32), (32, 1500))
        _ctx_1024t = jnp.einsum('bsk,bkd->bsd', _ctx_1024c, _ctx_1024P)
        _ctx_1024t = _ctx_1024t * jax.lax.rsqrt(jnp.mean(jnp.square(_ctx_1024t)) + 1e-12) * 0.953939
        ctx_1024 = -0.000125008 + 0.999885 * (_ctx_1024t + 0.3 * jax.random.normal(jax.random.fold_in(_rk, 611), (32, 1500, 128), jnp.float32))
        return (x, ctx_1024)
    x, ctx_1024 = _rec_inputs()

    def _L0_xattn_setup():
        import jax, jax.numpy as jnp
        import numpy as np
        EPS = 1e-05

        def layer_norm(x, g, b):
            mu = jnp.mean(x, axis=-1, keepdims=True)
            var = jnp.var(x, axis=-1, keepdims=True)
            return (x - mu) * jax.lax.rsqrt(var + EPS) * g + b
        key = jax.random.key(seed)
        ks = jax.random.split(key, 8)
        dim, heads, dim_head = (128, 16, 64)
        inner = heads * dim_head
        b, n, m = (8, 512, 64)
        s = dim ** (-0.5)
        return {'x': jax.random.normal(ks[0], (b, n, dim), jnp.float32), 'latents': jax.random.normal(ks[1], (b, m, dim), jnp.float32), 'ln_m_g': jnp.ones((dim,), jnp.float32), 'ln_m_b': jnp.zeros((dim,), jnp.float32), 'ln_l_g': jnp.ones((dim,), jnp.float32), 'ln_l_b': jnp.zeros((dim,), jnp.float32), 'Wq': jax.random.normal(ks[2], (dim, inner), jnp.float32) * s, 'Wkv': jax.random.normal(ks[3], (dim, 2 * inner), jnp.float32) * s, 'Wout': jax.random.normal(ks[4], (inner, dim), jnp.float32) * s}
    _L0_xattn_all = _L0_xattn_setup()
    _L0_xattn_in = {k: v for k, v in _L0_xattn_all.items() if k in ('ln_m_g', 'ln_m_b', 'ln_l_g', 'ln_l_b', 'Wq', 'Wkv', 'Wout')}
    del _L0_xattn_all

    def _L0_ffn_setup():
        import jax, jax.numpy as jnp
        import numpy as np
        NUM_EXPERTS = 8
        TOP_K = 2
        key = jax.random.key(seed)
        ks = jax.random.split(key, 6)
        B, S, D, F = (2, 256, 128, 512)
        E = NUM_EXPERTS
        sd = 1.0 / np.sqrt(D)
        sf = 1.0 / np.sqrt(F)
        return {'x': jax.random.normal(ks[0], (B, S, D), dtype=jnp.float32), 'gate_w': jax.random.normal(ks[1], (E, D), dtype=jnp.float32) * sd, 'w1': jax.random.uniform(ks[2], (F, E, D), dtype=jnp.float32, minval=-sd, maxval=sd), 'b1': jax.random.uniform(ks[3], (E, F), dtype=jnp.float32, minval=-sd, maxval=sd), 'w2': jax.random.uniform(ks[4], (D, E, F), dtype=jnp.float32, minval=-sf, maxval=sf), 'b2': jax.random.uniform(ks[5], (E, D), dtype=jnp.float32, minval=-sf, maxval=sf)}
    _L0_ffn_all = _L0_ffn_setup()
    _L0_ffn_in = {k: v for k, v in _L0_ffn_all.items() if k in ('gate_w', 'w1', 'b1', 'w2', 'b2')}
    del _L0_ffn_all
    return {'x': x, 'ctx_1024': ctx_1024, 'L0_xattn_ln_m_g': _L0_xattn_in['ln_m_g'], 'L0_xattn_ln_m_b': _L0_xattn_in['ln_m_b'], 'L0_xattn_ln_l_g': _L0_xattn_in['ln_l_g'], 'L0_xattn_ln_l_b': _L0_xattn_in['ln_l_b'], 'L0_xattn_Wq': _L0_xattn_in['Wq'], 'L0_xattn_Wkv': _L0_xattn_in['Wkv'], 'L0_xattn_Wout': _L0_xattn_in['Wout'], 'L0_ffn_gate_w': _L0_ffn_in['gate_w'], 'L0_ffn_w1': _L0_ffn_in['w1'], 'L0_ffn_b1': _L0_ffn_in['b1'], 'L0_ffn_w2': _L0_ffn_in['w2'], 'L0_ffn_b2': _L0_ffn_in['b2']}

def reference(x, ctx_1024, L0_xattn_ln_m_g, L0_xattn_ln_m_b, L0_xattn_ln_l_g, L0_xattn_ln_l_b, L0_xattn_Wq, L0_xattn_Wkv, L0_xattn_Wout, L0_ffn_gate_w, L0_ffn_w1, L0_ffn_b1, L0_ffn_w2, L0_ffn_b2):
    import jax
    import jax.numpy as jnp

    def _L0_xattn_ref(x, latents, ln_m_g, ln_m_b, ln_l_g, ln_l_b, Wq, Wkv, Wout):
        import jax, jax.numpy as jnp
        import numpy as np
        EPS = 1e-05

        def layer_norm(x, g, b):
            mu = jnp.mean(x, axis=-1, keepdims=True)
            var = jnp.var(x, axis=-1, keepdims=True)
            return (x - mu) * jax.lax.rsqrt(var + EPS) * g + b
        heads, dim_head = (16, 64)
        scale = dim_head ** (-0.5)
        x = layer_norm(x, ln_m_g, ln_m_b)
        lat = layer_norm(latents, ln_l_g, ln_l_b)
        b, m, _ = lat.shape
        q = lat @ Wq
        kv_input = jnp.concatenate([x, lat], axis=1)
        kv = kv_input @ Wkv
        k, v = jnp.split(kv, 2, axis=-1)

        def split_heads(t):
            return t.reshape(t.shape[0], t.shape[1], heads, dim_head).transpose(0, 2, 1, 3)
        q, k, v = (split_heads(q), split_heads(k), split_heads(v))
        dots = jnp.einsum('bhid,bhjd->bhij', q, k) * scale
        attn = jax.nn.softmax(dots, axis=-1)
        out = jnp.einsum('bhij,bhjd->bhid', attn, v)
        out = out.transpose(0, 2, 1, 3).reshape(b, m, heads * dim_head)
        return out @ Wout

    def _L0_ffn_ref(x, gate_w, w1, b1, w2, b2):
        import jax, jax.numpy as jnp
        import numpy as np
        NUM_EXPERTS = 8
        TOP_K = 2
        logits = jnp.einsum('bsd,ed->bse', x, gate_w)
        probs = jax.nn.softmax(logits, axis=-1)
        topk_probs, topk_idx = jax.lax.top_k(probs, TOP_K)
        oh = jax.nn.one_hot(topk_idx, NUM_EXPERTS, dtype=x.dtype)
        h = jnp.einsum('bsd,fed,bske->bskf', x, w1, oh)
        h = h + jnp.take(b1, topk_idx, axis=0)
        h = jax.nn.gelu(h)
        y = jnp.einsum('bskf,def,bske->bskd', h, w2, oh)
        y = y + jnp.take(b2, topk_idx, axis=0)
        out = jnp.sum(y * topk_probs[..., None], axis=-2)
        return out
    x = x + _L0_xattn_ref(ctx_1024, _layernorm(x, axis=-1), L0_xattn_ln_m_g, L0_xattn_ln_m_b, L0_xattn_ln_l_g, L0_xattn_ln_l_b, L0_xattn_Wq, L0_xattn_Wkv, L0_xattn_Wout)
    x = x + _L0_ffn_ref(_layernorm(x, axis=-1), L0_ffn_gate_w, L0_ffn_w1, L0_ffn_b1, L0_ffn_w2, L0_ffn_b2)
    return x

_drawn_inputs = setup_inputs


def setup_inputs(seed=0):
    import zlib

    import numpy as np

    out = dict(_drawn_inputs(seed))
    spreads = {'L0_xattn_ln_m_g': (1.0, 0.2),
     'L0_xattn_ln_m_b': (0.0, 0.1),
     'L0_xattn_ln_l_g': (1.0, 0.2),
     'L0_xattn_ln_l_b': (0.0, 0.1)}
    factors = {'L0_ffn_b1': 8.0, 'L0_ffn_b2': 8.0}
    for name, (base, spread) in spreads.items():
        noise = np.random.default_rng([zlib.crc32(name.encode()), seed]).standard_normal(out[name].shape)
        drawn = base * np.exp(spread * noise) if base else spread * noise
        out[name] = jnp.asarray(drawn.astype(out[name].dtype))
    for name, factor in factors.items():
        out[name] = (out[name] * factor).astype(out[name].dtype)
    return out
```

```python
from contextlib import ExitStack

import concourse.bass as bass
from concourse import mybir

ALU = mybir.AluOpType
ACT = mybir.ActivationFunctionType
AX = mybir.AxisListType
F32 = mybir.dt.float32
F16 = mybir.dt.float16


CONST = 1024.0
ZS = 16.0
PSHIFT = 5.545177444479562
EPS = 1e-5
LEAD, NSLOT, UNROLL = 4, 14, 4


def attention_and_experts(nc, x, ctx_rows, ln_m_g, ln_m_b, ln_l_g, ln_l_b, Wq, Wkv, Wout,
                          gate_w, w1, b1, w2, b2, out):
    NB, S, D = x.shape
    M = ctx_rows.shape[1]
    INNER = Wq.shape[1]
    DH = 64
    H = INNER // DH
    HH = H // 2
    HC = HH * S
    QC = H * S
    TP = 125
    CT = M // TP
    NT = CT + 1
    QT = QC // 128
    TOK = NB * S
    E, Dff = b1.shape
    assert D == 128 and M == CT * TP and CT == 12 and QC == 7 * 128 and DH == 64 and Dff == 512

    with ExitStack() as top:
        def sem(name):
            return top.enter_context(nc.semaphore(name))

        psum = [top.enter_context(nc.psum_tensor(f"bank_pair{i}", [128, 2, 512], F32)) for i in range(2)]
        out_bank = top.enter_context(nc.psum_tensor("out_bank", [128, 512], F32))
        max_bank = [top.enter_context(nc.psum_tensor(f"max_bank{i}", [128, 512], F32)) for i in range(2)]
        misc = top.enter_context(nc.psum_tensor("misc", [128, 512], F32))
        misc16 = misc[:, :].bitcast(F16)

        def sbuf(stack, name, shape, dt=F32):
            return stack.enter_context(nc.sbuf_tensor(name, shape, dt))

        ident = sbuf(top, "ident", [128, 128])
        ident16 = sbuf(top, "ident16", [128, 128], F16)
        yT = sbuf(top, "yT", [128, TOK])
        attention(nc, sem, sbuf, locals())
        experts(nc, sem, sbuf, locals())


def attention(nc, sem, sbuf, v):
    (x, ctx_rows, Wq, Wkv, Wout) = (v[n] for n in ("x", "ctx_rows", "Wq", "Wkv", "Wout"))
    gains = [v[n] for n in ("ln_m_g", "ln_m_b", "ln_l_g", "ln_l_b")]
    NB, S, D, H, HH, HC, QC, TP, CT, NT, QT = (v[n] for n in (
        "NB", "S", "D", "H", "HH", "HC", "QC", "TP", "CT", "NT", "QT"))
    score_banks, out_bank, max_bank, misc, misc16 = (v[n] for n in ("psum", "out_bank", "max_bank", "misc", "misc16"))
    ident, ident16, yT = v["ident"], v["ident16"], v["yT"]

    with ExitStack() as ctx:
        def sb(name, shape, dt=F32):
            return sbuf(ctx, name, shape, dt)

        raw = [sb(f"raw{i}", [128, NT, D]) for i in range(2)]
        stats = sb("stats", [128, NT, 6])
        sm = sb("sm", [128, 10, NT])
        half_pow = sb("half_pow", [128, NT])
        xn = sb("xn", [128, NT, D - 1])
        keys = [sb(f"keys{i}", [128, 2, NT, D], F16) for i in range(4)]
        keysT = [sb(f"keysT{i}", [128, 2, NT, 128], F16) for i in range(4)]
        Q = [sb(f"Q{i}", [128, 2, 2, QC], F16) for i in range(4)]
        A = sb("A", [128, 2, 2, H, 128], F16)
        B = sb("B", [128, 2, 2, H, 128], F16)
        prob = [sb(f"prob{i}", [128, 2 * HC]) for i in range(2)]
        probs = [sb(f"probs{i}", [128, 2, 2 * HC], F16) for i in range(4)]
        part_max = [sb(f"part_max{i}", [128, QT, 4]) for i in range(2)]
        neg_max = sb("neg_max", [128, 2, QT])
        neg_max16 = sb("neg_max16", [128, 2, QT], F16)
        O = [sb(f"O{i}", [128, 2, HC]) for i in range(2)]
        den = sb("den", [1, HC])
        recip = [sb(f"recip{i}", [1, HC]) for i in range(2)]
        recip_all = [sb(f"recip_all{i}", [128, HC]) for i in range(2)]
        On = sb("On", [128, 2, HC])
        Os = sb("Os", [128, 2, 2, QC], F16)
        vecs = sb("vecs", [128, 4])
        vecs64 = sb("vecs64", [128, 2])
        row1 = sb("row1", [1, 128])

        wq_sb = keysT[0][:, :, :, :].rearrange("p a t c -> p (a t c)").bitcast(F32)[:, 0:1024]
        wkv_sb = keysT[1][:, :, :, :].rearrange("p a t c -> p (a t c)").bitcast(F32)[:, 0:1024]
        wv_sb = keysT[2][:, :, :, :].rearrange("p a t c -> p (a t c)").bitcast(F32)[:, 0:1024]
        wout_sb = keysT[3][:, :, :, :].rearrange("p a t c -> p (a t c)").bitcast(F32)[:, 0:1024]
        fold = [Q[j][:, :, :, :].rearrange("p a t c -> p (a t c)").bitcast(F32)[:, 0:1024] for j in range(4)]
        fold.append(Os[:, :, :, :].rearrange("p a t c -> p (a t c)").bitcast(F32)[:, 0:1024])
        const_row = sb("const_row", [128, 128], F16)
        emb = sb("emb", [128, 4, 128])

        weights_in = sem("weights_in")
        passed = sem("passed")
        ident_ready = sem("ident_ready")
        filled = sem("filled")
        emb_ready = sem("emb_ready")
        setup_product = sem("setup_product")
        setup_high = sem("setup_high")
        setup_low = sem("setup_low")
        raw_in = [sem(f"raw_in{i}") for i in range(2)]
        stats_ready = sem("stats_ready")
        small_step = sem("small_step")
        xn_ready = sem("xn_ready")
        high_ready = sem("high_ready")
        keys_ready = sem("keys_ready")
        transposed = sem("transposed")
        q_product = sem("q_product")
        q_high = sem("q_high")
        max_product = sem("max_product")
        max_reduced = sem("max_reduced")
        shift_step = sem("shift_step")
        shift_turned = sem("shift_turned")
        score_ready = sem("score_ready")
        exp_done = sem("exp_done")
        p_high = sem("p_high")
        p_low_v = sem("p_low_v")
        p_low_g = sem("p_low_g")
        pv_done = sem("pv_done")
        misc_free = sem("misc_free")
        out_copied = sem("out_copied")
        den_ready = sem("den_ready")
        recip_ready = sem("recip_ready")
        recip_spread = [sem(f"recip_spread{i}") for i in range(2)]
        on_ready = sem("on_ready")
        os_high = sem("os_high")
        os_ready = sem("os_ready")
        y_product = sem("y_product")

        def count(b, per, extra):
            k, c = b
            return k * (UNROLL * per) + (c * per + extra)

        def wait(eng, s, b, per, extra):
            k, c = b
            if isinstance(k, int) and count(b, per, extra) <= 0:
                return
            eng.wait_ge(s, count(b, per, extra))
            if eng.engine in (nc.gpsimd.engine, nc.sync.engine):
                eng.sem_inc(passed, 1)

        def later(b, d):
            return (b[0], b[1] + d)

        def num(b):
            return b[0] * UNROLL + b[1]

        first, last = -3, NB

        MISC = [(0, "keysT", 2, 3), (1, "lat", -1, 1), (2, "q", 2, 0), (3, "q", 2, 1), (4, "q", 2, 2),
                (5, "q", 2, 3), (6, "y", -1, 0), (7, "keysT", 2, 0), (8, "lat", 0, 0), (9, "keysT", 2, 1),
                (10, "keysT", 2, 2), (11, "shift", 1, 0), (12, "shift", 1, 1)]

        def misc_uses(i):
            return [u for u in MISC if 0 <= i + u[2] < NB]

        STEADY = len(MISC)
        lead_uses = sum(len(misc_uses(i)) for i in range(first, 1)) - STEADY

        def misc_turn(eng, b, slot):
            k, c = b
            if isinstance(k, int):
                n = sum(len(misc_uses(i)) for i in range(first, c))
                n += len([u for u in misc_uses(c) if u[0] < slot])
                if n > 0:
                    eng.wait_ge(misc_free, n)
            else:
                before = len([u for u in MISC if u[0] < slot])
                eng.wait_ge(misc_free, count(b, STEADY, lead_uses + before))

        def steps(eng, run):
            for i in range(first, 1):
                run((0, i), i)
            with eng.Fori(0, (NB - 8) // UNROLL) as k:
                for c in range(1, UNROLL + 1):
                    run((k, c), None)
            for i in range(NB - 7, last + 1):
                run((0, i), i)

        def live(i, d):
            return i is None or 0 <= i + d < NB

        W_OF = (wq_sb, wkv_sb, wkv_sb, wv_sb, wv_sb)
        EMB_OF = (0, 1, 2, 3, 0)
        FOLDS = 2 * 5
        SETUP = [("fold", n, q) for n in range(5) for q in range(2)] + \
                [(m, var, q) for m in "AB" for var in range(2) for q in range(H // 4)]
        A_SCALE = 64 ** -0.5

        def setup_pe(pe):
            for g, (what, n, q) in enumerate(SETUP):
                bank = max_bank[g % 2]
                if g >= 2:
                    pe.wait_ge(setup_low, g - 1)
                if g == FOLDS:
                    pe.wait_ge(setup_low, FOLDS)
                for j in range(4):
                    o = bank[:, 128 * j:128 * j + 128]
                    if what == "fold":
                        t = 4 * q + j
                        mm = nc.tensor.matmul(o, W_OF[n][:, 128 * t:128 * t + 128], emb[:, EMB_OF[n], :],
                                              start=True, stop=True)
                        continue
                    h = 8 * (q // 2) + q % 2 + 2 * j
                    rows, cols = slice(64 * (h % 2), 64 * (h % 2) + 64), slice(128 * (h // 2), 128 * (h // 2) + 128)
                    l, r = (fold[0], fold[1 + n]) if what == "A" else (fold[3 + n], wout_sb)
                    mm = nc.tensor.matmul(o, l[rows, cols], r[rows, cols], start=True, stop=True)
                mm.then_inc(setup_product, 1)
            pe.wait_ge(setup_low, len(SETUP))

        def setup_split(what, n, q):
            first_head = 8 * (q // 2) + q % 2
            dst = (A if what == "A" else B)[:, n, :, first_head:first_head + 7:2, :]
            return dst, A_SCALE if what == "A" else 1.0

        block = ctx.enter_context(nc.Block())

        @block.sync
        def _(sp):
            for n, g in enumerate(gains):
                sp.dma_start(vecs[:, n:n + 1], g.rearrange("(p a) -> p a", a=1)).then_inc(weights_in, 16)
            sp.dma_start(wq_sb, Wq).then_inc(weights_in, 16)
            sp.dma_start(wkv_sb, Wkv[:, 0:H * 64]).then_inc(weights_in, 16)
            sp.dma_start(wv_sb, Wkv[:, H * 64:2 * H * 64]).then_inc(weights_in, 16)
            sp.dma_start(wout_sb.rearrange("p (t n) -> p t n", n=D),
                         Wout.rearrange("(t p) n -> p t n", p=128)).then_inc(weights_in, 16)
            sp.wait_ge(filled, 2)

            def load(b):
                p = b[1] % 2
                sp.dma_start(raw[p][0:TP, 0:CT, :],
                             ctx_rows[num(b)].rearrange("(p t) d -> p t d", t=CT)).then_inc(raw_in[p], 16)
                sp.dma_start(raw[p][0:S, CT, :], x[num(b)]).then_inc(raw_in[p], 16)

            load((0, 0))
            load((0, 1))

            def spread(b, half):
                wait(sp, recip_ready, b, 2, half + 1)
                wait(sp, on_ready, later(b, -1), 2, half + 1)
                sp.dma_start(recip_all[half][:, :], recip[half][0:1, :].unsqueeze(1).to_broadcast([1, 128, HC]))\
                  .then_inc(recip_spread[half], 16)

            def step(b, i):
                if live(i, -1):
                    spread(later(b, -1), 1)
                if live(i, 0):
                    spread(b, 0)
                if live(i, 5):
                    wait(sp, xn_ready, later(b, 3), 7, 7)
                    load(later(b, 5))

            steps(sp, step)

        @block.gpsimd
        def _(pool):
            pool.memset(ident[:, :], 0.0).then_inc(ident_ready, 1)
            pool.wait_ge(ident_ready, 1)
            pool.affine_select(out=ident[:, :], in_=ident[:, :], compare_op=ALU.not_equal, fill=1.0,
                               base=0, pattern=[[-1, 128]], channel_multiplier=1).then_inc(ident_ready, 1)
            pool.wait_ge(ident_ready, 2)
            pool.tensor_copy(ident16[:, :], ident[:, :]).then_inc(ident_ready, 1)
            for t in raw:
                pool.memset(t[:, CT, :], 0.0).then_inc(filled, 1)
            pool.memset(half_pow[:, :], -0.5).then_inc(filled, 1)
            for t in keys:
                pool.memset(t[:, :, :, :], 0.0).then_inc(filled, 1)
            pool.wait_ge(filled, 7)
            for t in keys:
                pool.memset(t[0:TP, 0, 0:CT, 0:1], CONST).then_inc(filled, 1)
                pool.memset(t[0:S, 0, CT, 0:1], CONST).then_inc(filled, 1)
            pool.wait_ge(filled, 15)

            SMALL = 17

            def small(b):
                wait(pool, stats_ready, b, 1, 1)
                n = 0

                def done(ins):
                    nonlocal n
                    n += 1
                    ins.then_inc(small_step, 1)
                    wait(pool, small_step, b, SMALL, n)

                wait(pool, xn_ready, b, 7, 0)
                st = stats[0:TP]
                w = [sm[0:TP, j, :] for j in range(10)]
                done(pool.tensor_tensor(w[0], st[:, :, 1], st[:, :, 4], ALU.add))
                done(pool.tensor_tensor(w[1], st[:, :, 1], st[:, :, 4], ALU.subtract))
                done(pool.tensor_tensor(w[2], st[:, :, 2], st[:, :, 5], ALU.add))
                done(pool.tensor_tensor(w[1], w[1], w[1], ALU.mult))
                done(pool.tensor_scalar(w[2], w[2], 1.0 / D, 0.0, ALU.mult, ALU.add))
                done(pool.tensor_scalar(w[1], w[1], 0.25, 0.0, ALU.mult, ALU.add))
                done(pool.tensor_tensor(w[2], w[2], w[1], ALU.add))
                done(pool.tensor_scalar(w[3], w[2], 1.0, EPS, ALU.mult, ALU.add))
                done(pool.tensor_tensor(w[4], w[3], half_pow[0:TP, :], ALU.pow))
                l2, l4, l5 = (w[j][:, CT:NT] for j in (2, 4, 5))
                done(pool.tensor_tensor(l5, l4, l4, ALU.mult))
                done(pool.tensor_tensor(l5, l5, l2, ALU.mult))
                done(pool.tensor_scalar(l5, l5, 1.0, EPS, ALU.mult, ALU.add))
                done(pool.tensor_tensor(l5, l5, half_pow[0:TP, 0:1], ALU.pow))
                done(pool.tensor_tensor(l4, l4, l5, ALU.mult))
                done(pool.tensor_scalar(w[6], w[4], ZS, 0.0, ALU.mult, ALU.add))
                done(pool.tensor_tensor(w[7], w[6], w[0], ALU.mult))
                done(pool.tensor_scalar(w[7], w[7], -0.5, 0.0, ALU.mult, ALU.add))

            def piece(b, n):
                tiles = range(2 * n, min(2 * n + 2, NT))
                a, e = tiles[0], tiles[-1] + 1
                kb = keys[b[1] % 4]
                if n == 0:
                    wait(pool, pv_done, later(b, -4), NSLOT, NSLOT)
                    wait(pool, keys_ready, b, 7, 0)
                for t in tiles:
                    ins = pool.tensor_scalar(xn[0:TP, t, :], raw[b[1] % 2][0:TP, t, 1:D],
                                             sm[0:TP, 6, t:t + 1], sm[0:TP, 7, t:t + 1], ALU.mult, ALU.add)
                ins.then_inc(xn_ready, 1)
                wait(pool, xn_ready, b, 7, n + 1)
                pool.tensor_copy(kb[0:TP, 0, a:e, 1:D], xn[0:TP, a:e, :]).then_inc(high_ready, 1)
                wait(pool, high_ready, b, 7, n + 1)
                pool.tensor_tensor(kb[0:TP, 1, a:e, 1:D], xn[0:TP, a:e, :], kb[0:TP, 0, a:e, 1:D],
                                   ALU.subtract).then_inc(keys_ready, 1)

            def step(b, i):
                for k in range(NSLOT):
                    if live(i, 0) and k % 7 != 6:
                        u = count(b, NSLOT, k)
                        wait(pool, p_high, b, NSLOT, k + 1)
                        pb = probs[(2 * b[1] + k) % 4]
                        pool.tensor_tensor(pb[:, 1, HC:], prob[k % 2][:, HC:], pb[:, 0, HC:],
                                           ALU.subtract).then_inc(p_low_g, 1)
                    if live(i, 3):
                        if k == 2:
                            small(later(b, 3))
                        if k in (3, 5, 7, 9, 11, 12, 13):
                            piece(later(b, 3), (3, 5, 7, 9, 11, 12, 13).index(k))

            steps(pool, step)

        @block.tensor
        def _(pe):
            PASSES = ((0, 0), (0, 1), (1, 0))
            pe.wait_ge(ident_ready, 3)
            pe.wait_ge(weights_in, 16 * 8)
            pe.wait_ge(emb_ready, 15)
            setup_pe(pe)

            def scores(b, k):
                qb, kb = Q[b[1] % 4], keysT[b[1] % 4]
                half, p = divmod(k, 7)
                wait(pe, exp_done, b, NSLOT, k - 1)
                if k == 0:
                    misc_turn(pe, b, 0)
                cols = slice(half * HC, half * HC + HC)
                for j, t in enumerate(range(2 * p, min(2 * p + 2, NT))):
                    var = int(t == CT)
                    o = score_banks[k % 2][:, j, 0:HC]
                    for n, (ks, qs) in enumerate(PASSES):
                        mm = nc.tensor.matmul(o, kb[:, ks, t, :], qb[:, var, qs, cols],
                                              start=(n == 0), stop=(n == 2 and not var))
                    if var:
                        for qs in range(2):
                            mm = nc.tensor.matmul(o, const_row[:, :], qb[:, 0, qs, cols],
                                                  start=False, stop=(qs == 1))
                mm.then_inc(score_ready, 1)

            def values(b, k):
                half, p = divmod(k, 7)
                kb, pb = keys[b[1] % 4], probs[(2 * b[1] + k) % 4]
                wait(pe, p_low_v, b, NSLOT, k + 1)
                wait(pe, p_low_g, b, 12, (k + 1) - (k + 1) // 7)
                if p == 0:
                    wait(pe, out_copied, b, 2, half)
                for j, t in enumerate(range(2 * p, min(2 * p + 2, NT))):
                    o = misc[:, 0:HC] if t == CT else out_bank[:, 0:HC]
                    for n, (ks, ps) in enumerate(PASSES):
                        mm = nc.tensor.matmul(o, kb[:, ks, t, :], pb[:, ps, j * HC:j * HC + HC],
                                              start=(n == 0 and t in (0, CT)), stop=(n == 2 and t in (CT - 1, CT)))
                mm.then_inc(pv_done, 1)

            def maxima(b, t, j):
                qb, kb = Q[b[1] % 4], keysT[b[1] % 4]
                if t == 0 and j == 0:
                    misc_turn(pe, later(b, -2), 11)
                wait(pe, max_reduced, b, 4 * QT, 4 * t + j - 1)
                if j < 3:
                    o, rhs = max_bank[j % 2][:, 0:4 * TP], kb[:, 0, 4 * j:4 * j + 4, 0:TP]
                else:
                    o, rhs = max_bank[1][:, 0:S], kb[:, 0, CT, 0:S]
                nc.tensor.matmul(o, qb[:, int(j == 3), 0, 128 * t:128 * t + 128], rhs,
                                 start=True, stop=True).then_inc(max_product, 1)

            def turn_keys(b, j):
                kb = keys[b[1] % 4]
                wait(pe, keys_ready, b, 7, 7)
                tiles = range(4 * j, min(4 * j + 4, NT))
                o = misc16.rearrange("p (a t c) -> p a t c", a=2, t=4)
                for a in range(2):
                    for t in tiles:
                        mm = nc.tensor.transpose(o[:, a, t - 4 * j, :], kb[:, a, t, :], ident16[:, :])
                mm.then_inc(transposed, 1)

            def queries(b, w):
                var, half = divmod(w, 2)
                kb = keysT[b[1] % 4]
                for h in range(HH):
                    for n, (a, z) in enumerate(PASSES):
                        mm = nc.tensor.matmul(misc[:, h * S:h * S + S], A[:, var, a, half * HH + h, :],
                                              kb[:, z, CT, 0:S], start=(n == 0), stop=(n == 2))
                mm.then_inc(q_product, 1)

            def shift(b, a):
                if a == 0:
                    wait(pe, shift_step, b, 4, 4)
                for t in range(QT):
                    mm = nc.tensor.transpose(misc16[0:1, 128 * t:128 * t + 128], neg_max16[:, a, t:t + 1],
                                             ident16[:, :])
                mm.then_inc(shift_turned, 1)

            def project(b):
                wait(pe, os_ready, b, 2, 2)
                n = 0
                for var in range(2):
                    for h in range(H):
                        for w, o in PASSES:
                            mm = nc.tensor.matmul(misc[:, 0:S], B[:, var, w, h, :],
                                                  Os[:, o, var, h * S:h * S + S],
                                                  start=(n == 0), stop=(n == 6 * H - 1))
                            n += 1
                mm.then_inc(y_product, 1)

            def misc_use(b, i, k):
                for slot, what, d, part in MISC:
                    if slot != k or not live(i, d):
                        continue
                    misc_turn(pe, b, slot)
                    g = later(b, d)
                    if what == "keysT":
                        turn_keys(g, part)
                    if what == "q":
                        queries(g, part)
                    if what == "y":
                        project(g)
                    if what == "shift":
                        shift(g, part)

            def chunks(b, i, k, which):
                m = k + 3
                d, m = (1, m) if m < NSLOT else (2, m - NSLOT)
                if live(i, d):
                    maxima(later(b, d), m // 2, 2 * (m % 2) + which)

            def step(b, i):
                for k in range(NSLOT):
                    if live(i, 0):
                        scores(b, k)
                    chunks(b, i, k, 0)
                    misc_use(b, i, k)
                    chunks(b, i, k, 1)
                    if k >= 2 and live(i, 0):
                        values(b, k - 2)
                    if k < 2 and live(i, -1):
                        values(later(b, -1), k + 12)

            steps(pe, step)

        @block.scalar
        def _(act):
            for g, (what, n, q) in enumerate(SETUP):
                if what == "fold":
                    continue
                dst, scale = setup_split(what, n, q)
                act.wait_ge(setup_product, g + 1)
                act.activation(dst[:, 0], max_bank[g % 2][:, :].rearrange("p (h c) -> p h c", h=4), ACT.Copy,
                               scale=scale).then_inc(setup_high, 1)

            def soften(b, k):
                w = HC if k % 7 == 6 else 2 * HC
                wait(act, score_ready, b, NSLOT, k + 1)
                wait(act, p_low_v, b, NSLOT, k - 1)
                wait(act, p_low_g, b, 12, (k - 1) - (k - 1) // 7)
                act.activation(prob[k % 2][:, 0:w].rearrange("p (j c) -> p j c", c=HC),
                               score_banks[k % 2][:, 0:w // HC, 0:HC], ACT.Exp,
                               scale=1.0 / CONST).then_inc(exp_done, 1)
                wait(act, exp_done, b, NSLOT, k + 1)
                wait(act, pv_done, b, NSLOT, k - 3)
                act.activation(probs[(2 * b[1] + k) % 4][:, 0, 0:w], prob[k % 2][:, 0:w],
                               ACT.Copy).then_inc(p_high, 1)

            def misc_copy(b, i, k):
                for slot, what, d, part in MISC:
                    if slot != k or not live(i, d):
                        continue
                    g = later(b, d)
                    qb = Q[g[1] % 4]
                    if what == "keysT":
                        wait(act, transposed, g, 4, (part + 1) % 4 + 1)
                        tiles = slice(4 * part, min(4 * part + 4, NT))
                        src = misc16.rearrange("p (a t c) -> p a t c", a=2, t=4)
                        act.activation(keysT[g[1] % 4][:, :, tiles, :], src[:, :, 0:tiles.stop - tiles.start, :],
                                       ACT.Copy).then_inc(misc_free, 1)
                    if what == "q":
                        var, half = divmod(part, 2)
                        wait(act, q_product, g, 4, part + 1)
                        act.activation(qb[:, var, 0, half * HC:half * HC + HC], misc[:, 0:HC], ACT.Copy,
                                       scale=1.0 / CONST).then_inc(q_high, 1)
                    if what == "y":
                        wait(act, y_product, g, 1, 1)
                        act.activation(yT[:, bass.ds(num(g) * S, S)], misc[:, 0:S], ACT.Copy,
                                       scale=1.0 / CONST).then_inc(misc_free, 1)
                    if what == "shift":
                        wait(act, shift_turned, g, 2, part + 1)
                        act.activation(qb[0:1, 0, part, :], misc16[0:1, 0:QC], ACT.Copy).then_inc(misc_free, 1)

            def step(b, i):
                for k in range(NSLOT):
                    if live(i, 0):
                        soften(b, k)
                    misc_copy(b, i, k)

            steps(act, step)

        @block.vector
        def _(dve):
            dve.memset(row1[:, :], -CONST / ZS).then_inc(emb_ready, 1)
            dve.memset(const_row[:, :], 0.0).then_inc(emb_ready, 1)
            dve.wait_ge(emb_ready, 2)
            dve.memset(const_row[0:1, 0:S], CONST).then_inc(emb_ready, 1)
            dve.wait_ge(ident_ready, 3)
            dve.wait_ge(weights_in, 16 * 8)
            gm, bm, gl, bl = (vecs[:, n:n + 1] for n in range(4))
            EMB = (gl, gm, gl, gm)
            for e, gain in enumerate(EMB):
                dve.tensor_scalar(emb[:, e, :], ident[:, :], gain, CONST / ZS, ALU.mult, ALU.mult)\
                   .then_inc(emb_ready, 1)
            dve.wait_ge(emb_ready, 7)
            for e, gain in enumerate(EMB):
                dve.tensor_scalar(emb[0:1, e, 1:128], row1[0:1, 1:128], gain[0:1, :], 1.0, ALU.mult,
                                  ALU.mult).then_inc(emb_ready, 1)
            dve.tensor_copy(emb[:, 0, 0:1], bl).then_inc(emb_ready, 1)
            dve.memset(emb[:, 1, 0:1], 0.0).then_inc(emb_ready, 1)
            dve.tensor_tensor(emb[:, 2, 0:1], bl, bm, ALU.subtract).then_inc(emb_ready, 1)
            dve.tensor_copy(emb[:, 3, 0:1], bm).then_inc(emb_ready, 1)
            for g, (what, n, q) in enumerate(SETUP):
                bank = max_bank[g % 2][:, :]
                if what == "fold":
                    dve.wait_ge(setup_product, g + 1)
                    dve.tensor_copy(fold[n][:, 512 * q:512 * q + 512], bank).then_inc(setup_low, 1)
                else:
                    dst, scale = setup_split(what, n, q)
                    dve.wait_ge(setup_high, g + 1 - FOLDS)
                    dve.scalar_tensor_tensor(out=dst[:, 1], in0=bank.rearrange("p (h c) -> p h c", h=4),
                                             scalar=scale, in1=dst[:, 0], op0=ALU.mult,
                                             op1=ALU.subtract).then_inc(setup_low, 1)

            def reduce_max(b, t, j):
                wait(dve, max_product, b, 4 * QT, 4 * t + j + 1)
                if t == 0 and j == 0:
                    wait(dve, shift_step, later(b, -2), 4, 1)
                w = 4 * TP if j < 3 else S
                dve.reduce_max(part_max[b[1] % 2][:, t, j:j + 1], max_bank[j % 2][:, 0:w], AX.X)\
                   .then_inc(max_reduced, 1)

            def make_shift(b):
                wait(dve, max_reduced, b, 4 * QT, 4 * QT)
                wait(dve, shift_turned, later(b, -1), 2, 2)
                dve.tensor_reduce(neg_max[:, 0, :], part_max[b[1] % 2][:, :, :], AX.X, ALU.max,
                                  negate=True).then_inc(shift_step, 1)
                wait(dve, shift_step, b, 4, 1)
                dve.tensor_scalar(neg_max[:, 1, :], neg_max[:, 0, :], 1.0 / CONST, PSHIFT, ALU.mult, ALU.add)\
                   .then_inc(shift_step, 1)
                wait(dve, shift_step, b, 4, 2)
                dve.tensor_copy(neg_max16[:, 0, :], neg_max[:, 1, :]).then_inc(shift_step, 1)
                wait(dve, shift_step, b, 4, 3)
                dve.tensor_tensor(neg_max16[:, 1, :], neg_max[:, 1, :], neg_max16[:, 0, :],
                                  ALU.subtract).then_inc(shift_step, 1)

            def low(b, k):
                pb = probs[(2 * b[1] + k) % 4]
                wait(dve, p_high, b, NSLOT, k + 1)
                dve.tensor_tensor(pb[:, 1, 0:HC], prob[k % 2][:, 0:HC], pb[:, 0, 0:HC],
                                  ALU.subtract).then_inc(p_low_v, 1)

            def query_low(b, w):
                var, half = divmod(w, 2)
                cols = slice(half * HC, half * HC + HC)
                qb = Q[b[1] % 4]
                wait(dve, q_high, b, 4, w + 1)
                dve.scalar_tensor_tensor(out=qb[:, var, 1, cols], in0=misc[:, 0:HC], scalar=1.0 / CONST,
                                         in1=qb[:, var, 0, cols], op0=ALU.mult,
                                         op1=ALU.subtract).then_inc(misc_free, 1)

            def statistics(b, part):
                if part == 0:
                    k, c = b
                    dve.wait_ge(raw_in[c % 2], k * (UNROLL // 2 * 32) + (c // 2 * 32 + 32))
                    wait(dve, small_step, b, 17, 0)
                for t in range(5 * part, min(5 * part + 5, NT)):
                    ins = dve.bn_stats(stats[0:TP, t, :], raw[b[1] % 2][0:TP, t, :])
                if part == 2:
                    ins.then_inc(stats_ready, 1)

            def out_copy(b, half):
                wait(dve, pv_done, b, NSLOT, 7 * half + 6)
                wait(dve, on_ready, later(b, -1), 2, half + 1)
                dve.tensor_copy(O[half][:, 0, :], out_bank[:, 0:HC]).then_inc(out_copied, 1)

            def denominator(b, half):
                wait(dve, pv_done, b, NSLOT, 7 * half + 7)
                dve.tensor_copy(O[half][:, 1, :], misc[:, 0:HC]).then_inc(misc_free, 1)
                misc_turn(dve, later(b, half), 2 if half else 9)
                wait(dve, out_copied, b, 2, half + 1)
                dve.tensor_tensor(den[:, :], O[half][0:1, 0, :], O[half][0:1, 1, :], ALU.add)\
                   .then_inc(den_ready, 1)
                wait(dve, den_ready, b, 2, half + 1)
                k, c = b
                dve.reciprocal(recip[half][:, :], den[:, :]).then_inc(recip_ready, 1)

            def normalise(b, half):
                k, c = b
                if isinstance(k, int):
                    dve.wait_ge(recip_spread[half], 16 * (c + 1))
                else:
                    dve.wait_ge(recip_spread[half], k * (UNROLL * 16) + 16 * (c + 1))
                wait(dve, os_ready, b, 2, half)
                rb = recip_all[half][:, :].unsqueeze(1).to_broadcast([128, 2, HC])
                dve.scalar_tensor_tensor(out=On[:, :, :], in0=O[half][:, :, :], scalar=CONST, in1=rb,
                                         op0=ALU.mult, op1=ALU.mult).then_inc(on_ready, 1)
                wait(dve, on_ready, b, 2, half + 1)
                if half == 0:
                    wait(dve, y_product, b, 1, 0)
                cols = slice(half * HC, half * HC + HC)
                dve.tensor_copy(Os[:, 0, :, cols], On[:, :, :]).then_inc(os_high, 1)

            def normal_low(b, half):
                wait(dve, os_high, b, 2, half + 1)
                cols = slice(half * HC, half * HC + HC)
                dve.tensor_tensor(Os[:, 1, :, cols], On[:, :, :], Os[:, 0, :, cols],
                                  ALU.subtract).then_inc(os_ready, 1)

            def step(b, i):
                for k in range(NSLOT):
                    m = k + 3
                    d, m = (1, m) if m < NSLOT else (2, m - NSLOT)
                    if live(i, d):
                        reduce_max(later(b, d), m // 2, 2 * (m % 2))
                    if live(i, 0):
                        low(b, k)
                    if k in (2, 3, 4, 5) and live(i, 2):
                        query_low(later(b, 2), k - 2)
                    if live(i, d):
                        reduce_max(later(b, d), m // 2, 2 * (m % 2) + 1)
                    if k == 0 and live(i, -1):
                        out_copy(later(b, -1), 1)
                    if k == 1 and live(i, -1):
                        denominator(later(b, -1), 1)
                    if k == 7 and live(i, 0):
                        out_copy(b, 0)
                    if k == 8 and live(i, 0):
                        denominator(b, 0)
                    if k == 4 and live(i, -1):
                        normalise(later(b, -1), 1)
                    if k == 5 and live(i, -1):
                        normal_low(later(b, -1), 1)
                    if k == 11 and live(i, 0):
                        normalise(b, 0)
                    if k == 12 and live(i, 0):
                        normal_low(b, 0)
                    if k == 10 and live(i, 1):
                        make_shift(later(b, 1))
                    if k < 3 and live(i, 3):
                        statistics(later(b, 3), k)

            steps(dve, step)


def experts(nc, sem, sbuf, v):
    NB, S, TOK, D, E, Dff = (v[n] for n in ("NB", "S", "TOK", "D", "E", "Dff"))
    x, out, gate_w, w1, b1, w2, b2 = (v[n] for n in ("x", "out", "gate_w", "w1", "b1", "w2", "b2"))
    yT, ident = v["yT"], v["ident"]
    h_banks, y_banks = v["psum"]
    turn_bank = [v["out_bank"], v["misc"]]
    weight_bank = v["max_bank"]
    T = TOK // 128
    FC = Dff // 128
    GROUPS = [range(g, min(g + 4, T)) for g in range(0, T, 4)]
    UNITS = len(GROUPS) * FC
    W1S, W2S, GS = 64.0, 256.0, 16.0
    x_rows = x.rearrange("b s d -> (b s) d").rearrange("(t p) d -> p t d", p=128)
    out_rows = out.rearrange("b s d -> (b s) d").rearrange("(t p) d -> p t d", p=128)

    with ExitStack() as ctx:
        def sb(name, shape, dt=F32):
            return sbuf(ctx, name, shape, dt)

        acc = sb("acc", [128, T, D])
        xm = sb("xm", [128, T, D])
        xmT = sb("xmT", [128, T * 128])
        xmTs = sb("xmTs", [128, 2, T * 128], F16)
        st = sb("st", [128, T, 6])
        mv = sb("mv", [128, T, 2])
        rstd = sb("rstd", [128, T])
        powers = sb("powers", [128, T])
        gate = sb("gate", [E, D])
        gateT = sb("gateT", [128, E])
        b1_rows = sb("b1_rows", [E * FC, 128])
        b1T = sb("b1T", [128, E * FC])
        b1_now = [sb(f"b1_now{i}", [128, FC]) for i in range(2)]
        b2_rows = sb("b2_rows", [E, D])
        logit = sb("logit", [128, T, E])
        p = sb("p", [128, T, E])
        above = sb("above", [128, T, E])
        rank = sb("rank", [128, T, E])
        col = sb("col", [128, 3, T])
        wgt = sb("wgt", [128, T, E])
        wgt_s = sb("wgt_s", [128, T, E])
        wgtT = sb("wgtT", [E, T * 128])
        w1n = [sb(f"w1n{i}", [128, FC, D]) for i in range(2)]
        w2n = [sb(f"w2n{i}", [128, FC, 128]) for i in range(2)]
        w1T = [sb(f"w1T{i}", [128, 2, Dff], F16) for i in range(2)]
        w2T = [sb(f"w2T{i}", [128, 2, Dff], F16) for i in range(2)]
        g32 = [sb(f"g32_{i}", [128, 512]) for i in range(2)]
        gs = [sb(f"gs{i}", [128, 2, 512], F16) for i in range(4)]

        x_in = sem("x_in")
        small_in = sem("small_in")
        weights_in = [sem(f"expert_in{i}") for i in range(2)]
        y_turned = sem("y_turned")
        residual = sem("residual")
        row_stats = sem("row_stats")
        token_stats = sem("token_stats")
        power_step = sem("power_step")
        token_norm = sem("token_norm")
        small_turned = sem("small_turned")
        small_copied = sem("small_copied")
        x_turned = sem("x_turned")
        xT_copied = sem("xT_copied")
        xT_high = sem("xT_high")
        xT_low = sem("xT_low")
        logits_ready = sem("logits_ready")
        route_step = sem("route_step")
        route_exp = sem("route_exp")
        weights_turned = sem("weights_turned")
        weights_high = sem("weights_high")
        weights_low = sem("weights_low")
        b1_ready = sem("b1_ready")
        h_ready = sem("h_ready")
        gelu_done = sem("gelu_done")
        g_high = sem("g_high")
        g_low = sem("g_low")
        y_done = sem("y_done")
        y_added = sem("y_added")
        wgt_turned = sem("wgt_turned")
        wgt_copied = sem("wgt_copied")
        bias_ready = sem("bias_ready")
        bias_added = sem("bias_added")
        stored = sem("stored")
        passed = sem("passed2")

        def wait(eng, s, e, per, extra):
            k, c = e
            n = k * (2 * per) + (c * per + extra)
            if isinstance(k, int) and n <= 0:
                return
            eng.wait_ge(s, n)
            if eng.engine == nc.sync.engine:
                eng.sem_inc(passed, 1)

        def run_experts(eng, body):
            body((0, 0))
            with eng.Fori(0, (E - 2) // 2) as k:
                body((k, 1))
                body((k, 2))
            body((0, E - 1))

        def is_first(e):
            return isinstance(e[0], int) and e[1] == 0

        def is_last(e):
            return isinstance(e[0], int) and e[1] == E - 1

        def nxt(e, d=1):
            return (e[0], e[1] + d)

        def width(g):
            return 128 * len(GROUPS[g])

        block = ctx.enter_context(nc.Block())

        @block.sync
        def _(sp):
            sp.dma_start(acc[:, :, :], x_rows).then_inc(x_in, 16)
            sp.dma_start(gate[:, :], gate_w).then_inc(small_in, 16)
            sp.dma_start(b1_rows[:, :], b1.rearrange("e (c f) -> (e c) f", f=128)).then_inc(small_in, 16)
            sp.dma_start(b2_rows[:, :], b2).then_inc(small_in, 16)

            def load(e):
                n = e[0] * 2 + e[1]
                s = weights_in[e[1] % 2]
                wait(sp, weights_turned, nxt(e, -2), 2, 2)
                sp.dma_start(w1n[e[1] % 2][:, :, :], w1[:, bass.ds(n, 1), :].rearrange(
                    "(c f) e d -> f (c e) d", f=128)).then_inc(s, 16)
                sp.dma_start(w2n[e[1] % 2][:, :, :], w2[:, bass.ds(n, 1), :].rearrange(
                    "d e (c f) -> d (e c) f", f=128)).then_inc(s, 16)

            load((0, 0))
            load((0, 1))
            with sp.Fori(0, (E - 2) // 2) as k:
                load((k, 2))
                load((k, 3))
            sp.wait_ge(y_added, E * len(GROUPS))
            sp.dma_start(out_rows, acc[:, :, :]).then_inc(stored, 16)
            sp.wait_ge(stored, 16)

        @block.gpsimd
        def _(pool):
            pool.memset(powers[:, :], -0.5).then_inc(power_step, 1)
            pool.wait_ge(power_step, 1)
            pool.wait_ge(token_stats, T)
            pool.tensor_scalar(rstd[:, :], mv[:, :, 1], 1.0, EPS, ALU.mult, ALU.add).then_inc(power_step, 1)
            pool.wait_ge(power_step, 2)
            pool.tensor_tensor(rstd[:, :], rstd[:, :], powers[:, :], ALU.pow).then_inc(power_step, 1)

        @block.tensor
        def _(pe):
            PASSES = ((0, 0), (0, 1), (1, 0))
            for t in range(T):
                if t >= 2:
                    pe.wait_ge(residual, t - 1)
                nc.tensor.transpose(turn_bank[t % 2][:, 0:128], yT[:, 128 * t:128 * t + 128], ident[:, :])\
                  .then_inc(y_turned, 1)
            pe.wait_ge(small_in, 48)
            nc.tensor.transpose(weight_bank[0][:, 0:E], gate[:, :], ident[0:E, 0:E]).then_inc(small_turned, 1)
            nc.tensor.transpose(weight_bank[1][:, 0:E * FC], b1_rows[:, :], ident[0:E * FC, 0:E * FC])\
              .then_inc(small_turned, 1)
            pe.wait_ge(small_copied, 2)

            def turn_weights(e, m):
                wait(pe, weights_in[e[1] % 2], (e[0], e[1] // 2 * 2), 16, 32)
                wait(pe, weights_low, nxt(e, -1), 2, m + 1)
                src = (w1n, w2n)[m][e[1] % 2]
                for c in range(FC):
                    mm = nc.tensor.transpose(weight_bank[m][:, 128 * c:128 * c + 128], src[:, c, :], ident[:, :])
                mm.then_inc(weights_turned, 1)

            turn_weights((0, 0), 0)
            turn_weights((0, 0), 1)
            pe.wait_ge(token_norm, T)
            for g, tiles in enumerate(GROUPS):
                if g >= 2:
                    pe.wait_ge(xT_low, g - 1)
                for j, t in enumerate(tiles):
                    mm = nc.tensor.transpose(turn_bank[g % 2][:, 128 * j:128 * j + 128], xm[:, t, :], ident[:, :])
                mm.then_inc(x_turned, 1)
            pe.wait_ge(xT_low, len(GROUPS))
            for t in range(T):
                mm = nc.tensor.matmul(turn_bank[0][:, E * t:E * t + E], xmT[:, 128 * t:128 * t + 128], gateT[:, :],
                                      start=True, stop=True)
            mm.then_inc(logits_ready, 1)
            def turn_router(part):
                pe.wait_ge(wgt_copied, part - 1) if part >= 2 else None
                for j, t in enumerate(GROUPS[part]):
                    mm = nc.tensor.transpose(turn_bank[part % 2][0:E, 128 * j:128 * j + 128], wgt[:, t, :],
                                             ident[:, :])
                mm.then_inc(wgt_turned, 1)

            def hidden(e, u):
                g, c = divmod(u, FC)
                w = width(g)
                if u == 0:
                    wait(pe, weights_low, e, 2, 2)
                wait(pe, gelu_done, e, UNITS, u - 1)
                for n, (a, z) in enumerate(PASSES):
                    mm = nc.tensor.matmul(h_banks[:, u % 2, 0:w], w1T[e[1] % 2][:, a, 128 * c:128 * c + 128],
                                          xmTs[:, z, 512 * g:512 * g + w], start=(n == 0), stop=(n == 2))
                mm.then_inc(h_ready, 1)

            def outputs(e, u):
                g, c = divmod(u, FC)
                wait(pe, g_low, e, UNITS, u + 1)
                if c == 0:
                    wait(pe, y_added, e, len(GROUPS), g - 1)
                for j in range(len(GROUPS[g])):
                    for n, (z, a) in enumerate(PASSES):
                        mm = nc.tensor.matmul(y_banks[:, g % 2, 128 * j:128 * j + 128],
                                              gs[u % 4][:, z, 128 * j:128 * j + 128],
                                              w2T[e[1] % 2][:, a, 128 * c:128 * c + 128],
                                              start=(c == 0 and j == 0 and n == 0),
                                              stop=(c == FC - 1 and n == 2), skip_group_check=True)
                mm.then_inc(y_done, 1)

            def body(e):
                for u in range(UNITS):
                    hidden(e, u)
                    if u in (4, 8) and not is_last(e):
                        turn_weights(nxt(e), u // 4 - 1)
                    if u >= 2:
                        outputs(e, u - 2)
                    elif not is_first(e):
                        outputs(nxt(e, -1), u + UNITS - 2)
                    if is_first(e) and u == 3:
                        pe.wait_ge(route_step, ROUTE_STEPS)
                        for part in range(len(GROUPS)):
                            turn_router(part)
                        pe.wait_ge(wgt_copied, len(GROUPS))
                        for part, tiles in enumerate(GROUPS):
                            if part >= 2:
                                pe.wait_ge(bias_added, part - 1)
                            for j, t in enumerate(tiles):
                                mm = nc.tensor.matmul(turn_bank[part % 2][:, 128 * j:128 * j + 128],
                                                      wgtT[:, 128 * t:128 * t + 128], b2_rows[:, :],
                                                      start=True, stop=True)
                            mm.then_inc(bias_ready, 1)

            run_experts(pe, body)
            outputs((0, E - 1), UNITS - 2)
            outputs((0, E - 1), UNITS - 1)

        @block.scalar
        def _(act):
            act.wait_ge(small_turned, 2)
            act.activation(gateT[:, :], weight_bank[0][:, 0:E], ACT.Copy).then_inc(small_copied, 1)
            act.activation(b1T[:, :], weight_bank[1][:, 0:E * FC], ACT.Copy).then_inc(small_copied, 1)
            act.wait_ge(small_copied, 2)

            def weights_split(e, m):
                wait(act, weights_turned, e, 2, m + 1)
                act.activation((w1T, w2T)[m][e[1] % 2][:, 0, :], weight_bank[m][:, :], ACT.Copy,
                               scale=(W1S, W2S)[m]).then_inc(weights_high, 1)

            weights_split((0, 0), 0)
            weights_split((0, 0), 1)
            for g, tiles in enumerate(GROUPS):
                cols = slice(512 * g, 512 * g + 128 * len(tiles))
                act.wait_ge(x_turned, g + 1)
                src = turn_bank[g % 2][:, 0:128 * len(tiles)]
                act.activation(xmT[:, cols], src, ACT.Copy).then_inc(xT_copied, 1)
                act.activation(xmTs[:, 0, cols], src, ACT.Copy, scale=ZS).then_inc(xT_high, 1)
            act.wait_ge(route_step, 2)
            act.activation(p[:, :, :], logit[:, :, :], ACT.Exp).then_inc(route_exp, 1)

            def body(e):
                n = e[0] * (2 * FC) + e[1] * FC
                b1_e = b1_now[e[1] % 2]
                act.activation(b1_e[:, :], b1T[:, bass.ds(n, FC)], ACT.Copy).then_inc(b1_ready, 1)
                wait(act, b1_ready, e, 1, 1)
                for u in range(UNITS):
                    g, c = divmod(u, FC)
                    w = width(g)
                    wait(act, h_ready, e, UNITS, u + 1)
                    wait(act, g_low, e, UNITS, u - 1)
                    act.activation(g32[u % 2][:, 0:w], h_banks[:, u % 2, 0:w], ACT.Gelu_apprx_tanh,
                                   bias=b1_e[:, c:c + 1],
                                   scale=1.0 / (W1S * ZS)).then_inc(gelu_done, 1)
                    wait(act, gelu_done, e, UNITS, u + 1)
                    wait(act, y_done, e, UNITS, u - 3)
                    act.activation(gs[u % 4][:, 0, 0:w], g32[u % 2][:, 0:w], ACT.Copy, scale=GS).then_inc(g_high, 1)
                    if u in (4, 8) and not is_last(e):
                        weights_split(nxt(e), u // 4 - 1)

            run_experts(act, body)

        @block.vector
        def _(dve):
            dve.wait_ge(x_in, 16)
            for t in range(T):
                dve.wait_ge(y_turned, t + 1)
                dve.tensor_tensor(acc[:, t, :], turn_bank[t % 2][:, 0:128], acc[:, t, :], ALU.add)\
                   .then_inc(residual, 1)
            for t in range(T):
                dve.wait_ge(residual, t + 1)
                dve.bn_stats(st[:, t, :], acc[:, t, :]).then_inc(row_stats, 1)
            for t in range(T):
                dve.wait_ge(row_stats, t + 1)
                ins = dve.bn_aggr(mv[:, t, :], st[:, t, :])
                ins.then_inc(token_stats, 1)
            dve.wait_ge(power_step, 3)
            for t in range(T):
                dve.tensor_scalar(xm[:, t, :], acc[:, t, :], mv[:, t, 0:1], rstd[:, t:t + 1], ALU.subtract,
                                  ALU.mult).then_inc(token_norm, 1)

            def weights_split(e, m):
                wait(dve, weights_high, e, 2, m + 1)
                dst = (w1T, w2T)[m][e[1] % 2]
                dve.scalar_tensor_tensor(out=dst[:, 1, :], in0=weight_bank[m][:, :], scalar=(W1S, W2S)[m],
                                         in1=dst[:, 0, :], op0=ALU.mult, op1=ALU.subtract)\
                   .then_inc(weights_low, 1)

            weights_split((0, 0), 0)
            weights_split((0, 0), 1)
            for g, tiles in enumerate(GROUPS):
                cols = slice(512 * g, 512 * g + 128 * len(tiles))
                dve.wait_ge(xT_high, g + 1)
                dve.scalar_tensor_tensor(out=xmTs[:, 1, cols], in0=turn_bank[g % 2][:, 0:128 * len(tiles)], scalar=ZS,
                                         in1=xmTs[:, 0, cols], op0=ALU.mult, op1=ALU.subtract).then_inc(xT_low, 1)

            n = 0

            def done(ins):
                nonlocal n
                n += 1
                ins.then_inc(route_step, 1)
                dve.wait_ge(route_step, n)

            def spread(ap):
                return ap.to_broadcast([128, T, E])

            dve.wait_ge(logits_ready, 1)
            logits = turn_bank[0][:, 0:T * E].rearrange("p (t e) -> p t e", e=E)
            done(dve.tensor_reduce(col[:, 0, :], logits, AX.X, ALU.max))
            done(dve.tensor_tensor(logit[:, :, :], logits, spread(col[:, 0, :].unsqueeze(2)), ALU.subtract))
            dve.wait_ge(route_exp, 1)
            done(dve.tensor_reduce(col[:, 1, :], p[:, :, :], AX.X, ALU.add))
            done(dve.reciprocal(col[:, 2, :], col[:, 1, :]))
            done(dve.tensor_tensor(p[:, :, :], p[:, :, :], spread(col[:, 2, :].unsqueeze(2)), ALU.mult))
            done(dve.memset(rank[:, :, :], 0.0))
            for e in range(E):
                for part, op in ((slice(0, e + 1), ALU.is_gt), (slice(e + 1, E), ALU.is_ge)):
                    w = part.stop - part.start
                    if w:
                        done(dve.tensor_tensor(above[:, :, part], p[:, :, e:e + 1].to_broadcast([128, T, w]),
                                               p[:, :, part], op))
                done(dve.tensor_tensor(rank[:, :, :], rank[:, :, :], above[:, :, :], ALU.add))
            done(dve.tensor_scalar(rank[:, :, :], rank[:, :, :], 2.0, 1.0, ALU.is_lt, ALU.mult))
            done(dve.tensor_tensor(wgt[:, :, :], p[:, :, :], rank[:, :, :], ALU.mult))
            done(dve.tensor_scalar(wgt_s[:, :, :], wgt[:, :, :], 1.0 / (W2S * GS), 1.0, ALU.mult, ALU.mult))
            assert n == ROUTE_STEPS

            def add_outputs(e, g):
                wait(dve, y_done, e, UNITS, FC * g + FC)
                k, c = e
                for j, t in enumerate(GROUPS[g]):
                    s = wgt_s[:, t, c:c + 1] if isinstance(k, int) else wgt_s[:, t, bass.ds(k * 2 + c, 1)]
                    ins = dve.scalar_tensor_tensor(out=acc[:, t, :], in0=y_banks[:, g % 2, 128 * j:128 * j + 128],
                                                   scalar=s, in1=acc[:, t, :], op0=ALU.mult, op1=ALU.add)
                ins.then_inc(y_added, 1)

            def body(e):
                for u in range(UNITS):
                    g, c = divmod(u, FC)
                    w = width(g)
                    wait(dve, g_high, e, UNITS, u + 1)
                    dve.scalar_tensor_tensor(out=gs[u % 4][:, 1, 0:w], in0=g32[u % 2][:, 0:w], scalar=GS,
                                             in1=gs[u % 4][:, 0, 0:w], op0=ALU.mult,
                                             op1=ALU.subtract).then_inc(g_low, 1)
                    if u in (4, 8) and not is_last(e):
                        weights_split(nxt(e), u // 4 - 1)
                    if is_first(e) and u == 3:
                        for part, tiles in enumerate(GROUPS):
                            dve.wait_ge(wgt_turned, part + 1)
                            dve.tensor_copy(wgtT[:, 512 * part:512 * part + width(part)],
                                            turn_bank[part % 2][0:E, 0:width(part)]).then_inc(wgt_copied, 1)
                        for part, tiles in enumerate(GROUPS):
                            dve.wait_ge(bias_ready, part + 1)
                            a, z = tiles[0], tiles[-1] + 1
                            dve.tensor_tensor(acc[:, a:z, :], turn_bank[part % 2][:, 0:width(part)].rearrange(
                                "p (t d) -> p t d", d=D), acc[:, a:z, :], ALU.add).then_inc(bias_added, 1)
                        dve.wait_ge(bias_added, len(GROUPS))
                    if u in (1, 5, 9, 13):
                        if u > 1:
                            add_outputs(e, u // 4 - 1)
                        elif not is_first(e):
                            add_outputs(nxt(e, -1), len(GROUPS) - 1)

            run_experts(dve, body)
            add_outputs((0, E - 1), len(GROUPS) - 1)


ROUTE_STEPS = 32


_INS = ["x", "ctx_1024", "L0_xattn_ln_m_g", "L0_xattn_ln_m_b", "L0_xattn_ln_l_g", "L0_xattn_ln_l_b",
        "L0_xattn_Wq", "L0_xattn_Wkv", "L0_xattn_Wout", "L0_ffn_gate_w", "L0_ffn_w1", "L0_ffn_b1",
        "L0_ffn_w2", "L0_ffn_b2"]


def kernel(**inputs):
    import numpy as _np
    import concourse.bacc as _bacc
    from concourse import mybir as _mybir
    from concourse.bass_utils import run_bass_kernel_spmd as _run

    nc = _bacc.Bacc("TRN2", target_bir_lowering=False, num_devices=1)
    arrays, args = {}, []
    for name in _INS:
        a = _np.ascontiguousarray(inputs[name])
        arrays[f"in_{name}"] = a
        args.append(nc.dram_tensor(f"in_{name}", a.shape, _mybir.dt.from_np(a.dtype), kind="ExternalInput").ap())
    shape = tuple(inputs["x"].shape)
    args.append(nc.dram_tensor("out_0", shape, _mybir.dt.float32, kind="ExternalOutput").ap())
    attention_and_experts(nc, *args)
    r = _run(nc, [arrays], core_ids=[0])
    return r.results[0]["out_0"]
```

```python
from contextlib import ExitStack

import concourse.bass as bass
from concourse import mybir

ALU = mybir.AluOpType
ACT = mybir.ActivationFunctionType
AX = mybir.AxisListType
F32 = mybir.dt.float32
F16 = mybir.dt.float16


CONST = 1024.0
ZS = 16.0
PSHIFT = 5.545177444479562
EPS = 1e-5
LEAD, NSLOT, UNROLL = 4, 14, 4


def attention_and_experts(nc, x, ctx_rows, ln_m_g, ln_m_b, ln_l_g, ln_l_b, Wq, Wkv, Wout,
                          gate_w, w1, b1, w2, b2, out):
    NB, S, D = x.shape
    M = ctx_rows.shape[1]
    INNER = Wq.shape[1]
    DH = 64
    H = INNER // DH
    HH = H // 2
    HC = HH * S
    QC = H * S
    TP = 125
    CT = M // TP
    NT = CT + 1
    QT = QC // 128
    TOK = NB * S
    E, Dff = b1.shape
    assert D == 128 and M == CT * TP and CT == 12 and QC == 7 * 128 and DH == 64 and Dff == 512

    with ExitStack() as top:
        def sem(name):
            return top.enter_context(nc.semaphore(name))

        psum = [top.enter_context(nc.psum_tensor(f"bank_pair{i}", [128, 2, 512], F32)) for i in range(2)]
        out_bank = top.enter_context(nc.psum_tensor("out_bank", [128, 512], F32))
        max_bank = [top.enter_context(nc.psum_tensor(f"max_bank{i}", [128, 512], F32)) for i in range(2)]
        misc = top.enter_context(nc.psum_tensor("misc", [128, 512], F32))
        misc16 = misc[:, :].bitcast(F16)

        def sbuf(stack, name, shape, dt=F32):
            return stack.enter_context(nc.sbuf_tensor(name, shape, dt))

        ident = sbuf(top, "ident", [128, 128])
        ident16 = sbuf(top, "ident16", [128, 128], F16)
        yT = sbuf(top, "yT", [128, TOK])
        attention(nc, sem, sbuf, locals())
        experts(nc, sem, sbuf, locals())


def attention(nc, sem, sbuf, v):
    (x, ctx_rows, Wq, Wkv, Wout) = (v[n] for n in ("x", "ctx_rows", "Wq", "Wkv", "Wout"))
    gains = [v[n] for n in ("ln_m_g", "ln_m_b", "ln_l_g", "ln_l_b")]
    NB, S, D, H, HH, HC, QC, TP, CT, NT, QT = (v[n] for n in (
        "NB", "S", "D", "H", "HH", "HC", "QC", "TP", "CT", "NT", "QT"))
    score_banks, out_bank, max_bank, misc, misc16 = (v[n] for n in ("psum", "out_bank", "max_bank", "misc", "misc16"))
    ident, ident16, yT = v["ident"], v["ident16"], v["yT"]

    with ExitStack() as ctx:
        def sb(name, shape, dt=F32):
            return sbuf(ctx, name, shape, dt)

        raw = [sb(f"raw{i}", [128, NT, D]) for i in range(4)]
        stats = [sb(f"stats{i}", [128, NT, 6]) for i in range(2)]
        sm = sb("sm", [128, 8, NT])
        half_pow = sb("half_pow", [128, NT])
        keys = [sb(f"keys{i}", [128, 2, NT, D], F16) for i in range(4)]
        keysT = [sb(f"keysT{i}", [128, 2, NT, 128], F16) for i in range(4)]
        Q = [sb(f"Q{i}", [128, 2, 2, QC], F16) for i in range(4)]
        A = sb("A", [128, 2, 2, H, 128], F16)
        B = sb("B", [128, 2, 2, H, 128], F16)
        prob = [sb(f"prob{i}", [128, 2 * HC]) for i in range(2)]
        probs = [sb(f"probs{i}", [128, 2, 2 * HC], F16) for i in range(4)]
        part_max = [sb(f"part_max{i}", [128, QT, 4]) for i in range(2)]
        neg_max = sb("neg_max", [128, 2, QT])
        neg_max16 = sb("neg_max16", [128, 2, QT], F16)
        shift_rows = sb("shift_rows", [2 * QT, 128], F16)
        O = [sb(f"O{i}", [128, 2, HC]) for i in range(2)]
        den = [sb(f"den{i}", [1, HC]) for i in range(2)]
        den64 = [sb(f"den64_{i}", [64, HC // 64]) for i in range(2)]
        recip64 = [sb(f"recip64_{i}", [64, HC // 64]) for i in range(2)]
        recip_dram = nc.dram_tensor("recip_dram", (2, HC), F32, kind="Internal").ap()
        recip_all = [sb(f"recip_all{i}", [128, HC]) for i in range(2)]
        On = sb("On", [128, 2, HC])
        Os = sb("Os", [128, 2, 2, 2, QC], F16)
        vecs = sb("vecs", [128, 4])
        vecs64 = sb("vecs64", [128, 2])
        row1 = sb("row1", [1, 128])

        wq_sb = keysT[0][:, :, :, :].rearrange("p a t c -> p (a t c)").bitcast(F32)[:, 0:1024]
        wkv_sb = keysT[1][:, :, :, :].rearrange("p a t c -> p (a t c)").bitcast(F32)[:, 0:1024]
        wv_sb = keysT[2][:, :, :, :].rearrange("p a t c -> p (a t c)").bitcast(F32)[:, 0:1024]
        wout_sb = keysT[3][:, :, :, :].rearrange("p a t c -> p (a t c)").bitcast(F32)[:, 0:1024]
        fold = [Q[j][:, :, :, :].rearrange("p a t c -> p (a t c)").bitcast(F32)[:, 0:1024] for j in range(4)]
        fold.append(Os[:, :, :, :, :].rearrange("p a t b c -> p (a t b c)").bitcast(F32)[:, 0:1024])
        lat_split = [sb(f"lat_split{i}", [128, D], F16) for i in range(4)]
        shift_pair = [sb(f"shift_pair{i}", [2, QC], F16) for i in range(2)]
        const_pair = sb("const_pair", [2, 128], F16)
        emb = sb("emb", [128, 4, 128])

        weights_in = sem("weights_in")
        passed = sem("passed")
        ident_ready = sem("ident_ready")
        filled = sem("filled")
        zeroed = sem("zeroed")
        emb_ready = sem("emb_ready")
        setup_product = sem("setup_product")
        setup_high = sem("setup_high")
        setup_low = sem("setup_low")
        raw_in = [sem(f"raw_in{i}") for i in range(4)]
        stats_ready = sem("stats_ready")
        small_step = sem("small_step")
        xn_ready = sem("xn_ready")
        high_ready = sem("high_ready")
        keys_ready = sem("keys_ready")
        transposed = sem("transposed")
        q_product = sem("q_product")
        q_high = sem("q_high")
        max_product = sem("max_product")
        max_reduced = sem("max_reduced")
        shift_step = sem("shift_step")
        shift_turned = sem("shift_turned")
        shift_in = sem("shift_in")
        score_ready = sem("score_ready")
        exp_done = sem("exp_done")
        p_high = sem("p_high")
        p_low_v = sem("p_low_v")
        p_low_g = sem("p_low_g")
        pv_done = sem("pv_done")
        misc_free = sem("misc_free")
        out_copied = sem("out_copied")
        den_ready = sem("den_ready")
        den_spread = [sem(f"den_spread{i}") for i in range(2)]
        recip_ready = sem("recip_ready")
        recip_out = [sem(f"recip_out{i}") for i in range(2)]
        recip_spread = [sem(f"recip_spread{i}") for i in range(2)]
        on_ready = sem("on_ready")
        os_high = sem("os_high")
        os_ready = sem("os_ready")
        y_product = sem("y_product")

        def count(b, per, extra):
            k, c = b
            return k * (UNROLL * per) + (c * per + extra)

        def wait(eng, s, b, per, extra):
            k, c = b
            if isinstance(k, int) and count(b, per, extra) <= 0:
                return
            eng.wait_ge(s, count(b, per, extra))
            if eng.engine in (nc.gpsimd.engine, nc.sync.engine):
                eng.sem_inc(passed, 1)

        def wait_pair(eng, s, b, extra):
            k, c = b
            if not isinstance(k, int) or c // 2 + extra > 0:
                eng.wait_ge(s, k * (UNROLL // 2) + (c // 2 + extra))

        def later(b, d):
            return (b[0], b[1] + d)

        def num(b):
            return b[0] * UNROLL + b[1]

        first, last = -4, NB

        MISC = [(0, "keysT", 2, 3), (1, "lat", -1, 1), (2, "q", 2, 0), (3, "q", 2, 1), (4, "q", 2, 2),
                (5, "q", 2, 3), (6, "keysT", 2, 0), (7, "y", -1, 0), (8, "lat", 0, 0), (9, "keysT", 2, 1),
                (10, "keysT", 2, 2), (11, "shift", 1, 0)]

        def misc_uses(i):
            return [u for u in MISC if 0 <= i + u[2] < NB and (u[1] != "y" or i % 2 == 0)]

        PIECES = [range(CT, NT)] + [range(t, t + 2) for t in range(0, CT, 2)]
        SCALE_SLOTS = (4, 5, 6, 7, 8, 9, 10)
        SMALL_STEPS = (0, 9, 10, 14, 16)
        FILLED = 8

        USES_PER_LOOP = sum(len(misc_uses(i)) for i in range(1, 1 + UNROLL))

        def misc_turn(eng, b, slot):
            k, c = b
            n = sum(len(misc_uses(i)) for i in range(first, c)) + len([u for u in misc_uses(c) if u[0] < slot])
            if not isinstance(k, int) or n > 0:
                eng.wait_ge(misc_free, k * USES_PER_LOOP + n)

        def steps(eng, run):
            for i in range(first, 1):
                run((0, i), i)
            with eng.Fori(0, (NB - 8) // UNROLL) as k:
                for c in range(1, UNROLL + 1):
                    run((k, c), None)
            for i in range(NB - 7, last + 1):
                run((0, i), i)

        def live(i, d):
            return i is None or 0 <= i + d < NB

        W_OF = (wq_sb, wkv_sb, wkv_sb, wv_sb, wv_sb)
        EMB_OF = (0, 1, 2, 3, 0)
        FOLDS = 2 * 5
        SETUP = [("fold", n, q) for n in range(5) for q in range(2)] + \
                [(m, var, q) for m in "AB" for var in range(2) for q in range(H // 4)]
        A_SCALE = 64 ** -0.5

        EARLY = FOLDS + H // 2
        B_STEP = -2
        B_SLOTS = tuple(range(2, 2 + len(SETUP) - EARLY))

        def setup_in(i, k):
            return [EARLY + B_SLOTS.index(k)] if i == B_STEP and k in B_SLOTS else []

        def setup_product_group(pe, g):
            what, n, q = SETUP[g]
            bank = max_bank[g % 2]
            if g >= 2:
                pe.wait_ge(setup_low, g - 1)
            if g == FOLDS:
                pe.wait_ge(setup_low, FOLDS)
            for j in range(4):
                o = bank[:, 128 * j:128 * j + 128]
                if what == "fold":
                    t = 4 * q + j
                    mm = nc.tensor.matmul(o, W_OF[n][:, 128 * t:128 * t + 128], emb[:, EMB_OF[n], :],
                                          start=True, stop=True)
                    continue
                h = 8 * (q // 2) + q % 2 + 2 * j
                rows, cols = slice(64 * (h % 2), 64 * (h % 2) + 64), slice(128 * (h // 2), 128 * (h // 2) + 128)
                l, r = (fold[0], fold[1 + n]) if what == "A" else (fold[3 + n], wout_sb)
                mm = nc.tensor.matmul(o, l[rows, cols], r[rows, cols], start=True, stop=True)
            mm.then_inc(setup_product, 1)

        def setup_split(what, n, q):
            first_head = 8 * (q // 2) + q % 2
            dst = (A if what == "A" else B)[:, n, :, first_head:first_head + 7:2, :]
            return dst, A_SCALE if what == "A" else 1.0

        block = ctx.enter_context(nc.Block())

        @block.sync
        def _(sp):
            def load_context(b):
                sp.dma_start(raw[b[1] % 4][0:TP, 0:CT, :],
                             ctx_rows[num(b)].rearrange("(p t) d -> p t d", t=CT)).then_inc(raw_in[b[1] % 4], 16)

            def load_latents(b):
                p = b[1] % 4
                sp.dma_start(raw[p][0:S, CT, :], x[num(b)]).then_inc(raw_in[p], 16)
                sp.dma_start(raw[p][64:64 + S, CT, :], x[num(b)]).then_inc(raw_in[p], 16)

            load_context((0, 0))
            sp.wait_ge(filled, 4)
            load_latents((0, 0))
            for n, g in enumerate(gains):
                sp.dma_start(vecs[:, n:n + 1], g.rearrange("(p a) -> p a", a=1)).then_inc(weights_in, 16)
            sp.dma_start(wq_sb, Wq).then_inc(weights_in, 16)
            sp.dma_start(wkv_sb, Wkv[:, 0:H * 64]).then_inc(weights_in, 16)
            sp.dma_start(wv_sb, Wkv[:, H * 64:2 * H * 64]).then_inc(weights_in, 16)
            sp.dma_start(wout_sb.rearrange("p (t n) -> p t n", n=D),
                         Wout.rearrange("(t p) n -> p t n", p=128)).then_inc(weights_in, 16)
            def load(b):
                load_context(b)
                load_latents(b)

            for n in range(1, 3):
                load((0, n))

            def spread(b, half):
                wait(sp, den_ready, b, 2, half + 1)
                sp.dma_start(den64[half][:, :], den[half][0:1, :].rearrange("o (p c) -> o p c", p=64))\
                  .then_inc(den_spread[half], 16)
                wait(sp, recip_ready, b, 2, half + 1)
                sp.dma_start(recip_dram[half].rearrange("(p c) -> p c", p=64), recip64[half][:, :])\
                  .then_inc(recip_out[half], 16)
                wait(sp, recip_out[half], b, 16, 16)
                wait(sp, on_ready, later(b, -1), 2, half + 1)
                sp.dma_start(recip_all[half][:, :], recip_dram[half:half + 1, :].to_broadcast([128, HC]))\
                  .then_inc(recip_spread[half], 16)

            def step(b, i):
                if live(i, -1):
                    spread(later(b, -1), 1)
                if live(i, 0):
                    spread(b, 0)
                if live(i, 7):
                    wait(sp, keys_ready, later(b, 3), 7, 7)
                    load(later(b, 7))

            steps(sp, step)

        @block.gpsimd
        def _(pool):
            pool.memset(ident[:, :], 0.0).then_inc(ident_ready, 1)
            pool.wait_ge(ident_ready, 1)
            pool.affine_select(out=ident[:, :], in_=ident[:, :], compare_op=ALU.not_equal, fill=1.0,
                               base=0, pattern=[[-1, 128]], channel_multiplier=1).then_inc(ident_ready, 1)
            pool.wait_ge(ident_ready, 2)
            pool.tensor_copy(ident16[:, :], ident[:, :]).then_inc(ident_ready, 1)
            for t in raw:
                pool.memset(t[:, CT, :], 0.0).then_inc(filled, 1)
            pool.memset(half_pow[:, :], -0.5).then_inc(filled, 1)
            pool.memset(keys[0][:, :, :, :], 0.0).then_inc(filled, 1)
            pool.wait_ge(filled, 6)
            pool.memset(keys[0][0:TP, 0, 0:CT, 0:1], CONST).then_inc(filled, 1)
            pool.memset(keys[0][0:S, 0, CT, 0:1], CONST).then_inc(filled, 1)
            pool.wait_ge(filled, FILLED)

            def small(b, part):
                n = SMALL_STEPS[part]

                def did(*ins):
                    nonlocal n
                    for i in ins:
                        i.then_inc(small_step, 1)
                    n += len(ins)
                    wait(pool, small_step, b, SMALL_STEPS[-1], n)

                st = stats[b[1] % 2][0:TP]
                w = [sm[0:TP, j, :] for j in range(8)]
                l2, l4, l5 = (w[j][:, CT:NT] for j in (2, 4, 5))
                if part == 0:
                    wait(pool, stats_ready, b, 1, 1)
                    wait(pool, xn_ready, b, 7, 0)
                    did(pool.tensor_tensor(w[0], st[:, :, 1], st[:, :, 4], ALU.add),
                        pool.tensor_tensor(w[1], st[:, :, 1], st[:, :, 4], ALU.subtract),
                        pool.tensor_tensor(w[2], st[:, :, 2], st[:, :, 5], ALU.add))
                    did(pool.tensor_tensor(w[1], w[1], w[1], ALU.mult),
                        pool.tensor_scalar(w[2], w[2], 1.0 / D, 0.0, ALU.mult, ALU.add),
                        pool.tensor_scalar(w[7], w[0], -0.5, 0.0, ALU.mult, ALU.add))
                    did(pool.tensor_scalar(w[1], w[1], 0.25, 0.0, ALU.mult, ALU.add))
                    did(pool.tensor_tensor(w[2], w[2], w[1], ALU.add))
                    did(pool.tensor_scalar(w[3], w[2], 1.0 / ZS ** 2, EPS / ZS ** 2, ALU.mult, ALU.add))
                if part == 1:
                    did(pool.tensor_tensor(w[6], w[3], half_pow[0:TP, :], ALU.pow))
                l6 = w[6][:, CT:NT]
                if part == 2:
                    did(pool.tensor_tensor(l4, l6, l6, ALU.mult))
                    did(pool.tensor_tensor(l4, l4, l2, ALU.mult))
                    did(pool.tensor_scalar(l4, l4, 1.0 / ZS ** 2, EPS, ALU.mult, ALU.add))
                    did(pool.tensor_tensor(l5, l4, half_pow[0:TP, 0:1], ALU.pow))
                if part == 3:
                    did(pool.tensor_tensor(l6, l6, l5, ALU.mult))
                    did(pool.tensor_tensor(w[7], w[6], w[7], ALU.mult))

            def scale_tiles(b, n):
                for t in PIECES[n]:
                    rows = raw[b[1] % 4][0:TP, t, 1:D]
                    ins = pool.tensor_scalar(rows, rows,
                                             sm[0:TP, 6, t:t + 1], sm[0:TP, 7, t:t + 1], ALU.mult, ALU.add)
                ins.then_inc(xn_ready, 1)

            def tiles_low(b, n):
                kb = keys[b[1] % 4]
                a, e = PIECES[n][0], PIECES[n][-1] + 1
                wait(pool, high_ready, b, 7, n + 1)
                pool.tensor_tensor(kb[0:TP, 1, a:e, 1:D], raw[b[1] % 4][0:TP, a:e, 1:D], kb[0:TP, 0, a:e, 1:D],
                                   ALU.subtract).then_inc(keys_ready, 1)

            def step(b, i):
                for k in range(NSLOT):
                    if live(i, 0) and k % 7 != 6:
                        u = count(b, NSLOT, k)
                        wait(pool, p_high, b, NSLOT, k + 1)
                        pb = probs[(2 * b[1] + k) % 4]
                        pool.tensor_tensor(pb[:, 1, HC:], prob[k % 2][:, HC:], pb[:, 0, HC:],
                                           ALU.subtract).then_inc(p_low_g, 1)
                    if live(i, 3):
                        if k < 4:
                            small(later(b, 3), k)
                        if k in SCALE_SLOTS:
                            scale_tiles(later(b, 3), SCALE_SLOTS.index(k))
                        if k - 2 in SCALE_SLOTS:
                            tiles_low(later(b, 3), SCALE_SLOTS.index(k - 2))

            steps(pool, step)

        @block.tensor
        def _(pe):
            PASSES = ((0, 0), (0, 1), (1, 0))
            pe.wait_ge(ident_ready, 3)
            pe.wait_ge(weights_in, 16 * 8)
            pe.wait_ge(emb_ready, 16)
            for g in range(EARLY):
                setup_product_group(pe, g)
            pe.wait_ge(setup_low, EARLY)

            def scores(b, k):
                qb, kb = Q[b[1] % 4], keysT[b[1] % 4]
                half, p = divmod(k, 7)
                wait(pe, exp_done, b, NSLOT, k - 1)
                if k == 0:
                    wait(pe, shift_in, b, 32, 32)
                cols = slice(half * HC, half * HC + HC)
                for j, t in enumerate(range(2 * p, min(2 * p + 2, NT))):
                    var = int(t == CT)
                    o = score_banks[k % 2][:, j, 0:HC]
                    for n, (ks, qs) in enumerate(PASSES):
                        mm = nc.tensor.matmul(o, kb[:, ks, t, :], qb[:, var, qs, cols],
                                              start=(n == 0), stop=(n == 2 and not var))
                    if var:
                        mm = nc.tensor.matmul(o, const_pair[:, :], shift_pair[b[1] % 2][:, cols],
                                              start=False, stop=True)
                mm.then_inc(score_ready, 1)

            def values(b, k):
                half, p = divmod(k, 7)
                kb, pb = keys[b[1] % 4], probs[(2 * b[1] + k) % 4]
                wait(pe, p_low_v, b, NSLOT, k + 1)
                wait(pe, p_low_g, b, 12, (k + 1) - (k + 1) // 7)
                if p == 0:
                    wait(pe, out_copied, b, 2, half)
                if p == 6:
                    misc_turn(pe, later(b, half), 1 if half else 8)
                for j, t in enumerate(range(2 * p, min(2 * p + 2, NT))):
                    if t == CT:
                        nc.tensor.matmul(misc[:, 0:HC], lat_split[b[1] % 4][:, :], pb[:, 0, 0:HC],
                                         start=True, stop=False)
                        mm = nc.tensor.matmul(misc[:, 0:HC], kb[0:64, 0, CT, :], pb[0:64, 1, 0:HC],
                                              start=False, stop=True)
                        continue
                    for n, (ks, ps) in enumerate(PASSES):
                        mm = nc.tensor.matmul(out_bank[:, 0:HC], kb[:, ks, t, :], pb[:, ps, j * HC:j * HC + HC],
                                              start=(n == 0 and t == 0), stop=(n == 2 and t == CT - 1))
                mm.then_inc(pv_done, 1)

            def maxima(b, t, j):
                qb, kb = Q[b[1] % 4], keysT[b[1] % 4]
                if t == 0 and j == 0 and isinstance(b[0], int) and b[1] == 0:
                    pe.wait_ge(setup_low, len(SETUP))
                if t == 0 and j == 0:
                    misc_turn(pe, later(b, -2), 11)
                wait(pe, max_reduced, b, 4 * QT, 4 * t + j - 1)
                if j < 3:
                    o, rhs = max_bank[j % 2][:, 0:4 * TP], kb[:, 0, 4 * j:4 * j + 4, 0:TP]
                else:
                    o, rhs = max_bank[1][:, 0:S], kb[:, 0, CT, 0:S]
                nc.tensor.matmul(o, qb[:, int(j == 3), 0, 128 * t:128 * t + 128], rhs,
                                 start=True, stop=True).then_inc(max_product, 1)

            def turn_keys(b, j):
                kb = keys[b[1] % 4]
                wait(pe, keys_ready, b, 7, 1 if j == 3 else 7)
                tiles = range(4 * j, min(4 * j + 4, NT))
                o = misc16.rearrange("p (a t c) -> p a t c", a=2, t=4)
                for a in range(2):
                    for t in tiles:
                        mm = nc.tensor.transpose(o[:, a, t - 4 * j, :], kb[:, a, t, :], ident16[:, :])
                mm.then_inc(transposed, 1)

            def queries(b, w):
                var, half = divmod(w, 2)
                kb = keysT[b[1] % 4]
                for h in range(HH):
                    for n, (a, z) in enumerate(PASSES):
                        mm = nc.tensor.matmul(misc[:, h * S:h * S + S], A[:, var, a, half * HH + h, :],
                                              kb[:, z, CT, 0:S], start=(n == 0), stop=(n == 2))
                mm.then_inc(q_product, 1)

            def shift(b):
                wait(pe, shift_step, b, 4, 4)
                nc.tensor.transpose(misc16[0:2 * QT, 0:128], neg_max16[:, :, :].rearrange("p a t -> p (a t)"),
                                    ident16[:, :]).then_inc(shift_turned, 1)

            def project(b):
                wait(pe, os_ready, b, 2, 2)
                n = 0
                for var in range(2):
                    for h in range(H):
                        for w, o in PASSES:
                            mm = nc.tensor.matmul(misc[:, 0:2 * S], B[:, var, w, h, :],
                                                  Os[:, o, var, :, h * S:h * S + S],
                                                  start=(n == 0), stop=(n == 6 * H - 1))
                            n += 1
                mm.then_inc(y_product, 1)

            def misc_use(b, i, k):
                for slot, what, d, part in MISC:
                    if slot != k or not live(i, d) or what == "lat" or (what == "y" and b[1] % 2):
                        continue
                    misc_turn(pe, b, slot)
                    g = later(b, d)
                    if what == "keysT":
                        turn_keys(g, part)
                    if what == "q":
                        queries(g, part)
                    if what == "y":
                        project(g)
                    if what == "shift":
                        shift(g)

            def chunks(b, i, k, which):
                m = k + 3
                d, m = (1, m) if m < NSLOT else (2, m - NSLOT)
                if live(i, d):
                    maxima(later(b, d), m // 2, 2 * (m % 2) + which)

            def step(b, i):
                for k in range(NSLOT):
                    if live(i, 0):
                        scores(b, k)
                    chunks(b, i, k, 0)
                    if k >= 2 and live(i, 0):
                        values(b, k - 2)
                    if k < 2 and live(i, -1):
                        values(later(b, -1), k + 12)
                    chunks(b, i, k, 1)
                    misc_use(b, i, k)
                    for g in setup_in(i, k):
                        setup_product_group(pe, g)

            steps(pe, step)

        @block.scalar
        def _(act):
            def setup_high_half(g):
                dst, scale = setup_split(*SETUP[g])
                act.wait_ge(setup_product, g + 1)
                act.activation(dst[:, 0], max_bank[g % 2][:, :].rearrange("p (h c) -> p h c", h=4), ACT.Copy,
                               scale=scale).then_inc(setup_high, 1)

            for g in range(FOLDS, EARLY):
                setup_high_half(g)

            def soften(b, k):
                w = HC if k % 7 == 6 else 2 * HC
                wait(act, score_ready, b, NSLOT, k + 1)
                wait(act, p_low_v, b, NSLOT, k - 1)
                wait(act, p_low_g, b, 12, (k - 1) - (k - 1) // 7)
                act.activation(prob[k % 2][:, 0:w].rearrange("p (j c) -> p j c", c=HC),
                               score_banks[k % 2][:, 0:w // HC, 0:HC], ACT.Exp,
                               scale=1.0 / CONST).then_inc(exp_done, 1)
                wait(act, exp_done, b, NSLOT, k + 1)
                wait(act, pv_done, b, NSLOT, k - 3)
                act.activation(probs[(2 * b[1] + k) % 4][:, 0, 0:w], prob[k % 2][:, 0:w],
                               ACT.Copy).then_inc(p_high, 1)

            def misc_copy(b, i, k):
                for slot, what, d, part in MISC:
                    if slot != k or not live(i, d) or (what == "y" and b[1] % 2):
                        continue
                    g = later(b, d)
                    qb = Q[g[1] % 4]
                    if what == "keysT":
                        wait(act, transposed, g, 4, (part + 1) % 4 + 1)
                        tiles = slice(4 * part, min(4 * part + 4, NT))
                        src = misc16.rearrange("p (a t c) -> p a t c", a=2, t=4)
                        act.activation(keysT[g[1] % 4][:, :, tiles, :], src[:, :, 0:tiles.stop - tiles.start, :],
                                       ACT.Copy).then_inc(misc_free, 1)
                    if what == "q":
                        var, half = divmod(part, 2)
                        wait(act, q_product, g, 4, part + 1)
                        act.activation(qb[:, var, 0, half * HC:half * HC + HC], misc[:, 0:HC], ACT.Copy,
                                       scale=1.0 / CONST).then_inc(q_high, 1)
                    if what == "y":
                        wait_pair(act, y_product, g, 1)
                        act.activation(yT[:, bass.ds(num(later(g, -1)) * S, 2 * S)], misc[:, 0:2 * S], ACT.Copy,
                                       scale=1.0 / CONST).then_inc(misc_free, 1)
                    if what == "shift":
                        wait(act, shift_turned, g, 1, 1)
                        wait(act, shift_in, later(g, -1), 32, 32)
                        act.activation(shift_rows[:, :], misc16[0:2 * QT, 0:128], ACT.Copy).then_inc(misc_free, 1)
                        misc_turn(act, b, 12)
                        act.dma_start(qb[0:1, 0, :, :].rearrange("o a (t c) -> o (a t) c", c=128),
                                      shift_rows[:, :]).then_inc(shift_in, 16)
                        act.dma_start(shift_pair[g[1] % 2][:, :].rearrange("a (t c) -> a t c", c=128),
                                      shift_rows[:, :]).then_inc(shift_in, 16)

            def step(b, i):
                for k in range(NSLOT):
                    if live(i, 0):
                        soften(b, k)
                    misc_copy(b, i, k)
                    for g in setup_in(i, k):
                        setup_high_half(g)

            steps(act, step)

        @block.vector
        def _(dve):
            def setup_low_half(g):
                what, n, q = SETUP[g]
                bank = max_bank[g % 2][:, :]
                if what == "fold":
                    dve.wait_ge(setup_product, g + 1)
                    dve.tensor_copy(fold[n][:, 512 * q:512 * q + 512], bank).then_inc(setup_low, 1)
                else:
                    dst, scale = setup_split(what, n, q)
                    dve.wait_ge(setup_high, g + 1 - FOLDS)
                    dve.scalar_tensor_tensor(out=dst[:, 1], in0=bank.rearrange("p (h c) -> p h c", h=4),
                                             scalar=scale, in1=dst[:, 0], op0=ALU.mult,
                                             op1=ALU.subtract).then_inc(setup_low, 1)

            def reduce_max(b, t, j):
                wait(dve, max_product, b, 4 * QT, 4 * t + j + 1)
                if t == 0 and j == 0:
                    wait(dve, shift_step, later(b, -2), 4, 1)
                w = 4 * TP if j < 3 else S
                dve.reduce_max(part_max[b[1] % 2][:, t, j:j + 1], max_bank[j % 2][:, 0:w], AX.X)\
                   .then_inc(max_reduced, 1)

            def make_shift(b):
                wait(dve, max_reduced, b, 4 * QT, 4 * QT)
                wait(dve, shift_turned, later(b, -1), 1, 1)
                dve.tensor_reduce(neg_max[:, 0, :], part_max[b[1] % 2][:, :, :], AX.X, ALU.max,
                                  negate=True).then_inc(shift_step, 1)
                wait(dve, shift_step, b, 4, 1)
                dve.tensor_scalar(neg_max[:, 1, :], neg_max[:, 0, :], 1.0 / CONST, PSHIFT, ALU.mult, ALU.add)\
                   .then_inc(shift_step, 1)
                wait(dve, shift_step, b, 4, 2)
                dve.tensor_copy(neg_max16[:, 0, :], neg_max[:, 1, :]).then_inc(shift_step, 1)
                wait(dve, shift_step, b, 4, 3)
                dve.tensor_tensor(neg_max16[:, 1, :], neg_max[:, 1, :], neg_max16[:, 0, :],
                                  ALU.subtract).then_inc(shift_step, 1)

            def low(b, k):
                pb = probs[(2 * b[1] + k) % 4]
                wait(dve, p_high, b, NSLOT, k + 1)
                dve.tensor_tensor(pb[:, 1, 0:HC], prob[k % 2][:, 0:HC], pb[:, 0, 0:HC],
                                  ALU.subtract).then_inc(p_low_v, 1)

            def query_low(b, w):
                var, half = divmod(w, 2)
                cols = slice(half * HC, half * HC + HC)
                qb = Q[b[1] % 4]
                wait(dve, q_high, b, 4, w + 1)
                dve.scalar_tensor_tensor(out=qb[:, var, 1, cols], in0=misc[:, 0:HC], scalar=1.0 / CONST,
                                         in1=qb[:, var, 0, cols], op0=ALU.mult,
                                         op1=ALU.subtract).then_inc(misc_free, 1)

            def statistics(b, t):
                if t == 0:
                    wait(dve, raw_in[b[1] % 4], (b[0], b[1] // 4 * 4), 12, 48)
                    wait(dve, small_step, later(b, -2), SMALL_STEPS[-1], SMALL_STEPS[-1])
                ins = dve.bn_stats(stats[b[1] % 2][0:TP, t, :], raw[b[1] % 4][0:TP, t, :])
                if t == NT - 1:
                    ins.then_inc(stats_ready, 1)

            def tiles_high(b, n):
                wait(dve, xn_ready, b, 7, n + 1)
                if n == 0:
                    wait(dve, pv_done, later(b, -4), NSLOT, NSLOT)
                if n == 1:
                    ls, kl, rl = lat_split[b[1] % 4], keys[b[1] % 4], raw[b[1] % 4]
                    wait(dve, high_ready, b, 7, 1)
                    dve.tensor_copy(ls[0:S, 1:D], kl[0:S, 0, CT, 1:D])
                    dve.tensor_tensor(ls[64:64 + S, 1:D], rl[64:64 + S, CT, 1:D], kl[64:64 + S, 0, CT, 1:D],
                                      ALU.subtract)
                a, e = PIECES[n][0], PIECES[n][-1] + 1
                dve.tensor_copy(keys[b[1] % 4][0:TP, 0, a:e, 1:D], raw[b[1] % 4][0:TP, a:e, 1:D])\
                   .then_inc(high_ready, 1)

            def out_copy(b, half):
                wait(dve, pv_done, b, NSLOT, 7 * half + 6)
                wait(dve, on_ready, later(b, -1), 2, half + 1)
                dve.tensor_copy(O[half][:, 0, :], out_bank[:, 0:HC]).then_inc(out_copied, 1)

            def latent_copy(b, half):
                wait(dve, pv_done, b, NSLOT, 7 * half + 7)
                dve.tensor_copy(O[half][:, 1, :], misc[:, 0:HC]).then_inc(misc_free, 1)

            def denominator(b, half):
                misc_turn(dve, later(b, half), 2 if half else 9)
                wait(dve, out_copied, b, 2, half + 1)
                dve.tensor_tensor(den[half][:, :], O[half][0:1, 0, :], O[half][0:1, 1, :], ALU.add)\
                   .then_inc(den_ready, 1)

            def reciprocals(b, half):
                wait(dve, den_spread[half], b, 16, 16)
                dve.reciprocal(recip64[half][:, :], den64[half][:, :]).then_inc(recip_ready, 1)

            def normalise(b, half):
                wait(dve, recip_spread[half], b, 16, 16)
                wait(dve, os_ready, b, 2, half)
                rb = recip_all[half][:, :].unsqueeze(1).to_broadcast([128, 2, HC])
                dve.scalar_tensor_tensor(out=On[:, :, :], in0=O[half][:, :, :], scalar=CONST, in1=rb,
                                         op0=ALU.mult, op1=ALU.mult).then_inc(on_ready, 1)
                wait(dve, on_ready, b, 2, half + 1)
                if half == 0:
                    wait_pair(dve, y_product, b, 0)
                cols = slice(half * HC, half * HC + HC)
                dve.tensor_copy(Os[:, 0, :, b[1] % 2, cols], On[:, :, :]).then_inc(os_high, 1)

            def normal_low(b, half):
                wait(dve, os_high, b, 2, half + 1)
                cols = slice(half * HC, half * HC + HC)
                dve.tensor_tensor(Os[:, 1, :, b[1] % 2, cols], On[:, :, :], Os[:, 0, :, b[1] % 2, cols],
                                  ALU.subtract).then_inc(os_ready, 1)

            def step(b, i):
                for k in range(NSLOT):
                    if k == 2 and live(i, -1):
                        latent_copy(later(b, -1), 1)
                    if k == 9 and live(i, 0):
                        latent_copy(b, 0)
                    if k >= 1 and live(i, 0):
                        low(b, k - 1)
                    if k == 0 and live(i, -1):
                        low(later(b, -1), NSLOT - 1)
                    if k in (3, 4, 5, 6) and live(i, 2):
                        query_low(later(b, 2), k - 3)
                    if k == 1 and live(i, -1):
                        out_copy(later(b, -1), 1)
                    if k == 2 and live(i, -1):
                        denominator(later(b, -1), 1)
                    if k == 8 and live(i, 0):
                        out_copy(b, 0)
                    if k == 9 and live(i, 0):
                        denominator(b, 0)
                    m = k + 3
                    d, m = (1, m) if m < NSLOT else (2, m - NSLOT)
                    if live(i, d):
                        reduce_max(later(b, d), m // 2, 2 * (m % 2))
                    if k == 3 and live(i, -1):
                        reciprocals(later(b, -1), 1)
                    if k == 5 and live(i, -1):
                        normalise(later(b, -1), 1)
                    if k == 6 and live(i, -1):
                        normal_low(later(b, -1), 1)
                    if k == 10 and live(i, 0):
                        reciprocals(b, 0)
                    if k == 12 and live(i, 0):
                        normalise(b, 0)
                    if k == 13 and live(i, 0):
                        normal_low(b, 0)
                    if k - 1 in SCALE_SLOTS and live(i, 3) and i != -3:
                        tiles_high(later(b, 3), SCALE_SLOTS.index(k - 1))
                    if k < NT and live(i, 4) and (i is None or i > -2):
                        statistics(later(b, 4), k)
                    if live(i, d):
                        reduce_max(later(b, d), m // 2, 2 * (m % 2) + 1)
                    if k == 10 and live(i, 1):
                        make_shift(later(b, 1))
                    for g in setup_in(i, k - 1):
                        setup_low_half(g)

            dve.memset(row1[:, :], -CONST / ZS).then_inc(emb_ready, 1)
            dve.memset(const_pair[:, :], 0.0).then_inc(emb_ready, 1)
            dve.wait_ge(emb_ready, 2)
            for row in (0, 64):
                dve.memset(const_pair[:, row:row + S], CONST).then_inc(emb_ready, 1)
            for t in keys[1:]:
                dve.memset(t[:, :, :, :], 0.0).then_inc(zeroed, 1)
            for l in lat_split:
                dve.memset(l[:, :], 0.0).then_inc(zeroed, 1)
            dve.wait_ge(zeroed, 7)
            dve.wait_ge(filled, 6)
            for t, l in zip(keys, lat_split):
                if t is not keys[0]:
                    dve.memset(t[0:TP, 0, 0:CT, 0:1], CONST)
                    dve.memset(t[0:S, 0, CT, 0:1], CONST)
                dve.memset(t[64:64 + S, 0, CT, 0:1], CONST)
                dve.memset(l[0:S, 0:1], CONST)
            for t in range(NT):
                statistics((0, 0), t)
            dve.wait_ge(ident_ready, 3)
            dve.wait_ge(weights_in, 16 * 8)
            gm, bm, gl, bl = (vecs[:, n:n + 1] for n in range(4))
            EMB = (gl, gm, gl, gm)
            for e, gain in enumerate(EMB):
                dve.tensor_scalar(emb[:, e, :], ident[:, :], gain, CONST / ZS, ALU.mult, ALU.mult)\
                   .then_inc(emb_ready, 1)
            dve.wait_ge(emb_ready, 8)
            for e, gain in enumerate(EMB):
                dve.tensor_scalar(emb[0:1, e, 1:128], row1[0:1, 1:128], gain[0:1, :], 1.0, ALU.mult,
                                  ALU.mult).then_inc(emb_ready, 1)
            dve.tensor_copy(emb[:, 0, 0:1], bl).then_inc(emb_ready, 1)
            dve.memset(emb[:, 1, 0:1], 0.0).then_inc(emb_ready, 1)
            dve.tensor_tensor(emb[:, 2, 0:1], bl, bm, ALU.subtract).then_inc(emb_ready, 1)
            dve.tensor_copy(emb[:, 3, 0:1], bm).then_inc(emb_ready, 1)
            for g in range(EARLY):
                setup_low_half(g)
                if g < NT:
                    statistics((0, 1), g)
                if g - 8 in range(len(PIECES)):
                    tiles_high((0, 0), g - 8)
                if g - 14 in range(4):
                    for t in range(3 * (g - 14), min(3 * (g - 14) + 3, NT) if g < 17 else NT):
                        statistics((0, 2), t)
            steps(dve, step)


def experts(nc, sem, sbuf, v):
    NB, S, TOK, D, E, Dff = (v[n] for n in ("NB", "S", "TOK", "D", "E", "Dff"))
    x, out, gate_w, w1, b1, w2, b2 = (v[n] for n in ("x", "out", "gate_w", "w1", "b1", "w2", "b2"))
    yT, ident = v["yT"], v["ident"]
    h_banks, y_banks = v["psum"]
    turn_bank = [v["out_bank"], v["misc"]]
    weight_bank = v["max_bank"]
    T = TOK // 128
    FC = Dff // 128
    GROUPS = [range(g, min(g + 4, T)) for g in range(0, T, 4)]
    UNITS = len(GROUPS) * FC
    W1S, W2S, GS = 64.0, 256.0, 16.0
    x_rows = x.rearrange("b s d -> (b s) d").rearrange("(t p) d -> p t d", p=128)
    out_rows = out.rearrange("b s d -> (b s) d").rearrange("(t p) d -> p t d", p=128)

    with ExitStack() as ctx:
        def sb(name, shape, dt=F32):
            return sbuf(ctx, name, shape, dt)

        acc = sb("acc", [128, T, D])
        xm = sb("xm", [128, T, D])
        xmT = sb("xmT", [128, T * 128])
        xmTs = sb("xmTs", [128, 2, T * 128], F16)
        st = sb("st", [128, T, 6])
        mv = sb("mv", [128, T, 2])
        rstd = sb("rstd", [128, T])
        powers = sb("powers", [128, T])
        gate = sb("gate", [E, D])
        gateT = sb("gateT", [128, E])
        b1_rows = sb("b1_rows", [E * FC, 128])
        b1T = sb("b1T", [128, E * FC])
        b1_now = [sb(f"b1_now{i}", [128, FC]) for i in range(2)]
        b2_rows = sb("b2_rows", [E, D])
        logit = sb("logit", [128, T, E])
        p = sb("p", [128, T, E])
        above = sb("above", [128, T, E])
        rank = sb("rank", [128, T, E])
        col = sb("col", [128, 3, T])
        wgt = sb("wgt", [128, T, E])
        wgt_s = sb("wgt_s", [128, T, E])
        wgtT = sb("wgtT", [E, T * 128])
        w1n = [sb(f"w1n{i}", [128, FC, D]) for i in range(2)]
        w2n = [sb(f"w2n{i}", [128, FC, 128]) for i in range(2)]
        w1T = [sb(f"w1T{i}", [128, 2, Dff], F16) for i in range(2)]
        w2T = [sb(f"w2T{i}", [128, 2, Dff], F16) for i in range(2)]
        g32 = [sb(f"g32_{i}", [128, 512]) for i in range(2)]
        gs = [sb(f"gs{i}", [128, 2, 512], F16) for i in range(4)]

        x_in = sem("x_in")
        small_in = sem("small_in")
        weights_in = [sem(f"expert_in{i}") for i in range(2)]
        y_turned = sem("y_turned")
        residual = sem("residual")
        row_stats = sem("row_stats")
        token_stats = sem("token_stats")
        power_step = sem("power_step")
        token_norm = sem("token_norm")
        small_turned = sem("small_turned")
        small_copied = sem("small_copied")
        x_turned = sem("x_turned")
        xT_copied = sem("xT_copied")
        xT_high = sem("xT_high")
        xT_low = sem("xT_low")
        logits_ready = sem("logits_ready")
        route_step = sem("route_step")
        route_exp = sem("route_exp")
        weights_turned = sem("weights_turned")
        weights_high = sem("weights_high")
        weights_low = sem("weights_low")
        b1_ready = sem("b1_ready")
        h_ready = sem("h_ready")
        gelu_done = sem("gelu_done")
        g_high = sem("g_high")
        g_low = sem("g_low")
        y_done = sem("y_done")
        y_added = sem("y_added")
        wgt_turned = sem("wgt_turned")
        wgt_copied = sem("wgt_copied")
        bias_ready = sem("bias_ready")
        bias_added = sem("bias_added")
        stored = sem("stored")
        passed = sem("passed2")

        def wait(eng, s, e, per, extra):
            k, c = e
            n = k * (2 * per) + (c * per + extra)
            if isinstance(k, int) and n <= 0:
                return
            eng.wait_ge(s, n)
            if eng.engine == nc.sync.engine:
                eng.sem_inc(passed, 1)

        def run_experts(eng, body):
            body((0, 0))
            with eng.Fori(0, (E - 2) // 2) as k:
                body((k, 1))
                body((k, 2))
            body((0, E - 1))

        def is_first(e):
            return isinstance(e[0], int) and e[1] == 0

        def is_last(e):
            return isinstance(e[0], int) and e[1] == E - 1

        def nxt(e, d=1):
            return (e[0], e[1] + d)

        def width(g):
            return 128 * len(GROUPS[g])

        block = ctx.enter_context(nc.Block())

        @block.sync
        def _(sp):
            sp.dma_start(acc[:, :, :], x_rows).then_inc(x_in, 16)
            sp.dma_start(gate[:, :], gate_w).then_inc(small_in, 16)
            sp.dma_start(b1_rows[:, :], b1.rearrange("e (c f) -> (e c) f", f=128)).then_inc(small_in, 16)
            sp.dma_start(b2_rows[:, :], b2).then_inc(small_in, 16)

            def load(e):
                n = e[0] * 2 + e[1]
                s = weights_in[e[1] % 2]
                wait(sp, weights_turned, nxt(e, -2), 2, 2)
                sp.dma_start(w1n[e[1] % 2][:, :, :], w1[:, bass.ds(n, 1), :].rearrange(
                    "(c f) e d -> f (c e) d", f=128)).then_inc(s, 16)
                sp.dma_start(w2n[e[1] % 2][:, :, :], w2[:, bass.ds(n, 1), :].rearrange(
                    "d e (c f) -> d (e c) f", f=128)).then_inc(s, 16)

            load((0, 0))
            load((0, 1))
            with sp.Fori(0, (E - 2) // 2) as k:
                load((k, 2))
                load((k, 3))
            sp.wait_ge(y_added, E * len(GROUPS))
            sp.dma_start(out_rows, acc[:, :, :]).then_inc(stored, 16)
            sp.wait_ge(stored, 16)

        @block.gpsimd
        def _(pool):
            pool.memset(powers[:, :], -0.5).then_inc(power_step, 1)
            pool.wait_ge(power_step, 1)
            pool.wait_ge(token_stats, T)
            pool.tensor_scalar(rstd[:, :], mv[:, :, 1], 1.0, EPS, ALU.mult, ALU.add).then_inc(power_step, 1)
            pool.wait_ge(power_step, 2)
            pool.tensor_tensor(rstd[:, :], rstd[:, :], powers[:, :], ALU.pow).then_inc(power_step, 1)

        @block.tensor
        def _(pe):
            PASSES = ((0, 0), (0, 1), (1, 0))
            for t in range(T):
                if t >= 2:
                    pe.wait_ge(residual, t - 1)
                nc.tensor.transpose(turn_bank[t % 2][:, 0:128], yT[:, 128 * t:128 * t + 128], ident[:, :])\
                  .then_inc(y_turned, 1)
            pe.wait_ge(small_in, 48)
            nc.tensor.transpose(weight_bank[0][:, 0:E], gate[:, :], ident[0:E, 0:E]).then_inc(small_turned, 1)
            nc.tensor.transpose(weight_bank[1][:, 0:E * FC], b1_rows[:, :], ident[0:E * FC, 0:E * FC])\
              .then_inc(small_turned, 1)
            pe.wait_ge(small_copied, 2)

            def turn_weights(e, m):
                wait(pe, weights_in[e[1] % 2], (e[0], e[1] // 2 * 2), 16, 32)
                wait(pe, weights_low, nxt(e, -1), 2, m + 1)
                src = (w1n, w2n)[m][e[1] % 2]
                for c in range(FC):
                    mm = nc.tensor.transpose(weight_bank[m][:, 128 * c:128 * c + 128], src[:, c, :], ident[:, :])
                mm.then_inc(weights_turned, 1)

            turn_weights((0, 0), 0)
            turn_weights((0, 0), 1)
            pe.wait_ge(token_norm, T)
            for g, tiles in enumerate(GROUPS):
                if g >= 2:
                    pe.wait_ge(xT_low, g - 1)
                for j, t in enumerate(tiles):
                    mm = nc.tensor.transpose(turn_bank[g % 2][:, 128 * j:128 * j + 128], xm[:, t, :], ident[:, :])
                mm.then_inc(x_turned, 1)
            pe.wait_ge(xT_low, len(GROUPS))
            for t in range(T):
                mm = nc.tensor.matmul(turn_bank[0][:, E * t:E * t + E], xmT[:, 128 * t:128 * t + 128], gateT[:, :],
                                      start=True, stop=True)
            mm.then_inc(logits_ready, 1)
            def turn_router(part):
                pe.wait_ge(wgt_copied, part - 1) if part >= 2 else None
                for j, t in enumerate(GROUPS[part]):
                    mm = nc.tensor.transpose(turn_bank[part % 2][0:E, 128 * j:128 * j + 128], wgt[:, t, :],
                                             ident[:, :])
                mm.then_inc(wgt_turned, 1)

            def hidden(e, u):
                g, c = divmod(u, FC)
                w = width(g)
                if u == 0:
                    wait(pe, weights_low, e, 2, 2)
                wait(pe, gelu_done, e, UNITS, u - 1)
                for n, (a, z) in enumerate(PASSES):
                    mm = nc.tensor.matmul(h_banks[:, u % 2, 0:w], w1T[e[1] % 2][:, a, 128 * c:128 * c + 128],
                                          xmTs[:, z, 512 * g:512 * g + w], start=(n == 0), stop=(n == 2))
                mm.then_inc(h_ready, 1)

            def outputs(e, u):
                g, c = divmod(u, FC)
                wait(pe, g_low, e, UNITS, u + 1)
                if c == 0:
                    wait(pe, y_added, e, len(GROUPS), g - 1)
                for j in range(len(GROUPS[g])):
                    for n, (z, a) in enumerate(PASSES):
                        mm = nc.tensor.matmul(y_banks[:, g % 2, 128 * j:128 * j + 128],
                                              gs[u % 4][:, z, 128 * j:128 * j + 128],
                                              w2T[e[1] % 2][:, a, 128 * c:128 * c + 128],
                                              start=(c == 0 and j == 0 and n == 0),
                                              stop=(c == FC - 1 and n == 2), skip_group_check=True)
                mm.then_inc(y_done, 1)

            def body(e):
                for u in range(UNITS):
                    hidden(e, u)
                    if u in (4, 8) and not is_last(e):
                        turn_weights(nxt(e), u // 4 - 1)
                    if u >= 2:
                        outputs(e, u - 2)
                    elif not is_first(e):
                        outputs(nxt(e, -1), u + UNITS - 2)
                    if is_first(e) and u == 3:
                        pe.wait_ge(route_step, ROUTE_STEPS)
                        for part in range(len(GROUPS)):
                            turn_router(part)
                        pe.wait_ge(wgt_copied, len(GROUPS))
                        for part, tiles in enumerate(GROUPS):
                            if part >= 2:
                                pe.wait_ge(bias_added, part - 1)
                            for j, t in enumerate(tiles):
                                mm = nc.tensor.matmul(turn_bank[part % 2][:, 128 * j:128 * j + 128],
                                                      wgtT[:, 128 * t:128 * t + 128], b2_rows[:, :],
                                                      start=True, stop=True)
                            mm.then_inc(bias_ready, 1)

            run_experts(pe, body)
            outputs((0, E - 1), UNITS - 2)
            outputs((0, E - 1), UNITS - 1)

        @block.scalar
        def _(act):
            act.wait_ge(small_turned, 2)
            act.activation(gateT[:, :], weight_bank[0][:, 0:E], ACT.Copy).then_inc(small_copied, 1)
            act.activation(b1T[:, :], weight_bank[1][:, 0:E * FC], ACT.Copy).then_inc(small_copied, 1)
            act.wait_ge(small_copied, 2)

            def weights_split(e, m):
                wait(act, weights_turned, e, 2, m + 1)
                act.activation((w1T, w2T)[m][e[1] % 2][:, 0, :], weight_bank[m][:, :], ACT.Copy,
                               scale=(W1S, W2S)[m]).then_inc(weights_high, 1)

            weights_split((0, 0), 0)
            weights_split((0, 0), 1)
            for g, tiles in enumerate(GROUPS):
                cols = slice(512 * g, 512 * g + 128 * len(tiles))
                act.wait_ge(x_turned, g + 1)
                src = turn_bank[g % 2][:, 0:128 * len(tiles)]
                act.activation(xmT[:, cols], src, ACT.Copy).then_inc(xT_copied, 1)
                act.activation(xmTs[:, 0, cols], src, ACT.Copy, scale=ZS).then_inc(xT_high, 1)
            act.wait_ge(route_step, 2)
            act.activation(p[:, :, :], logit[:, :, :], ACT.Exp).then_inc(route_exp, 1)

            def body(e):
                n = e[0] * (2 * FC) + e[1] * FC
                b1_e = b1_now[e[1] % 2]
                act.activation(b1_e[:, :], b1T[:, bass.ds(n, FC)], ACT.Copy).then_inc(b1_ready, 1)
                wait(act, b1_ready, e, 1, 1)
                for u in range(UNITS):
                    g, c = divmod(u, FC)
                    w = width(g)
                    wait(act, h_ready, e, UNITS, u + 1)
                    wait(act, g_low, e, UNITS, u - 1)
                    act.activation(g32[u % 2][:, 0:w], h_banks[:, u % 2, 0:w], ACT.Gelu_apprx_tanh,
                                   bias=b1_e[:, c:c + 1],
                                   scale=1.0 / (W1S * ZS)).then_inc(gelu_done, 1)
                    wait(act, gelu_done, e, UNITS, u + 1)
                    wait(act, y_done, e, UNITS, u - 3)
                    act.activation(gs[u % 4][:, 0, 0:w], g32[u % 2][:, 0:w], ACT.Copy, scale=GS).then_inc(g_high, 1)
                    if u in (4, 8) and not is_last(e):
                        weights_split(nxt(e), u // 4 - 1)

            run_experts(act, body)

        @block.vector
        def _(dve):
            dve.wait_ge(x_in, 16)
            for t in range(T):
                dve.wait_ge(y_turned, t + 1)
                dve.tensor_tensor(acc[:, t, :], turn_bank[t % 2][:, 0:128], acc[:, t, :], ALU.add)\
                   .then_inc(residual, 1)
            for t in range(T):
                dve.wait_ge(residual, t + 1)
                dve.bn_stats(st[:, t, :], acc[:, t, :]).then_inc(row_stats, 1)
            for t in range(T):
                dve.wait_ge(row_stats, t + 1)
                ins = dve.bn_aggr(mv[:, t, :], st[:, t, :])
                ins.then_inc(token_stats, 1)
            dve.wait_ge(power_step, 3)
            for t in range(T):
                dve.tensor_scalar(xm[:, t, :], acc[:, t, :], mv[:, t, 0:1], rstd[:, t:t + 1], ALU.subtract,
                                  ALU.mult).then_inc(token_norm, 1)

            def weights_split(e, m):
                wait(dve, weights_high, e, 2, m + 1)
                dst = (w1T, w2T)[m][e[1] % 2]
                dve.scalar_tensor_tensor(out=dst[:, 1, :], in0=weight_bank[m][:, :], scalar=(W1S, W2S)[m],
                                         in1=dst[:, 0, :], op0=ALU.mult, op1=ALU.subtract)\
                   .then_inc(weights_low, 1)

            weights_split((0, 0), 0)
            weights_split((0, 0), 1)
            for g, tiles in enumerate(GROUPS):
                cols = slice(512 * g, 512 * g + 128 * len(tiles))
                dve.wait_ge(xT_high, g + 1)
                dve.scalar_tensor_tensor(out=xmTs[:, 1, cols], in0=turn_bank[g % 2][:, 0:128 * len(tiles)], scalar=ZS,
                                         in1=xmTs[:, 0, cols], op0=ALU.mult, op1=ALU.subtract).then_inc(xT_low, 1)

            n = 0

            def done(ins):
                nonlocal n
                n += 1
                ins.then_inc(route_step, 1)
                dve.wait_ge(route_step, n)

            def spread(ap):
                return ap.to_broadcast([128, T, E])

            dve.wait_ge(logits_ready, 1)
            logits = turn_bank[0][:, 0:T * E].rearrange("p (t e) -> p t e", e=E)
            done(dve.tensor_reduce(col[:, 0, :], logits, AX.X, ALU.max))
            done(dve.tensor_tensor(logit[:, :, :], logits, spread(col[:, 0, :].unsqueeze(2)), ALU.subtract))
            dve.wait_ge(route_exp, 1)
            done(dve.tensor_reduce(col[:, 1, :], p[:, :, :], AX.X, ALU.add))
            done(dve.reciprocal(col[:, 2, :], col[:, 1, :]))
            done(dve.tensor_tensor(p[:, :, :], p[:, :, :], spread(col[:, 2, :].unsqueeze(2)), ALU.mult))
            done(dve.memset(rank[:, :, :], 0.0))
            for e in range(E):
                for part, op in ((slice(0, e + 1), ALU.is_gt), (slice(e + 1, E), ALU.is_ge)):
                    w = part.stop - part.start
                    if w:
                        done(dve.tensor_tensor(above[:, :, part], p[:, :, e:e + 1].to_broadcast([128, T, w]),
                                               p[:, :, part], op))
                done(dve.tensor_tensor(rank[:, :, :], rank[:, :, :], above[:, :, :], ALU.add))
            done(dve.tensor_scalar(rank[:, :, :], rank[:, :, :], 2.0, 1.0, ALU.is_lt, ALU.mult))
            done(dve.tensor_tensor(wgt[:, :, :], p[:, :, :], rank[:, :, :], ALU.mult))
            done(dve.tensor_scalar(wgt_s[:, :, :], wgt[:, :, :], 1.0 / (W2S * GS), 1.0, ALU.mult, ALU.mult))
            assert n == ROUTE_STEPS

            def add_outputs(e, g):
                wait(dve, y_done, e, UNITS, FC * g + FC)
                k, c = e
                for j, t in enumerate(GROUPS[g]):
                    s = wgt_s[:, t, c:c + 1] if isinstance(k, int) else wgt_s[:, t, bass.ds(k * 2 + c, 1)]
                    ins = dve.scalar_tensor_tensor(out=acc[:, t, :], in0=y_banks[:, g % 2, 128 * j:128 * j + 128],
                                                   scalar=s, in1=acc[:, t, :], op0=ALU.mult, op1=ALU.add)
                ins.then_inc(y_added, 1)

            def body(e):
                for u in range(UNITS):
                    g, c = divmod(u, FC)
                    w = width(g)
                    wait(dve, g_high, e, UNITS, u + 1)
                    dve.scalar_tensor_tensor(out=gs[u % 4][:, 1, 0:w], in0=g32[u % 2][:, 0:w], scalar=GS,
                                             in1=gs[u % 4][:, 0, 0:w], op0=ALU.mult,
                                             op1=ALU.subtract).then_inc(g_low, 1)
                    if u in (4, 8) and not is_last(e):
                        weights_split(nxt(e), u // 4 - 1)
                    if is_first(e) and u == 3:
                        for part, tiles in enumerate(GROUPS):
                            dve.wait_ge(wgt_turned, part + 1)
                            dve.tensor_copy(wgtT[:, 512 * part:512 * part + width(part)],
                                            turn_bank[part % 2][0:E, 0:width(part)]).then_inc(wgt_copied, 1)
                        for part, tiles in enumerate(GROUPS):
                            dve.wait_ge(bias_ready, part + 1)
                            a, z = tiles[0], tiles[-1] + 1
                            dve.tensor_tensor(acc[:, a:z, :], turn_bank[part % 2][:, 0:width(part)].rearrange(
                                "p (t d) -> p t d", d=D), acc[:, a:z, :], ALU.add).then_inc(bias_added, 1)
                        dve.wait_ge(bias_added, len(GROUPS))
                    if u in (1, 5, 9, 13):
                        if u > 1:
                            add_outputs(e, u // 4 - 1)
                        elif not is_first(e):
                            add_outputs(nxt(e, -1), len(GROUPS) - 1)

            run_experts(dve, body)
            add_outputs((0, E - 1), len(GROUPS) - 1)


ROUTE_STEPS = 32


_INS = ["x", "ctx_1024", "L0_xattn_ln_m_g", "L0_xattn_ln_m_b", "L0_xattn_ln_l_g", "L0_xattn_ln_l_b",
        "L0_xattn_Wq", "L0_xattn_Wkv", "L0_xattn_Wout", "L0_ffn_gate_w", "L0_ffn_w1", "L0_ffn_b1",
        "L0_ffn_w2", "L0_ffn_b2"]


def kernel(**inputs):
    import numpy as _np
    import concourse.bacc as _bacc
    from concourse import mybir as _mybir
    from concourse.bass_utils import run_bass_kernel_spmd as _run

    nc = _bacc.Bacc("TRN2", target_bir_lowering=False, num_devices=1)
    arrays, args = {}, []
    for name in _INS:
        a = _np.ascontiguousarray(inputs[name])
        arrays[f"in_{name}"] = a
        args.append(nc.dram_tensor(f"in_{name}", a.shape, _mybir.dt.from_np(a.dtype), kind="ExternalInput").ap())
    shape = tuple(inputs["x"].shape)
    args.append(nc.dram_tensor("out_0", shape, _mybir.dt.float32, kind="ExternalOutput").ap())
    attention_and_experts(nc, *args)
    r = _run(nc, [arrays], core_ids=[0])
    return r.results[0]["out_0"]
```

```python
from contextlib import ExitStack

import concourse.bass as bass
from concourse import mybir

ALU = mybir.AluOpType
ACT = mybir.ActivationFunctionType
AX = mybir.AxisListType
F32 = mybir.dt.float32
F16 = mybir.dt.float16


CONST = 1024.0
ZS = 16.0
PSHIFT = 5.545177444479562
EPS = 1e-5
LEAD, NSLOT, UNROLL = 4, 14, 4


def attention_and_experts(nc, x, ctx_rows, ln_m_g, ln_m_b, ln_l_g, ln_l_b, Wq, Wkv, Wout,
                          gate_w, w1, b1, w2, b2, out):
    NB, S, D = x.shape
    M = ctx_rows.shape[1]
    INNER = Wq.shape[1]
    DH = 64
    H = INNER // DH
    HH = H // 2
    HC = HH * S
    QC = H * S
    TP = 125
    CT = M // TP
    NT = CT + 1
    QT = QC // 128
    TOK = NB * S
    E, Dff = b1.shape
    assert D == 128 and M == CT * TP and CT == 12 and QC == 7 * 128 and DH == 64 and Dff == 512

    with ExitStack() as top:
        def sem(name):
            return top.enter_context(nc.semaphore(name))

        psum = [top.enter_context(nc.psum_tensor(f"bank_pair{i}", [128, 2, 512], F32)) for i in range(2)]
        out_bank = top.enter_context(nc.psum_tensor("out_bank", [128, 512], F32))
        max_bank = [top.enter_context(nc.psum_tensor(f"max_bank{i}", [128, 512], F32)) for i in range(2)]
        misc = top.enter_context(nc.psum_tensor("misc", [128, 512], F32))
        misc16 = misc[:, :].bitcast(F16)

        def sbuf(stack, name, shape, dt=F32):
            return stack.enter_context(nc.sbuf_tensor(name, shape, dt))

        ident = sbuf(top, "ident", [128, 128])
        ident16 = sbuf(top, "ident16", [128, 128], F16)
        yT = sbuf(top, "yT", [128, TOK])

        T = TOK // 128
        FC = Dff // 128
        GROUP_COUNT = (T + 3) // 4
        GROUPS = [range(T - T * (n + 1) // GROUP_COUNT, T - T * n // GROUP_COUNT)
                  for n in reversed(range(GROUP_COUNT))]
        assert TOK == 128 * T
        W1S, W2S, GS = 64.0, 256.0, 16.0
        x_rows = x.rearrange("b s d -> (b s) d").rearrange("(t p) d -> p t d", p=128)

        raw_memory = sbuf(top, "raw_memory", [128, 4 * NT * D])
        A_memory = sbuf(top, "A_memory", [128, 2 * H * 128])

        def carve(memory):
            at = 0

            def take(n):
                nonlocal at
                at += n
                assert at <= memory.shape[1]
                return memory[:, at - n:at]
            return take

        take = carve(raw_memory)
        acc = take(T * D).rearrange("p (t d) -> p t d", d=D)
        xmT = take(T * 128)
        xmTs = take(T * 128).bitcast(F16).rearrange("p (a n) -> p a n", a=2)
        xm = [take(4 * D).rearrange("p (t d) -> p t d", d=D) for _ in range(2)]
        st = take(T * 6).rearrange("p (t c) -> p t c", c=6)
        mv = take(T * 2).rearrange("p (t c) -> p t c", c=2)
        rstd = take(T)
        powers = take(T)
        take = carve(A_memory)
        w1n = [take(FC * D).rearrange("p (c d) -> p c d", d=D) for _ in range(2)]
        w2n = [take(FC * 128).rearrange("p (c d) -> p c d", d=128) for _ in range(2)]
        w1T_first, w2T_first = (take(Dff).bitcast(F16).rearrange("p (a n) -> p a n", a=2) for _ in range(2))
        gate, b1_rows, b2_rows = (take(D) for _ in range(3))
        gateT = take(E)
        b1T = take(E * FC)
        gate, b2_rows, b1_rows = gate[0:E, :], b2_rows[0:E, :], b1_rows[0:E * FC, :]

        expert_in = [sem(f"expert_in{i}") for i in range(2)]
        weights_turned = sem("weights_turned")
        weights_high = sem("weights_high")
        weights_low = sem("weights_low")
        attention(nc, sem, sbuf, locals())
        experts(nc, sem, sbuf, locals())


def attention(nc, sem, sbuf, v):
    (x, ctx_rows, Wq, Wkv, Wout) = (v[n] for n in ("x", "ctx_rows", "Wq", "Wkv", "Wout"))
    gains = [v[n] for n in ("ln_m_g", "ln_m_b", "ln_l_g", "ln_l_b")]
    NB, S, D, H, HH, HC, QC, TP, CT, NT, QT = (v[n] for n in (
        "NB", "S", "D", "H", "HH", "HC", "QC", "TP", "CT", "NT", "QT"))
    score_banks, out_bank, max_bank, misc, misc16 = (v[n] for n in ("psum", "out_bank", "max_bank", "misc", "misc16"))
    ident, ident16, yT = v["ident"], v["ident16"], v["yT"]
    T, E, FC, GROUPS, x_rows, gate_w, w1, b1, w2, b2 = (v[n] for n in (
        "T", "E", "FC", "GROUPS", "x_rows", "gate_w", "w1", "b1", "w2", "b2"))
    acc, xmT, xmTs, xm, st, mv, rstd, powers = (v[n] for n in (
        "acc", "xmT", "xmTs", "xm", "st", "mv", "rstd", "powers"))
    w1n, w2n, gate, b1_rows, b2_rows, gateT, b1T = (v[n] for n in (
        "w1n", "w2n", "gate", "b1_rows", "b2_rows", "gateT", "b1T"))
    expert_in, weights_turned, weights_high, weights_low = (v[n] for n in (
        "expert_in", "weights_turned", "weights_high", "weights_low"))

    with ExitStack() as ctx:
        def sb(name, shape, dt=F32):
            return sbuf(ctx, name, shape, dt)

        raw = [v["raw_memory"][:, i * NT * D:(i + 1) * NT * D].rearrange("p (t d) -> p t d", d=D)
               for i in range(4)]
        stats = [sb(f"stats{i}", [128, NT, 6]) for i in range(2)]
        sm = sb("sm", [128, 8, NT])
        half_pow = sb("half_pow", [128, NT])
        keys = [sb(f"keys{i}", [128, 2, NT, D], F16) for i in range(4)]
        keysT = [sb(f"keysT{i}", [128, 2, NT, 128], F16) for i in range(4)]
        Q_all = sb("Q_all", [128, 4, 2, 2, QC], F16)
        Q = [Q_all[:, i] for i in range(4)]
        pair_rows = sb("pair_rows", [128, 1, D])
        pair_stats = sb("pair_stats", [128, 1, 6])
        pair_sm = sb("pair_sm", [128, 8, 1])
        pair_split = sb("pair_split", [128, 2, D], F16)
        pair_T = sb("pair_T", [128, 2, 2, 64], F16)
        A = v["A_memory"][:, :].bitcast(F16).rearrange("p (v a h c) -> p v a h c", v=2, a=2, c=128)
        B = sb("B", [128, 2, 2, H, 128], F16)
        prob = [sb(f"prob{i}", [128, 2 * HC]) for i in range(2)]
        probs = [sb(f"probs{i}", [128, 2, 2 * HC], F16) for i in range(4)]
        part_max = [sb(f"part_max{i}", [128, QT, 4]) for i in range(2)]
        neg_max = sb("neg_max", [128, 2, QT])
        neg_max16 = sb("neg_max16", [128, 2, QT], F16)
        shift_rows = sb("shift_rows", [2 * QT, 128], F16)
        O = [sb(f"O{i}", [128, 2, HC]) for i in range(2)]
        den = [sb(f"den{i}", [1, HC]) for i in range(2)]
        den64 = [sb(f"den64_{i}", [64, HC // 64]) for i in range(2)]
        recip64 = [sb(f"recip64_{i}", [64, HC // 64]) for i in range(2)]
        recip_dram = nc.dram_tensor("recip_dram", (2, HC), F32, kind="Internal").ap()
        recip_all = [sb(f"recip_all{i}", [128, HC]) for i in range(2)]
        On = sb("On", [128, 2, HC])
        Os = sb("Os", [128, 2, 2, 2, QC], F16)
        vecs = sb("vecs", [128, 4])
        vecs64 = sb("vecs64", [128, 2])
        row1 = sb("row1", [1, 128])

        wq_sb = keysT[0][:, :, :, :].rearrange("p a t c -> p (a t c)").bitcast(F32)[:, 0:1024]
        wkv_sb = keysT[1][:, :, :, :].rearrange("p a t c -> p (a t c)").bitcast(F32)[:, 0:1024]
        wv_sb = keysT[2][:, :, :, :].rearrange("p a t c -> p (a t c)").bitcast(F32)[:, 0:1024]
        wout_sb = keysT[3][:, :, :, :].rearrange("p a t c -> p (a t c)").bitcast(F32)[:, 0:1024]
        fold = [Q[j][:, :, :, :].rearrange("p a t c -> p (a t c)").bitcast(F32)[:, 0:1024] for j in range(4)]
        fold.append(Os[:, :, :, :, :].rearrange("p a t b c -> p (a t b c)").bitcast(F32)[:, 0:1024])
        lat_split = [sb(f"lat_split{i}", [128, D], F16) for i in range(4)]
        shift_pair = [sb(f"shift_pair{i}", [2, QC], F16) for i in range(2)]
        const_pair = sb("const_pair", [2, 128], F16)
        emb = Os[:, :, :, :, :].rearrange("p a t b c -> p (a t b c)").bitcast(F32)[:, 1024:1536]\
            .rearrange("p (e c) -> p e c", e=4)

        gains_in = sem("gains_in")
        wq_in = sem("wq_in")
        wk_in = sem("wk_in")
        wv_in = sem("wv_in")
        wout_in = sem("wout_in")
        passed = sem("passed")
        ident_ready = sem("ident_ready")
        filled = sem("filled")
        zeroed = sem("zeroed")
        emb_ready = sem("emb_ready")
        setup_product = sem("setup_product")
        setup_high = sem("setup_high")
        setup_low = sem("setup_low")
        raw_in = [sem(f"raw_in{i}") for i in range(4)]
        stats_ready = sem("stats_ready")
        small_step = sem("small_step")
        xn_ready = sem("xn_ready")
        high_ready = sem("high_ready")
        keys_ready = sem("keys_ready")
        transposed = sem("transposed")
        pair_in = sem("pair_in")
        pair_stats_ready = sem("pair_stats_ready")
        pair_step = sem("pair_step")
        pair_scaled = sem("pair_scaled")
        pair_high = sem("pair_high")
        pair_low = sem("pair_low")
        pair_turned = sem("pair_turned")
        q_product = sem("q_product")
        q_high = sem("q_high")
        max_product = sem("max_product")
        max_reduced = sem("max_reduced")
        shift_step = sem("shift_step")
        shift_turned = sem("shift_turned")
        shift_in = sem("shift_in")
        score_ready = sem("score_ready")
        exp_done = sem("exp_done")
        p_high = sem("p_high")
        p_low_v = sem("p_low_v")
        p_low_g = sem("p_low_g")
        pv_done = sem("pv_done")
        misc_free = sem("misc_free")
        out_copied = sem("out_copied")
        den_ready = sem("den_ready")
        den_spread = [sem(f"den_spread{i}") for i in range(2)]
        recip_ready = sem("recip_ready")
        recip_out = [sem(f"recip_out{i}") for i in range(2)]
        recip_spread = [sem(f"recip_spread{i}") for i in range(2)]
        on_ready = sem("on_ready")
        os_high = sem("os_high")
        os_ready = sem("os_ready")
        y_product = sem("y_product")
        last_reciprocal = sem("last_reciprocal")
        last_spread = sem("last_spread")
        x_in = sem("x_in")
        small_in = sem("small_in")
        y_turned = sem("y_turned")
        residual = sem("residual")
        row_stats = sem("row_stats")
        token_stats = sem("token_stats")
        power_step = sem("power_step")
        token_norm = sem("token_norm")
        small_turned = sem("small_turned")
        small_copied = sem("small_copied")
        x_turned = sem("x_turned")
        xT_high = sem("xT_high")
        xT_low = sem("xT_low")

        def count(b, per, extra):
            k, c = b
            return k * (UNROLL * per) + (c * per + extra)

        def wait(eng, s, b, per, extra):
            k, c = b
            if isinstance(k, int) and count(b, per, extra) <= 0:
                return
            eng.wait_ge(s, count(b, per, extra))
            if eng.engine in (nc.gpsimd.engine, nc.sync.engine):
                eng.sem_inc(passed, 1)

        def wait_pair(eng, s, b, extra, per=1):
            k, c = b
            n = c // 2 * per + extra
            if isinstance(k, int):
                if n > 0:
                    eng.wait_ge(s, n)
                return
            eng.wait_ge(s, k * (UNROLL // 2 * per) + n)
            if eng.engine in (nc.gpsimd.engine, nc.sync.engine):
                eng.sem_inc(passed, 1)

        def later(b, d):
            return (b[0], b[1] + d)

        def num(b):
            return b[0] * UNROLL + b[1]

        first, last = -4, NB

        MISC = [(0, "keysT", 2, 3), (1, "lat", -1, 1), (2, "q", 2, 0), (3, "q", 2, 1), (4, "q", 2, 2),
                (5, "q", 2, 3), (6, "keysT", 2, 0), (7, "keysT", 2, 1), (8, "lat", 0, 0), (9, "y", -1, 0),
                (10, "keysT", 2, 2), (11, "shift", 1, 0), (12, "pairT", 3, 0)]

        def in_step(what, c):
            return c % 2 == {"y": 0, "pairT": 1}.get(what, c % 2)

        QH = 4

        def query_place(b):
            return b[1] % 2, (b[1] - b[1] % 2) % 4

        MAXIMA = 3 * QT + 1

        def misc_uses(i):
            return [u for u in MISC if 0 <= i + u[2] < NB and in_step(u[1], i)]

        PIECES = [range(CT, NT)] + [range(t, t + 2) for t in range(0, CT, 2)]
        SCALE_SLOTS = (4, 5, 6, 7, 8, 9, 10)
        SMALL_STEPS = (0, 9, 10, 14, 16)
        FILLED = 9

        USES_PER_LOOP = sum(len(misc_uses(i)) for i in range(1, 1 + UNROLL))

        def second_bank(b, what, part):
            return isinstance(b[0], int) and b[1] < 2 and (what, part) in (("q", 1), ("q", 3), ("keysT", 1))

        def misc_bank(b, what, part):
            return out_bank if second_bank(b, what, part) else misc

        def query_part(b, w, a):
            var, first_of = query_place(b)
            return Q_all[:, first_of:first_of + 2, var, a, QH * S * w:QH * S * (w + 1)]

        def query_products(b, w):
            return misc_bank(b, "q", w)[:, 0:HC].rearrange("p (b n) -> p b n", b=2)

        def in_flight(i, slot):
            return int(i is not None and i in (-2, -1) and slot in (3, 4, 5, 7, 10))

        def misc_turn(eng, b, slot, less=0):
            k, c = b
            n = -less + sum(len(misc_uses(i)) for i in range(first, c)) + len([u for u in misc_uses(c) if u[0] < slot])
            if not isinstance(k, int) or n > 0:
                eng.wait_ge(misc_free, k * USES_PER_LOOP + n)

        def steps(eng, run):
            for i in range(first, 1):
                run((0, i), i)
            with eng.Fori(0, (NB - 8) // UNROLL) as k:
                for c in range(1, UNROLL + 1):
                    run((k, c), None)
            for i in range(NB - 7, last + 1):
                run((0, i), i)

        def live(i, d):
            return i is None or 0 <= i + d < NB

        W_OF = (wq_sb, wkv_sb, wkv_sb, wv_sb, wv_sb)
        EMB_OF = (0, 1, 2, 3, 0)
        FOLDS = 2 * 5
        SETUP = [("fold", n, q) for n in range(5) for q in range(2)] + \
                [(m, var, q) for m in "AB" for var in range(2) for q in range(H // 4)]
        A_SCALE = 64 ** -0.5
        ROW1 = -CONST / ZS

        EARLY = FOLDS + H // 2
        B_STEP = -1
        B_SLOTS = tuple(range(2, 2 + len(SETUP) - EARLY))

        def setup_in(i, k):
            return [EARLY + B_SLOTS.index(k)] if i == B_STEP and k in B_SLOTS else []

        TAIL = {}

        def in_tail(what, g, i, k):
            TAIL.setdefault((i + k // NSLOT, k % NSLOT), []).append((what, g))

        for g in range(len(GROUPS) - 1):
            for what, k in (("turn_y", 0), ("add_x", 1), ("power", 2), ("norm", 3), ("turn_x", 4),
                            ("xT_high", 5), ("xT_low", 6)):
                in_tail(what, g, NB - 1, 4 * g + k)
        for what, k in (("turn_y", 9), ("add_x", 10), ("power", 10), ("norm", 11), ("turn_x", 11),
                        ("xT_high", 12), ("xT_low", 13)):
            in_tail(what, len(GROUPS) - 1, NB, k)
        for what, k in (("turn_weights", 2), ("weights_high", 3), ("spread", 2), ("weights_low", 7), ("logits", 6)):
            in_tail(what, 0, NB, k)
        assert 128 * GROUPS[-1][0] <= (NB - 4) * S

        def tail(i, k, whats):
            return [t for t in TAIL.get((i, k), []) if t[0] in whats]

        def group_columns(g):
            return slice(128 * GROUPS[g][0], 128 * GROUPS[g][-1] + 128)

        def group_tiles(g):
            return slice(GROUPS[g][0], GROUPS[g][-1] + 1)

        def setup_bank(g):
            return max_bank[g % 2][:, :] if g < EARLY else score_banks[g % 2][:, 0, :]

        def setup_product_group(pe, g):
            what, n, q = SETUP[g]
            bank = setup_bank(g)
            if g >= 2:
                pe.wait_ge(setup_low, g - 1)
            if g == FOLDS:
                pe.wait_ge(setup_low, FOLDS)
            for j in range(4):
                o = bank[:, 128 * j:128 * j + 128]
                if what == "fold":
                    t = 4 * q + j
                    mm = nc.tensor.matmul(o, W_OF[n][:, 128 * t:128 * t + 128], emb[:, EMB_OF[n], :],
                                          start=True, stop=True)
                    continue
                h = 8 * (q // 2) + q % 2 + 2 * j
                rows, cols = slice(64 * (h % 2), 64 * (h % 2) + 64), slice(128 * (h // 2), 128 * (h // 2) + 128)
                l, r = (fold[0], fold[1 + n]) if what == "A" else (fold[3 + n], wout_sb)
                mm = nc.tensor.matmul(o, l[rows, cols], r[rows, cols], start=True, stop=True)
            mm.then_inc(setup_product, 1)

        def setup_split(what, n, q):
            first_head = 8 * (q // 2) + q % 2
            dst = (A if what == "A" else B)[:, n, :, first_head:first_head + 7:2, :]
            return dst, A_SCALE if what == "A" else 1.0

        block = ctx.enter_context(nc.Block())

        @block.sync
        def _(sp):
            def load_context(b):
                sp.dma_start(raw[b[1] % 4][0:TP, 0:CT, :],
                             ctx_rows[num(b)].rearrange("(p t) d -> p t d", t=CT)).then_inc(raw_in[b[1] % 4], 16)

            def load_latents(b):
                p = b[1] % 4
                sp.dma_start(raw[p][0:S, CT, :], x[num(b)]).then_inc(raw_in[p], 16)
                sp.dma_start(raw[p][64:64 + S, CT, :], x[num(b)]).then_inc(raw_in[p], 16)

            def load_pair(b):
                wait_pair(sp, pair_low, b, 0)
                for n, row in enumerate((0, 64)):
                    sp.dma_start(pair_rows[row:row + S, 0, :], x[num(later(b, n))]).then_inc(pair_in, 16)

            for n, g in enumerate(gains):
                sp.dma_start(vecs[:, n:n + 1], g.rearrange("(p a) -> p a", a=1)).then_inc(gains_in, 16)
            sp.wait_ge(filled, 1)
            load_pair((0, 0))
            sp.dma_start(wq_sb, Wq).then_inc(wq_in, 16)
            sp.dma_start(wkv_sb, Wkv[:, 0:H * 64]).then_inc(wk_in, 16)
            load_context((0, 0))
            sp.wait_ge(filled, 5)
            load_latents((0, 0))
            sp.dma_start(wv_sb, Wkv[:, H * 64:2 * H * 64]).then_inc(wv_in, 16)
            sp.dma_start(wout_sb.rearrange("p (t n) -> p t n", n=D),
                         Wout.rearrange("(t p) n -> p t n", p=128)).then_inc(wout_in, 16)
            def load(b):
                load_context(b)
                load_latents(b)

            for n in range(1, 3):
                load((0, n))

            def spread(b, half):
                wait(sp, den_ready, b, 2, half + 1)
                sp.dma_start(den64[half][:, :], den[half][0:1, :].rearrange("o (p c) -> o p c", p=64))\
                  .then_inc(den_spread[half], 16)
                wait(sp, recip_ready, b, 2, half + 1)
                sp.dma_start(recip_dram[half].rearrange("(p c) -> p c", p=64), recip64[half][:, :])\
                  .then_inc(recip_out[half], 16)
                wait(sp, recip_out[half], b, 16, 16)
                wait(sp, on_ready, later(b, -1), 2, half + 1)
                sp.dma_start(recip_all[half][:, :], recip_dram[half:half + 1, :].to_broadcast([128, HC]))\
                  .then_inc(recip_spread[half], 16)

            def step(b, i):
                if live(i, -1) and i != NB:
                    spread(later(b, -1), 1)
                if live(i, 0):
                    spread(b, 0)
                if live(i, 7):
                    wait(sp, keys_ready, later(b, 3), 7, 7)
                    load(later(b, 7))
                if b[1] % 2 and live(i, 5):
                    load_pair(later(b, 5))
                if i == NB - 3:
                    sp.wait_ge(keys_ready, 7 * NB)
                    sp.dma_start(acc, x_rows).then_inc(x_in, 16)
                if i == NB - 2:
                    sp.wait_ge(q_product, 4 * NB)
                    sp.dma_start(gate, gate_w).then_inc(small_in, 16)
                    sp.dma_start(b1_rows, b1.rearrange("e (c f) -> (e c) f", f=128)).then_inc(small_in, 16)
                    sp.dma_start(b2_rows, b2).then_inc(small_in, 16)
                    for e in range(2):
                        sp.dma_start(w1n[e], w1[:, e:e + 1, :].rearrange("(c f) e d -> f (c e) d", f=128))\
                          .then_inc(expert_in[e], 16)
                        sp.dma_start(w2n[e], w2[:, e:e + 1, :].rearrange("d e (c f) -> d (e c) f", f=128))\
                          .then_inc(expert_in[e], 16)

            steps(sp, step)

        @block.gpsimd
        def _(pool):
            pool.memset(pair_rows[:, :, :], 0.0).then_inc(filled, 1)
            pool.memset(ident[:, :], 0.0).then_inc(ident_ready, 1)
            pool.wait_ge(ident_ready, 1)
            pool.affine_select(out=ident[:, :], in_=ident[:, :], compare_op=ALU.not_equal, fill=1.0,
                               base=0, pattern=[[-1, 128]], channel_multiplier=1).then_inc(ident_ready, 1)
            pool.wait_ge(ident_ready, 2)
            pool.tensor_copy(ident16[:, :], ident[:, :]).then_inc(ident_ready, 1)
            for t in raw:
                pool.memset(t[:, CT, :], 0.0).then_inc(filled, 1)
            pool.memset(half_pow[:, :], -0.5).then_inc(filled, 1)
            pool.memset(keys[0][:, :, :, :], 0.0).then_inc(filled, 1)
            pool.wait_ge(filled, 7)
            pool.memset(keys[0][0:TP, 0, 0:CT, 0:1], CONST).then_inc(filled, 1)
            pool.memset(keys[0][0:S, 0, CT, 0:1], CONST).then_inc(filled, 1)
            pool.wait_ge(filled, FILLED)

            def arithmetic(part, did, st, w, pow_, lat):
                l2, l4, l5, l6 = (w[j][:, lat] for j in (2, 4, 5, 6))
                if part == 0:
                    did(pool.tensor_tensor(w[0], st[:, :, 1], st[:, :, 4], ALU.add),
                        pool.tensor_tensor(w[1], st[:, :, 1], st[:, :, 4], ALU.subtract),
                        pool.tensor_tensor(w[2], st[:, :, 2], st[:, :, 5], ALU.add))
                    did(pool.tensor_tensor(w[1], w[1], w[1], ALU.mult),
                        pool.tensor_scalar(w[2], w[2], 1.0 / D, 0.0, ALU.mult, ALU.add),
                        pool.tensor_scalar(w[7], w[0], -0.5, 0.0, ALU.mult, ALU.add))
                    did(pool.tensor_scalar(w[1], w[1], 0.25, 0.0, ALU.mult, ALU.add))
                    did(pool.tensor_tensor(w[2], w[2], w[1], ALU.add))
                    did(pool.tensor_scalar(w[3], w[2], 1.0 / ZS ** 2, EPS / ZS ** 2, ALU.mult, ALU.add))
                if part == 1:
                    did(pool.tensor_tensor(w[6], w[3], pow_, ALU.pow))
                if part == 2:
                    did(pool.tensor_tensor(l4, l6, l6, ALU.mult))
                    did(pool.tensor_tensor(l4, l4, l2, ALU.mult))
                    did(pool.tensor_scalar(l4, l4, 1.0 / ZS ** 2, EPS, ALU.mult, ALU.add))
                    did(pool.tensor_tensor(l5, l4, pow_[:, 0:1], ALU.pow))
                if part == 3:
                    did(pool.tensor_tensor(l6, l6, l5, ALU.mult))
                    did(pool.tensor_tensor(w[7], w[6], w[7], ALU.mult))

            def counted(part, s, waited):
                n = SMALL_STEPS[part]

                def did(*ins):
                    nonlocal n
                    for i in ins:
                        i.then_inc(s, 1)
                    n += len(ins)
                    waited(n)
                return did

            def small(b, part):
                if part == 0:
                    wait(pool, stats_ready, b, 1, 1)
                    wait(pool, xn_ready, b, 7, 0)
                did = counted(part, small_step, lambda n: wait(pool, small_step, b, SMALL_STEPS[-1], n))
                arithmetic(part, did, stats[b[1] % 2][0:TP], [sm[0:TP, j, :] for j in range(8)],
                           half_pow[0:TP, :], slice(CT, NT))

            def pair_small(b, part):
                if part == 0:
                    wait_pair(pool, pair_stats_ready, b, 1)
                did = counted(part, pair_step, lambda n: wait_pair(pool, pair_step, b, n, SMALL_STEPS[-1]))
                arithmetic(part, did, pair_stats[:, :, :], [pair_sm[:, j, :] for j in range(8)],
                           half_pow[:, 0:1], slice(0, 1))

            def pair_scale():
                rows = pair_rows[:, 0, 1:D]
                pool.tensor_scalar(rows, rows, pair_sm[:, 6, :], pair_sm[:, 7, :], ALU.mult, ALU.add)\
                    .then_inc(pair_scaled, 1)

            def pair_low_half(b):
                wait_pair(pool, pair_high, b, 1)
                pool.tensor_tensor(pair_split[:, 1, 1:D], pair_rows[:, 0, 1:D], pair_split[:, 0, 1:D],
                                   ALU.subtract).then_inc(pair_low, 1)

            def scale_tiles(b, n):
                for t in PIECES[n]:
                    rows = raw[b[1] % 4][0:TP, t, 1:D]
                    ins = pool.tensor_scalar(rows, rows,
                                             sm[0:TP, 6, t:t + 1], sm[0:TP, 7, t:t + 1], ALU.mult, ALU.add)
                ins.then_inc(xn_ready, 1)

            def tiles_low(b, n):
                kb = keys[b[1] % 4]
                a, e = PIECES[n][0], PIECES[n][-1] + 1
                wait(pool, high_ready, b, 7, n + 1)
                pool.tensor_tensor(kb[0:TP, 1, a:e, 1:D], raw[b[1] % 4][0:TP, a:e, 1:D], kb[0:TP, 0, a:e, 1:D],
                                   ALU.subtract).then_inc(keys_ready, 1)

            def step(b, i):
                for k in range(NSLOT):
                    if live(i, 0) and k % 7 != 6:
                        u = count(b, NSLOT, k)
                        wait(pool, p_high, b, NSLOT, k + 1)
                        pb = probs[(2 * b[1] + k) % 4]
                        pool.tensor_tensor(pb[:, 1, HC:], prob[k % 2][:, HC:], pb[:, 0, HC:],
                                           ALU.subtract).then_inc(p_low_g, 1)
                    if live(i, 3):
                        if k < 4:
                            small(later(b, 3), k)
                        if k in SCALE_SLOTS:
                            scale_tiles(later(b, 3), SCALE_SLOTS.index(k))
                        if k - 2 in SCALE_SLOTS:
                            tiles_low(later(b, 3), SCALE_SLOTS.index(k - 2))
                    if b[1] % 2 == 0 and live(i, 4) and k >= 10:
                        pair_small(later(b, 4), k - 10)
                        if k == 13:
                            pair_scale()
                    if b[1] % 2 and live(i, 3) and k == 7:
                        pair_low_half(later(b, 3))
                    for what, g in tail(i, k, ("power",)):
                        if g == 0:
                            pool.memset(powers, -0.5).then_inc(power_step, 1)
                            pool.wait_ge(power_step, 1)
                        tiles = group_tiles(g)
                        pool.wait_ge(token_stats, g + 1)
                        pool.tensor_scalar(rstd[:, tiles], mv[:, tiles, 1], 1.0, EPS, ALU.mult, ALU.add)\
                            .then_inc(power_step, 1)
                        pool.wait_ge(power_step, 2 * g + 2)
                        pool.tensor_tensor(rstd[:, tiles], rstd[:, tiles], powers[:, tiles], ALU.pow)\
                            .then_inc(power_step, 1)

            steps(pool, step)

        @block.tensor
        def _(pe):
            PASSES = ((0, 0), (0, 1), (1, 0))
            pe.wait_ge(ident_ready, 3)
            pe.wait_ge(emb_ready, 16)
            for g in range(EARLY):
                if g in (0, 2, 6):
                    pe.wait_ge((wq_in, wk_in, wk_in, wv_in)[g // 2], 16)
                if g == FOLDS:
                    pe.wait_ge(wout_in, 16)
                setup_product_group(pe, g)
            pe.wait_ge(setup_low, EARLY)

            def scores(b, k):
                qb, kb = Q[b[1] % 4], keysT[b[1] % 4]
                half, p = divmod(k, 7)
                wait(pe, exp_done, b, NSLOT, k - 1)
                if k == 0 and isinstance(b[0], int) and b[1] == 0:
                    pe.wait_ge(setup_low, len(SETUP))
                if k == 0:
                    wait(pe, shift_in, b, 32, 32)
                cols = slice(half * HC, half * HC + HC)
                for j, t in enumerate(range(2 * p, min(2 * p + 2, NT))):
                    var = int(t == CT)
                    o = score_banks[k % 2][:, j, 0:HC]
                    for n, (ks, qs) in enumerate(PASSES):
                        mm = nc.tensor.matmul(o, kb[:, ks, t, :], qb[:, var, qs, cols],
                                              start=(n == 0), stop=(n == 2 and not var))
                    if var:
                        mm = nc.tensor.matmul(o, const_pair[:, :], shift_pair[b[1] % 2][:, cols],
                                              start=False, stop=True)
                mm.then_inc(score_ready, 1)

            def values(b, k):
                half, p = divmod(k, 7)
                kb, pb = keys[b[1] % 4], probs[(2 * b[1] + k) % 4]
                wait(pe, p_low_v, b, NSLOT, k + 1)
                wait(pe, p_low_g, b, 12, (k + 1) - (k + 1) // 7)
                if p == 0:
                    wait(pe, out_copied, b, 2, half)
                if p == 6:
                    misc_turn(pe, later(b, half), 1 if half else 8)
                for j, t in enumerate(range(2 * p, min(2 * p + 2, NT))):
                    if t == CT:
                        nc.tensor.matmul(misc[:, 0:HC], lat_split[b[1] % 4][:, :], pb[:, 0, 0:HC],
                                         start=True, stop=False)
                        mm = nc.tensor.matmul(misc[:, 0:HC], kb[0:64, 0, CT, :], pb[0:64, 1, 0:HC],
                                              start=False, stop=True)
                        continue
                    for n, (ks, ps) in enumerate(PASSES):
                        mm = nc.tensor.matmul(out_bank[:, 0:HC], kb[:, ks, t, :], pb[:, ps, j * HC:j * HC + HC],
                                              start=(n == 0 and t == 0), stop=(n == 2 and t == CT - 1))
                mm.then_inc(pv_done, 1)

            def maxima(b, t, j):
                qb, kb = Q[b[1] % 4], keysT[b[1] % 4]
                n = 3 * t + j if j < 3 else MAXIMA - 1
                if n == 0:
                    misc_turn(pe, later(b, -2), 11)
                if j == 3:
                    misc_turn(pe, later(b, -1), 6)
                wait(pe, max_reduced, b, MAXIMA, n - 1)
                if j < 3:
                    mm = nc.tensor.matmul(max_bank[n % 2][:, 0:4 * TP], qb[:, 0, 0, 128 * t:128 * t + 128],
                                          kb[:, 0, 4 * j:4 * j + 4, 0:TP], start=True, stop=True)
                else:
                    for q in range(QT):
                        mm = nc.tensor.matmul(max_bank[n % 2][:, q * S:q * S + S], qb[:, 1, 0, 128 * q:128 * q + 128],
                                              kb[:, 0, CT, 0:S], start=True, stop=True)
                mm.then_inc(max_product, 1)

            def turn_keys(b, j):
                kb = keys[b[1] % 4]
                wait(pe, keys_ready, b, 7, 1 if j == 3 else 7)
                tiles = range(4 * j, min(4 * j + 4, NT))
                o = misc_bank(b, "keysT", j)[:, :].bitcast(F16).rearrange("p (a t c) -> p a t c", a=2, t=4)
                for a in range(2):
                    for t in tiles:
                        mm = nc.tensor.transpose(o[:, a, t - 4 * j, :], kb[:, a, t, :], ident16[:, :])
                mm.then_inc(transposed, 1)

            def turn_pair(b):
                wait_pair(pe, pair_low, b, 1)
                for a in range(2):
                    mm = nc.tensor.transpose(misc16[:, 128 * a:128 * a + 128], pair_split[:, a, :], ident16[:, :])
                mm.then_inc(pair_turned, 1)

            def queries(b, w):
                var, _ = query_place(b)
                o = misc_bank(b, "q", w)[:, 0:HC].rearrange("p (b h c) -> p b h c", b=2, h=QH)
                for h in range(QH):
                    for n, (a, z) in enumerate(PASSES):
                        mm = nc.tensor.matmul(o[:, :, h, :], A[:, var, a, QH * w + h, :], pair_T[:, z, :, 0:S],
                                              start=(n == 0), stop=(n == 2))
                mm.then_inc(q_product, 1)

            def shift(b):
                wait(pe, shift_step, b, 4, 4)
                nc.tensor.transpose(misc16[0:2 * QT, 0:128], neg_max16[:, :, :].rearrange("p a t -> p (a t)"),
                                    ident16[:, :]).then_inc(shift_turned, 1)

            def project(b):
                wait(pe, os_ready, b, 2, 2)
                n = 0
                for var in range(2):
                    for h in range(H):
                        for w, o in PASSES:
                            mm = nc.tensor.matmul(misc[:, 0:2 * S], B[:, var, w, h, :],
                                                  Os[:, o, var, :, h * S:h * S + S],
                                                  start=(n == 0), stop=(n == 6 * H - 1))
                            n += 1
                mm.then_inc(y_product, 1)

            def misc_use(b, i, k):
                for slot, what, d, part in MISC:
                    if slot != k or not live(i, d) or what == "lat" or not in_step(what, b[1]):
                        continue
                    misc_turn(pe, b, slot, in_flight(i, slot))
                    g = later(b, d)
                    if what == "keysT":
                        turn_keys(g, part)
                    if what == "q":
                        queries(g, part)
                    if what == "pairT":
                        turn_pair(g)
                    if what == "y":
                        project(g)
                    if what == "shift":
                        shift(g)

            def experts_part(b, what, g):
                if what == "turn_y":
                    if g == 0:
                        pe.wait_ge(max_reduced, MAXIMA * NB)
                    if g == len(GROUPS) - 1:
                        misc_turn(pe, b, 10)
                    if g > 0:
                        pe.wait_ge(residual, g)
                    for j, t in enumerate(GROUPS[g]):
                        mm = nc.tensor.transpose(max_bank[0][:, 128 * j:128 * j + 128],
                                                 yT[:, 128 * t:128 * t + 128], ident[:, :])
                    mm.then_inc(y_turned, 1)
                if what == "turn_x":
                    pe.wait_ge(token_norm, g + 1)
                    if g > 0:
                        pe.wait_ge(xT_low, g)
                    for j in range(len(GROUPS[g])):
                        mm = nc.tensor.transpose(max_bank[1][:, 128 * j:128 * j + 128], xm[g % 2][:, j, :],
                                                 ident[:, :])
                    mm.then_inc(x_turned, 1)
                if what == "turn_weights":
                    pe.wait_ge(exp_done, NSLOT * NB)
                    pe.wait_ge(small_in, 48)
                    nc.tensor.transpose(score_banks[1][:, 0, 0:E], gate, ident[0:E, 0:E]).then_inc(small_turned, 1)
                    nc.tensor.transpose(score_banks[1][:, 1, 0:E * FC], b1_rows, ident[0:E * FC, 0:E * FC])\
                      .then_inc(small_turned, 1)
                    pe.wait_ge(expert_in[0], 32)
                    for m, w in enumerate((w1n[0], w2n[0])):
                        for c in range(FC):
                            mm = nc.tensor.transpose(score_banks[0][:, m, 128 * c:128 * c + 128], w[:, c, :],
                                                     ident[:, :])
                        mm.then_inc(weights_turned, 1)
                if what == "spread":
                    pe.wait_ge(last_reciprocal, 1)
                    nc.tensor.matmul(max_bank[1][:, 0:HC], row1[:, :], recip_all[1][0:1, :],
                                     start=True, stop=True).then_inc(last_spread, 1)
                if what == "logits":
                    pe.wait_ge(small_copied, 2)
                    pe.wait_ge(xT_high, 2 * (len(GROUPS) - 1))
                    for t in range(GROUPS[-1][0]):
                        nc.tensor.matmul(score_banks[1][:, 1, E * t:E * t + E], xmT[:, 128 * t:128 * t + 128],
                                         gateT, start=True, stop=True)

            def chunks(b, i, k, which):
                m = k + 3
                d, m = (1, m) if m < NSLOT else (2, m - NSLOT)
                t, j = m // 2, 2 * (m % 2) + which
                if live(i, d) and (j < 3 or t == QT - 1):
                    maxima(later(b, d), t, j)

            def step(b, i):
                for k in range(NSLOT):
                    if live(i, 0):
                        scores(b, k)
                    chunks(b, i, k, 0)
                    if k >= 2 and live(i, 0):
                        values(b, k - 2)
                    if k < 2 and live(i, -1):
                        values(later(b, -1), k + 12)
                    chunks(b, i, k, 1)
                    misc_use(b, i, k)
                    for g in setup_in(i, k):
                        setup_product_group(pe, g)
                    for what, g in tail(i, k, ("turn_y", "turn_x", "turn_weights", "spread", "logits")):
                        experts_part(b, what, g)

            steps(pe, step)

        @block.scalar
        def _(act):
            def setup_high_half(g):
                dst, scale = setup_split(*SETUP[g])
                act.wait_ge(setup_product, g + 1)
                act.activation(dst[:, 0], setup_bank(g).rearrange("p (h c) -> p h c", h=4), ACT.Copy,
                               scale=scale).then_inc(setup_high, 1)

            for g in range(FOLDS, EARLY):
                setup_high_half(g)

            def soften(b, k):
                w = HC if k % 7 == 6 else 2 * HC
                wait(act, score_ready, b, NSLOT, k + 1)
                wait(act, p_low_v, b, NSLOT, k - 1)
                wait(act, p_low_g, b, 12, (k - 1) - (k - 1) // 7)
                act.activation(prob[k % 2][:, 0:w].rearrange("p (j c) -> p j c", c=HC),
                               score_banks[k % 2][:, 0:w // HC, 0:HC], ACT.Exp,
                               scale=1.0 / CONST).then_inc(exp_done, 1)
                wait(act, exp_done, b, NSLOT, k + 1)
                wait(act, pv_done, b, NSLOT, k - 3)
                act.activation(probs[(2 * b[1] + k) % 4][:, 0, 0:w], prob[k % 2][:, 0:w],
                               ACT.Copy).then_inc(p_high, 1)

            def misc_copy(b, i, k):
                for slot, what, d, part in MISC:
                    if slot != k or not live(i, d) or not in_step(what, b[1]):
                        continue
                    g = later(b, d)
                    qb = Q[g[1] % 4]
                    if what == "keysT":
                        wait(act, transposed, g, 4, (part + 1) % 4 + 1)
                        tiles = slice(4 * part, min(4 * part + 4, NT))
                        src = misc_bank(g, "keysT", part)[:, :].bitcast(F16).rearrange(
                            "p (a t c) -> p a t c", a=2, t=4)
                        act.activation(keysT[g[1] % 4][:, :, tiles, :], src[:, :, 0:tiles.stop - tiles.start, :],
                                       ACT.Copy).then_inc(misc_free, 1)
                    if what == "q":
                        wait(act, q_product, g, 4, part + 1)
                        act.activation(query_part(g, part, 0), query_products(g, part), ACT.Copy,
                                       scale=1.0 / CONST).then_inc(q_high, 1)
                    if what == "pairT":
                        wait_pair(act, pair_turned, g, 1)
                        act.activation(pair_T[:, :, :, :], misc16[:, 0:256].rearrange(
                            "p (a b c) -> p a b c", a=2, b=2), ACT.Copy).then_inc(misc_free, 1)
                    if what == "y":
                        wait_pair(act, y_product, g, 1)
                        act.activation(yT[:, bass.ds(num(later(g, -1)) * S, 2 * S)], misc[:, 0:2 * S], ACT.Copy,
                                       scale=1.0 / CONST).then_inc(misc_free, 1)
                    if what == "shift":
                        wait(act, shift_turned, g, 1, 1)
                        wait(act, shift_in, later(g, -1), 32, 32)
                        act.activation(shift_rows[:, :], misc16[0:2 * QT, 0:128], ACT.Copy).then_inc(misc_free, 1)
                        misc_turn(act, b, 12)
                        act.dma_start(qb[0:1, 0, :, :].rearrange("o a (t c) -> o (a t) c", c=128),
                                      shift_rows[:, :]).then_inc(shift_in, 16)
                        act.dma_start(shift_pair[g[1] % 2][:, :].rearrange("a (t c) -> a t c", c=128),
                                      shift_rows[:, :]).then_inc(shift_in, 16)

            def experts_part(what, g):
                if what == "xT_high":
                    act.wait_ge(x_turned, g + 1)
                    src = max_bank[1][:, 0:128 * len(GROUPS[g])]
                    act.activation(xmTs[:, 0, group_columns(g)], src, ACT.Copy, scale=ZS).then_inc(xT_high, 1)
                    act.activation(xmT[:, group_columns(g)], src, ACT.Copy).then_inc(xT_high, 1)
                if what == "weights_high":
                    act.wait_ge(small_turned, 2)
                    act.activation(gateT, score_banks[1][:, 0, 0:E], ACT.Copy).then_inc(small_copied, 1)
                    act.activation(b1T, score_banks[1][:, 1, 0:E * FC], ACT.Copy).then_inc(small_copied, 1)
                    for m, (w, scale) in enumerate(((v["w1T_first"], v["W1S"]), (v["w2T_first"], v["W2S"]))):
                        act.wait_ge(weights_turned, m + 1)
                        act.activation(w[:, 0, :], score_banks[0][:, m, :], ACT.Copy,
                                       scale=scale).then_inc(weights_high, 1)

            def step(b, i):
                for k in range(NSLOT):
                    if live(i, 0):
                        soften(b, k)
                    misc_copy(b, i, k)
                    for g in setup_in(i, k):
                        setup_high_half(g)
                    for what, g in tail(i, k, ("xT_high", "weights_high")):
                        experts_part(what, g)

            steps(act, step)

        @block.vector
        def _(dve):
            def experts_part(what, g):
                if what == "add_x":
                    tiles = group_tiles(g)
                    dve.wait_ge(x_in, 16)
                    dve.wait_ge(y_turned, g + 1)
                    dve.tensor_tensor(acc[:, tiles, :], max_bank[0][:, 0:128 * len(GROUPS[g])].rearrange(
                        "p (t d) -> p t d", d=D), acc[:, tiles, :], ALU.add).then_inc(residual, 1)
                    dve.wait_ge(residual, g + 1)
                    for t in GROUPS[g]:
                        dve.bn_stats(st[:, t, :], acc[:, t, :]).then_inc(row_stats, 1)
                    for t in GROUPS[g]:
                        dve.wait_ge(row_stats, t + 1)
                        ins = dve.bn_aggr(mv[:, t, :], st[:, t, :])
                    ins.then_inc(token_stats, 1)
                if what == "norm":
                    dve.wait_ge(power_step, 2 * g + 3)
                    if g >= 2:
                        dve.wait_ge(x_turned, g - 1)
                    for j, t in enumerate(GROUPS[g]):
                        ins = dve.tensor_scalar(xm[g % 2][:, j, :], acc[:, t, :], mv[:, t, 0:1], rstd[:, t:t + 1],
                                                ALU.subtract, ALU.mult)
                    ins.then_inc(token_norm, 1)
                if what == "xT_low":
                    dve.wait_ge(xT_high, 2 * g + 2)
                    dve.scalar_tensor_tensor(out=xmTs[:, 1, group_columns(g)],
                                             in0=max_bank[1][:, 0:128 * len(GROUPS[g])], scalar=ZS,
                                             in1=xmTs[:, 0, group_columns(g)], op0=ALU.mult,
                                             op1=ALU.subtract).then_inc(xT_low, 1)
                if what == "weights_low":
                    for m, (w, scale) in enumerate(((v["w1T_first"], v["W1S"]), (v["w2T_first"], v["W2S"]))):
                        dve.wait_ge(weights_high, m + 1)
                        dve.scalar_tensor_tensor(out=w[:, 1, :], in0=score_banks[0][:, m, :], scalar=scale,
                                                 in1=w[:, 0, :], op0=ALU.mult,
                                                 op1=ALU.subtract).then_inc(weights_low, 1)

            def setup_low_half(g):
                what, n, q = SETUP[g]
                bank = setup_bank(g)
                if what == "fold":
                    dve.wait_ge(setup_product, g + 1)
                    dve.tensor_copy(fold[n][:, 512 * q:512 * q + 512], bank).then_inc(setup_low, 1)
                else:
                    dst, scale = setup_split(what, n, q)
                    dve.wait_ge(setup_high, g + 1 - FOLDS)
                    dve.scalar_tensor_tensor(out=dst[:, 1], in0=bank.rearrange("p (h c) -> p h c", h=4),
                                             scalar=scale, in1=dst[:, 0], op0=ALU.mult,
                                             op1=ALU.subtract).then_inc(setup_low, 1)

            def reduce_max(b, t, j):
                n = 3 * t + j if j < 3 else MAXIMA - 1
                wait(dve, max_product, b, MAXIMA, n + 1)
                if n == 0:
                    wait(dve, shift_step, later(b, -2), 4, 1)
                pm = part_max[b[1] % 2]
                if j < 3:
                    dve.reduce_max(pm[:, t, j:j + 1], max_bank[n % 2][:, 0:4 * TP], AX.X).then_inc(max_reduced, 1)
                else:
                    dve.reduce_max(pm[:, :, 3], max_bank[n % 2][:, 0:QT * S].rearrange("p (t c) -> p t c", c=S),
                                   AX.X).then_inc(max_reduced, 1)

            def reduce_part(b, i, m, which):
                d, m = (1, m) if m < NSLOT else (2, m - NSLOT)
                t, j = m // 2, 2 * (m % 2) + which
                if live(i, d) and (j < 3 or t == QT - 1):
                    reduce_max(later(b, d), t, j)

            def make_shift(b):
                wait(dve, max_reduced, b, MAXIMA, MAXIMA)
                wait(dve, shift_turned, later(b, -1), 1, 1)
                dve.tensor_reduce(neg_max[:, 0, :], part_max[b[1] % 2][:, :, :], AX.X, ALU.max,
                                  negate=True).then_inc(shift_step, 1)
                wait(dve, shift_step, b, 4, 1)
                dve.tensor_scalar(neg_max[:, 1, :], neg_max[:, 0, :], 1.0 / CONST, PSHIFT, ALU.mult, ALU.add)\
                   .then_inc(shift_step, 1)
                wait(dve, shift_step, b, 4, 2)
                dve.tensor_copy(neg_max16[:, 0, :], neg_max[:, 1, :]).then_inc(shift_step, 1)
                wait(dve, shift_step, b, 4, 3)
                dve.tensor_tensor(neg_max16[:, 1, :], neg_max[:, 1, :], neg_max16[:, 0, :],
                                  ALU.subtract).then_inc(shift_step, 1)

            def low(b, k):
                pb = probs[(2 * b[1] + k) % 4]
                wait(dve, p_high, b, NSLOT, k + 1)
                dve.tensor_tensor(pb[:, 1, 0:HC], prob[k % 2][:, 0:HC], pb[:, 0, 0:HC],
                                  ALU.subtract).then_inc(p_low_v, 1)

            def query_low(b, w):
                wait(dve, q_high, b, 4, w + 1)
                dve.scalar_tensor_tensor(out=query_part(b, w, 1), in0=query_products(b, w), scalar=1.0 / CONST,
                                         in1=query_part(b, w, 0), op0=ALU.mult,
                                         op1=ALU.subtract).then_inc(misc_free, 1)

            def pair_statistics(b):
                wait_pair(dve, pair_step, b, 0, SMALL_STEPS[-1])
                wait_pair(dve, pair_in, b, 32, 32)
                dve.bn_stats(pair_stats[:, 0, :], pair_rows[:, 0, :]).then_inc(pair_stats_ready, 1)

            def pair_high_half(b):
                wait_pair(dve, pair_turned, b, 0)
                wait_pair(dve, pair_scaled, b, 1)
                dve.tensor_copy(pair_split[:, 0, 1:D], pair_rows[:, 0, 1:D]).then_inc(pair_high, 1)

            def statistics(b, t):
                if t == 0:
                    wait(dve, raw_in[b[1] % 4], (b[0], b[1] // 4 * 4), 12, 48)
                    wait(dve, small_step, later(b, -2), SMALL_STEPS[-1], SMALL_STEPS[-1])
                ins = dve.bn_stats(stats[b[1] % 2][0:TP, t, :], raw[b[1] % 4][0:TP, t, :])
                if t == NT - 1:
                    ins.then_inc(stats_ready, 1)

            def tiles_high(b, n):
                wait(dve, xn_ready, b, 7, n + 1)
                if n == 0:
                    wait(dve, pv_done, later(b, -4), NSLOT, NSLOT)
                if n == 1:
                    ls, kl, rl = lat_split[b[1] % 4], keys[b[1] % 4], raw[b[1] % 4]
                    wait(dve, high_ready, b, 7, 1)
                    dve.tensor_copy(ls[0:S, 1:D], kl[0:S, 0, CT, 1:D])
                    dve.tensor_tensor(ls[64:64 + S, 1:D], rl[64:64 + S, CT, 1:D], kl[64:64 + S, 0, CT, 1:D],
                                      ALU.subtract)
                a, e = PIECES[n][0], PIECES[n][-1] + 1
                dve.tensor_copy(keys[b[1] % 4][0:TP, 0, a:e, 1:D], raw[b[1] % 4][0:TP, a:e, 1:D])\
                   .then_inc(high_ready, 1)

            def out_copy(b, half):
                wait(dve, pv_done, b, NSLOT, 7 * half + 6)
                wait(dve, on_ready, later(b, -1), 2, half + 1)
                dve.tensor_copy(O[half][:, 0, :], out_bank[:, 0:HC]).then_inc(out_copied, 1)

            def latent_copy(b, half):
                wait(dve, pv_done, b, NSLOT, 7 * half + 7)
                dve.tensor_copy(O[half][:, 1, :], misc[:, 0:HC]).then_inc(misc_free, 1)

            def denominator(b, half):
                misc_turn(dve, later(b, half), 2 if half else 9)
                wait(dve, out_copied, b, 2, half + 1)
                dve.tensor_tensor(den[half][:, :], O[half][0:1, 0, :], O[half][0:1, 1, :], ALU.add)\
                   .then_inc(den_ready, 1)

            def reciprocals(b, half):
                wait(dve, den_spread[half], b, 16, 16)
                dve.reciprocal(recip64[half][:, :], den64[half][:, :]).then_inc(recip_ready, 1)

            def last_reciprocals():
                dve.wait_ge(den_ready, 2 * NB)
                dve.wait_ge(xT_low, len(GROUPS) - 1)
                dve.reciprocal(recip_all[1][0:1, :], den[1][:, :]).then_inc(last_reciprocal, 1)

            def normalise(b, half, last=False):
                if last:
                    dve.wait_ge(last_spread, 1)
                else:
                    wait(dve, recip_spread[half], b, 16, 16)
                wait(dve, os_ready, b, 2, half)
                rb = (max_bank[1][:, 0:HC] if last else recip_all[half][:, :]).unsqueeze(1)\
                    .to_broadcast([128, 2, HC])
                dve.scalar_tensor_tensor(out=On[:, :, :], in0=O[half][:, :, :],
                                         scalar=CONST / ROW1 if last else CONST, in1=rb,
                                         op0=ALU.mult, op1=ALU.mult).then_inc(on_ready, 1)
                wait(dve, on_ready, b, 2, half + 1)
                if half == 0:
                    wait_pair(dve, y_product, b, 0)
                cols = slice(half * HC, half * HC + HC)
                dve.tensor_copy(Os[:, 0, :, b[1] % 2, cols], On[:, :, :]).then_inc(os_high, 1)

            def normal_low(b, half):
                wait(dve, os_high, b, 2, half + 1)
                cols = slice(half * HC, half * HC + HC)
                dve.tensor_tensor(Os[:, 1, :, b[1] % 2, cols], On[:, :, :], Os[:, 0, :, b[1] % 2, cols],
                                  ALU.subtract).then_inc(os_ready, 1)

            def step(b, i):
                for k in range(NSLOT):
                    if k == 2 and live(i, -1):
                        latent_copy(later(b, -1), 1)
                    if k == 9 and live(i, 0):
                        latent_copy(b, 0)
                    if k == 6 and live(i, 2):
                        query_low(later(b, 2), 3)
                    if k >= 1 and live(i, 0):
                        low(b, k - 1)
                    if k == 0 and live(i, -1):
                        low(later(b, -1), NSLOT - 1)
                    if k in (3, 4, 5) and live(i, 2):
                        query_low(later(b, 2), k - 3)
                    if k == 1 and live(i, -1):
                        out_copy(later(b, -1), 1)
                    if k == 2 and live(i, -1):
                        denominator(later(b, -1), 1)
                    if k == 8 and live(i, 0):
                        out_copy(b, 0)
                    if k == 9 and live(i, 0):
                        denominator(b, 0)
                    reduce_part(b, i, k + 3, 0)
                    if k == 3 and i == NB:
                        last_reciprocals()
                    elif k == 3 and live(i, -1):
                        reciprocals(later(b, -1), 1)
                    if k == 5 and live(i, -1):
                        normalise(later(b, -1), 1, i == NB)
                    if k == 6 and live(i, -1):
                        normal_low(later(b, -1), 1)
                    if k == 10 and live(i, 0):
                        reciprocals(b, 0)
                    if k == 12 and live(i, 0):
                        normalise(b, 0)
                    if k == 13 and live(i, 0):
                        normal_low(b, 0)
                    if k - 1 in SCALE_SLOTS and live(i, 3) and i != -3:
                        tiles_high(later(b, 3), SCALE_SLOTS.index(k - 1))
                    if k == 1 and b[1] % 2 and live(i, 3) and i != -3:
                        pair_high_half(later(b, 3))
                    if k == 2 and b[1] % 2 == 0 and live(i, 4) and i != -4:
                        pair_statistics(later(b, 4))
                    if k < NT and live(i, 4) and (i is None or i > -2):
                        statistics(later(b, 4), k)
                    reduce_part(b, i, k + 3, 1)
                    if k == 10 and live(i, 1):
                        make_shift(later(b, 1))
                    for g in setup_in(i, k - 1):
                        setup_low_half(g)
                    for what, g in tail(i, k, ("add_x", "norm", "xT_low", "weights_low")):
                        experts_part(what, g)

            dve.memset(row1[:, :], ROW1).then_inc(emb_ready, 1)
            dve.memset(const_pair[:, :], 0.0).then_inc(emb_ready, 1)
            dve.wait_ge(emb_ready, 2)
            for row in (0, 64):
                dve.memset(const_pair[:, row:row + S], CONST).then_inc(emb_ready, 1)
            dve.memset(pair_split[:, 1, 0:1], 0.0)
            dve.memset(pair_split[:, 0, 0:1], CONST)
            for t in keys[1:]:
                dve.memset(t[:, :, :, :], 0.0).then_inc(zeroed, 1)
            pair_statistics((0, 0))
            for l in lat_split:
                dve.memset(l[:, :], 0.0).then_inc(zeroed, 1)
            dve.wait_ge(zeroed, 7)
            dve.wait_ge(filled, 7)
            for t, l in zip(keys, lat_split):
                if t is not keys[0]:
                    dve.memset(t[0:TP, 0, 0:CT, 0:1], CONST)
                    dve.memset(t[0:S, 0, CT, 0:1], CONST)
                dve.memset(t[64:64 + S, 0, CT, 0:1], CONST)
                dve.memset(l[0:S, 0:1], CONST)
            dve.wait_ge(ident_ready, 3)
            dve.wait_ge(gains_in, 64)
            gm, bm, gl, bl = (vecs[:, n:n + 1] for n in range(4))
            EMB = (gl, gm, gl, gm)
            for e, gain in enumerate(EMB):
                dve.tensor_scalar(emb[:, e, :], ident[:, :], gain, CONST / ZS, ALU.mult, ALU.mult)\
                   .then_inc(emb_ready, 1)
            dve.wait_ge(emb_ready, 8)
            for e, gain in enumerate(EMB):
                dve.tensor_scalar(emb[0:1, e, 1:128], row1[0:1, 1:128], gain[0:1, :], 1.0, ALU.mult,
                                  ALU.mult).then_inc(emb_ready, 1)
            dve.tensor_copy(emb[:, 0, 0:1], bl).then_inc(emb_ready, 1)
            dve.memset(emb[:, 1, 0:1], 0.0).then_inc(emb_ready, 1)
            dve.tensor_tensor(emb[:, 2, 0:1], bl, bm, ALU.subtract).then_inc(emb_ready, 1)
            dve.tensor_copy(emb[:, 3, 0:1], bm).then_inc(emb_ready, 1)
            for t in range(6):
                statistics((0, 0), t)
            for g in range(EARLY):
                setup_low_half(g)
                if g < 2:
                    for t in (range(6, 10), range(10, NT))[g]:
                        statistics((0, 0), t)
                if g - 2 in range(NT):
                    statistics((0, 1), g - 2)
                if g == 6:
                    pair_high_half((0, 0))
                if g - 8 in range(len(PIECES)):
                    tiles_high((0, 0), g - 8)
                if g - 14 in range(4):
                    for t in range(3 * (g - 14), min(3 * (g - 14) + 3, NT) if g < 17 else NT):
                        statistics((0, 2), t)
            steps(dve, step)


def experts(nc, sem, sbuf, v):
    NB, S, TOK, D, E, Dff = (v[n] for n in ("NB", "S", "TOK", "D", "E", "Dff"))
    x, out, gate_w, w1, b1, w2, b2 = (v[n] for n in ("x", "out", "gate_w", "w1", "b1", "w2", "b2"))
    yT, ident = v["yT"], v["ident"]
    h_banks, y_banks = v["psum"]
    turn_bank = [v["out_bank"], v["misc"]]
    weight_bank = v["max_bank"]
    T, FC, GROUPS, W1S, W2S, GS = (v[n] for n in ("T", "FC", "GROUPS", "W1S", "W2S", "GS"))
    acc, xmT, xmTs, w1n, w2n, gateT, b1T, b2_rows = (v[n] for n in (
        "acc", "xmT", "xmTs", "w1n", "w2n", "gateT", "b1T", "b2_rows"))
    weights_in, weights_turned, weights_high, weights_low = (v[n] for n in (
        "expert_in", "weights_turned", "weights_high", "weights_low"))
    UNITS = len(GROUPS) * FC
    ROUTE_STEPS = 8
    TURN_UNITS, BIAS_UNITS, FIRST_UNITS = (4, 5), (6, 7), {9: 0, 10: 1, 13: 2}
    LATER_UNITS = {5: 0, 9: 1, 13: 2}
    out_rows = out.rearrange("b s d -> (b s) d").rearrange("(t p) d -> p t d", p=128)

    with ExitStack() as ctx:
        def sb(name, shape, dt=F32):
            return sbuf(ctx, name, shape, dt)

        b1_now = [sb(f"b1_now{i}", [128, FC]) for i in range(2)]
        logit = sb("logit", [128, T, E])
        p = sb("p", [128, T, E])
        above = sb("above", [128, T, E, E])
        rank = sb("rank", [128, T, E])
        col = sb("col", [128, 3, T])
        wgt = sb("wgt", [128, T, E])
        wgtT = sb("wgtT", [E, T * 128])
        wgt_dram = nc.dram_tensor("wgt_dram", (E, TOK), F32, kind="Internal").ap()
        wgt_all = [sb(f"wgt_all{i}", [128, TOK]) for i in range(2)]
        accT = sb("accT", [128, TOK])
        product = [sb(f"product{i}", [128, 512]) for i in range(2)]
        w1T, w2T = ([v[f"{w}T_first"], sb(f"{w}T_second", [128, 2, Dff], F16)] for w in ("w1", "w2"))
        g32 = [sb(f"g32_{i}", [128, 512]) for i in range(2)]
        gs = [sb(f"gs{i}", [128, 2, 512], F16) for i in range(4)]

        logits_ready = sem("logits_ready")
        route_step = sem("route_step")
        compared = sem("compared")
        route_exp = sem("route_exp")
        b1_ready = sem("b1_ready")
        h_ready = sem("h_ready")
        gelu_done = sem("gelu_done")
        g_high = sem("g_high")
        g_low = sem("g_low")
        y_done = sem("y_done")
        y_weighted = sem("y_weighted")
        y_summed = sem("y_summed")
        wgt_out = sem("wgt_out")
        wgt_in = [sem(f"wgt_in{i}") for i in range(2)]
        sum_turned = sem("sum_turned")
        out_ready = sem("out_ready")
        wgt_turned = sem("wgt_turned")
        wgt_copied = sem("wgt_copied")
        bias_ready = sem("bias_ready")
        bias_added = sem("bias_added")
        stored = sem("stored")
        passed = sem("passed2")

        def wait(eng, s, e, per, extra):
            k, c = e
            n = k * (2 * per) + (c * per + extra)
            if isinstance(k, int) and n <= 0:
                return
            eng.wait_ge(s, n)
            if eng.engine in (nc.gpsimd.engine, nc.sync.engine):
                eng.sem_inc(passed, 1)

        def run_experts(eng, body):
            body((0, 0))
            with eng.Fori(0, (E - 2) // 2) as k:
                body((k, 1))
                body((k, 2))
            body((0, E - 1))

        def is_first(e):
            return isinstance(e[0], int) and e[1] == 0

        def is_last(e):
            return isinstance(e[0], int) and e[1] == E - 1

        def nxt(e, d=1):
            return (e[0], e[1] + d)

        def width(g):
            return 128 * len(GROUPS[g])

        def columns(g):
            return slice(128 * GROUPS[g][0], 128 * GROUPS[g][-1] + 128)

        def two_groups(u, units):
            return range(2 * units.index(u), min(2 * units.index(u) + 2, len(GROUPS)))

        last_bank = turn_bank + weight_bank

        block = ctx.enter_context(nc.Block())

        @block.sync
        def _(sp):
            def load(e):
                n = e[0] * 2 + e[1]
                s = weights_in[e[1] % 2]
                wait(sp, weights_turned, nxt(e, -2), 2, 2)
                sp.dma_start(w1n[e[1] % 2][:, :, :], w1[:, bass.ds(n, 1), :].rearrange(
                    "(c f) e d -> f (c e) d", f=128)).then_inc(s, 16)
                sp.dma_start(w2n[e[1] % 2][:, :, :], w2[:, bass.ds(n, 1), :].rearrange(
                    "d e (c f) -> d (e c) f", f=128)).then_inc(s, 16)

            def load_routing(e):
                n = e[0] * 2 + e[1]
                wait(sp, y_weighted, nxt(e, -2), len(GROUPS), len(GROUPS))
                sp.dma_start(wgt_all[e[1] % 2][:, :], wgt_dram[bass.ds(n, 1), :].to_broadcast([128, TOK]))\
                  .then_inc(wgt_in[e[1] % 2], 16)

            sp.wait_ge(wgt_copied, len(GROUPS))
            sp.dma_start(wgt_dram, wgtT[:, :]).then_inc(wgt_out, 16)
            sp.wait_ge(wgt_out, 16)
            load_routing((0, 0))
            load_routing((0, 1))
            with sp.Fori(0, (E - 2) // 2) as k:
                load((k, 2))
                load_routing((k, 2))
                load((k, 3))
                load_routing((k, 3))
            for g, tiles in enumerate(GROUPS):
                rows = slice(tiles[0], tiles[-1] + 1)
                sp.wait_ge(out_ready, g + 1)
                sp.dma_start(out_rows[:, rows, :], acc[:, rows, :]).then_inc(stored, 16)
            sp.wait_ge(stored, 16 * len(GROUPS))

        @block.gpsimd
        def _(pool):
            def body(e):
                for g in range(len(GROUPS)):
                    wait(pool, y_weighted, e, len(GROUPS), g + 1)
                    pool.tensor_tensor(accT[:, columns(g)], accT[:, columns(g)], product[g % 2][:, 0:width(g)],
                                       ALU.add).then_inc(y_summed, 1)

            pool.wait_ge(bias_added, len(GROUPS))
            run_experts(pool, body)

        @block.tensor
        def _(pe):
            PASSES = ((0, 0), (0, 1), (1, 0))

            def turn_weights(e, m):
                wait(pe, weights_in[e[1] % 2], (e[0], e[1] // 2 * 2), 16, 32)
                wait(pe, weights_low, nxt(e, -1), 2, m + 1)
                src = (w1n, w2n)[m][e[1] % 2]
                for c in range(FC):
                    mm = nc.tensor.transpose(weight_bank[m][:, 128 * c:128 * c + 128], src[:, c, :], ident[:, :])
                mm.then_inc(weights_turned, 1)

            for t in GROUPS[-1]:
                mm = nc.tensor.matmul(y_banks[:, 1, E * t:E * t + E], xmT[:, 128 * t:128 * t + 128], gateT,
                                      start=True, stop=True)
            mm.then_inc(logits_ready, 1)

            def turn_router(part):
                if part >= 2:
                    pe.wait_ge(wgt_copied, part - 1)
                for j, t in enumerate(GROUPS[part]):
                    mm = nc.tensor.transpose(turn_bank[part % 2][0:E, 128 * j:128 * j + 128], wgt[:, t, :],
                                             ident[:, :])
                mm.then_inc(wgt_turned, 1)

            def hidden(e, u):
                g, c = divmod(u, FC)
                w = width(g)
                if u == 0:
                    wait(pe, weights_low, e, 2, 2)
                wait(pe, gelu_done, e, UNITS, u - 1)
                for n, (a, z) in enumerate(PASSES):
                    mm = nc.tensor.matmul(h_banks[:, u % 2, 0:w], w1T[e[1] % 2][:, a, 128 * c:128 * c + 128],
                                          xmTs[:, z, columns(g)], start=(n == 0), stop=(n == 2))
                mm.then_inc(h_ready, 1)

            def outputs(e, u):
                g, c = divmod(u, FC)
                wait(pe, g_low, e, UNITS, u + 1)
                if c == 0:
                    wait(pe, y_weighted, e, len(GROUPS), g - 1)
                for n, (z, a) in enumerate(PASSES):
                    mm = nc.tensor.matmul(y_banks[:, g % 2, 0:width(g)],
                                          w2T[e[1] % 2][:, a, 128 * c:128 * c + 128],
                                          gs[u % 4][:, z, 0:width(g)],
                                          start=(c == 0 and n == 0), stop=(c == FC - 1 and n == 2))
                mm.then_inc(y_done, 1)

            def body(e):
                for u in range(UNITS):
                    hidden(e, u)
                    if u in (4, 8) and not is_last(e):
                        turn_weights(nxt(e), u // 4 - 1)
                    if u >= 2:
                        outputs(e, u - 2)
                    elif not is_first(e):
                        outputs(nxt(e, -1), u + UNITS - 2)
                    if is_first(e) and u in TURN_UNITS:
                        pe.wait_ge(route_step, ROUTE_STEPS)
                        for part in two_groups(u, TURN_UNITS):
                            turn_router(part)
                    if is_first(e) and u in BIAS_UNITS:
                        pe.wait_ge(wgt_copied, len(GROUPS))
                        for part in two_groups(u, BIAS_UNITS):
                            if part >= 2:
                                pe.wait_ge(bias_added, part - 1)
                            nc.tensor.matmul(turn_bank[part % 2][:, 0:width(part)], b2_rows,
                                             wgtT[:, columns(part)], start=True, stop=True).then_inc(bias_ready, 1)

            def turn_sum(g):
                pe.wait_ge(y_summed, (E - 1) * len(GROUPS) + g + 1)
                for j, t in enumerate(GROUPS[g]):
                    mm = nc.tensor.transpose(last_bank[g][:, 128 * j:128 * j + 128],
                                             accT[:, 128 * t:128 * t + 128], ident[:, :])
                mm.then_inc(sum_turned, 1)

            run_experts(pe, body)
            outputs((0, E - 1), UNITS - 2)
            turn_sum(0)
            outputs((0, E - 1), UNITS - 1)
            for g in range(1, len(GROUPS)):
                turn_sum(g)

        @block.scalar
        def _(act):
            def weights_split(e, m):
                wait(act, weights_turned, e, 2, m + 1)
                act.activation((w1T, w2T)[m][e[1] % 2][:, 0, :], weight_bank[m][:, :], ACT.Copy,
                               scale=(W1S, W2S)[m]).then_inc(weights_high, 1)

            act.wait_ge(route_step, 2)
            act.activation(p[:, :, :], logit[:, :, :], ACT.Exp).then_inc(route_exp, 1)

            def body(e):
                n = e[0] * (2 * FC) + e[1] * FC
                b1_e = b1_now[e[1] % 2]
                act.activation(b1_e[:, :], b1T[:, bass.ds(n, FC)], ACT.Copy).then_inc(b1_ready, 1)
                wait(act, b1_ready, e, 1, 1)
                for u in range(UNITS):
                    g, c = divmod(u, FC)
                    w = width(g)
                    wait(act, h_ready, e, UNITS, u + 1)
                    wait(act, g_low, e, UNITS, u - 1)
                    act.activation(g32[u % 2][:, 0:w], h_banks[:, u % 2, 0:w], ACT.Gelu_apprx_tanh,
                                   bias=b1_e[:, c:c + 1],
                                   scale=1.0 / (W1S * ZS)).then_inc(gelu_done, 1)
                    wait(act, gelu_done, e, UNITS, u + 1)
                    wait(act, y_done, e, UNITS, u - 3)
                    act.activation(gs[u % 4][:, 0, 0:w], g32[u % 2][:, 0:w], ACT.Copy, scale=GS).then_inc(g_high, 1)
                    if u in (4, 8) and not is_last(e):
                        weights_split(nxt(e), u // 4 - 1)

            run_experts(act, body)

        @block.vector
        def _(dve):
            def weights_split(e, m):
                wait(dve, weights_high, e, 2, m + 1)
                dst = (w1T, w2T)[m][e[1] % 2]
                dve.scalar_tensor_tensor(out=dst[:, 1, :], in0=weight_bank[m][:, :], scalar=(W1S, W2S)[m],
                                         in1=dst[:, 0, :], op0=ALU.mult, op1=ALU.subtract)\
                   .then_inc(weights_low, 1)

            n = 0

            def done(ins):
                nonlocal n
                n += 1
                ins.then_inc(route_step, 1)
                dve.wait_ge(route_step, n)

            def spread(ap):
                return ap.to_broadcast([128, T, E])

            dve.wait_ge(logits_ready, 1)
            logits = y_banks[:, 1, 0:T * E].rearrange("p (t e) -> p t e", e=E)
            done(dve.tensor_reduce(col[:, 0, :], logits, AX.X, ALU.max))
            done(dve.tensor_tensor(logit[:, :, :], logits, spread(col[:, 0, :].unsqueeze(2)), ALU.subtract))
            dve.wait_ge(route_exp, 1)
            done(dve.tensor_reduce(col[:, 1, :], p[:, :, :], AX.X, ALU.add))
            done(dve.reciprocal(col[:, 2, :], col[:, 1, :]))
            done(dve.tensor_tensor(p[:, :, :], p[:, :, :], spread(col[:, 2, :].unsqueeze(2)), ALU.mult))
            def compare(experts):
                for e in experts:
                    for part, op in ((slice(0, e + 1), ALU.is_gt), (slice(e + 1, E), ALU.is_ge)):
                        w = part.stop - part.start
                        if w:
                            ins = dve.tensor_tensor(above[:, :, part, e], p[:, :, e:e + 1].to_broadcast([128, T, w]),
                                                    p[:, :, part], op)
                ins.then_inc(compared, 1)

            def choose():
                dve.wait_ge(compared, 2)
                done(dve.tensor_reduce(rank[:, :, :], above[:, :, :, :], AX.X, ALU.add))
                done(dve.tensor_scalar(rank[:, :, :], rank[:, :, :], 2.0, 1.0, ALU.is_lt, ALU.mult))
                done(dve.tensor_tensor(wgt[:, :, :], p[:, :, :], rank[:, :, :], ALU.mult))
                assert n == ROUTE_STEPS

            def weight_outputs(e, g):
                wait(dve, wgt_in[e[1] % 2], (e[0], e[1] // 2 * 2), 8, 16)
                wait(dve, y_summed, e, len(GROUPS), g - 1)
                wait(dve, y_done, e, UNITS, FC * g + FC)
                dve.scalar_tensor_tensor(out=product[g % 2][:, 0:width(g)], in0=y_banks[:, g % 2, 0:width(g)],
                                         scalar=1.0 / (W2S * GS), in1=wgt_all[e[1] % 2][:, columns(g)],
                                         op0=ALU.mult, op1=ALU.mult).then_inc(y_weighted, 1)

            def finish(g):
                tiles = slice(GROUPS[g][0], GROUPS[g][-1] + 1)
                dve.wait_ge(sum_turned, g + 1)
                dve.tensor_tensor(acc[:, tiles, :], last_bank[g][:, 0:width(g)].rearrange(
                    "p (t d) -> p t d", d=D), acc[:, tiles, :], ALU.add).then_inc(out_ready, 1)

            def body(e):
                for u in range(UNITS):
                    g, c = divmod(u, FC)
                    w = width(g)
                    wait(dve, g_high, e, UNITS, u + 1)
                    dve.scalar_tensor_tensor(out=gs[u % 4][:, 1, 0:w], in0=g32[u % 2][:, 0:w], scalar=GS,
                                             in1=gs[u % 4][:, 0, 0:w], op0=ALU.mult,
                                             op1=ALU.subtract).then_inc(g_low, 1)
                    if u in (4, 8) and not is_last(e):
                        weights_split(nxt(e), u // 4 - 1)
                    if is_first(e) and u in (1, 2):
                        compare(range((u - 1) * E // 2, u * E // 2))
                    if is_first(e) and u == 3:
                        choose()
                    if is_first(e) and u in TURN_UNITS:
                        for part in two_groups(u, TURN_UNITS):
                            dve.wait_ge(wgt_turned, part + 1)
                            dve.tensor_copy(wgtT[:, columns(part)],
                                            turn_bank[part % 2][0:E, 0:width(part)]).then_inc(wgt_copied, 1)
                    if is_first(e) and u in BIAS_UNITS:
                        for part in two_groups(u, BIAS_UNITS):
                            dve.wait_ge(bias_ready, part + 1)
                            dve.tensor_copy(accT[:, columns(part)],
                                            turn_bank[part % 2][:, 0:width(part)]).then_inc(bias_added, 1)
                    if not is_first(e) and u == 1:
                        weight_outputs(nxt(e, -1), len(GROUPS) - 1)
                    of_unit = FIRST_UNITS if is_first(e) else LATER_UNITS
                    if u in of_unit:
                        weight_outputs(e, of_unit[u])

            run_experts(dve, body)
            finish(0)
            weight_outputs((0, E - 1), len(GROUPS) - 1)
            for g in range(1, len(GROUPS)):
                finish(g)


_INS = ["x", "ctx_1024", "L0_xattn_ln_m_g", "L0_xattn_ln_m_b", "L0_xattn_ln_l_g", "L0_xattn_ln_l_b",
        "L0_xattn_Wq", "L0_xattn_Wkv", "L0_xattn_Wout", "L0_ffn_gate_w", "L0_ffn_w1", "L0_ffn_b1",
        "L0_ffn_w2", "L0_ffn_b2"]


def kernel(**inputs):
    import numpy as _np
    import concourse.bacc as _bacc
    from concourse import mybir as _mybir
    from concourse.bass_utils import run_bass_kernel_spmd as _run

    nc = _bacc.Bacc("TRN2", target_bir_lowering=False, num_devices=1)
    arrays, args = {}, []
    for name in _INS:
        a = _np.ascontiguousarray(inputs[name])
        arrays[f"in_{name}"] = a
        args.append(nc.dram_tensor(f"in_{name}", a.shape, _mybir.dt.from_np(a.dtype), kind="ExternalInput").ap())
    shape = tuple(inputs["x"].shape)
    args.append(nc.dram_tensor("out_0", shape, _mybir.dt.float32, kind="ExternalOutput").ap())
    attention_and_experts(nc, *args)
    r = _run(nc, [arrays], core_ids=[0])
    return r.results[0]["out_0"]
```
